# Optimizing a Trainium2 kernel written in Bass

```python
import numpy as np
import jax
import jax.numpy as jnp

def _softmax(x, axis=-1):
    return jax.nn.softmax(x, axis=axis)

def _gelu(x):
    return jax.nn.gelu(x, approximate=True)

def _silu(x):
    return jax.nn.silu(x)

def _sigmoid(x):
    return jax.nn.sigmoid(x)

def _layernorm(x, axis=-1, eps=1e-05):
    m = jnp.mean(x, axis=axis, keepdims=True)
    v = jnp.var(x, axis=axis, keepdims=True)
    return (x - m) / jnp.sqrt(v + eps)

def _scatter_add(tgt, idx, src, axis=0):
    return tgt.at[idx].add(src)

def _segment_sum(src, seg, n):
    return jax.ops.segment_sum(src, seg, n)
kernel_name = 'mk_flamingo_gated_d2_seqx_r2_f53e9f'

def setup_inputs(seed: int=0):
    np.random.seed(seed)
    _w = jnp.asarray

    def _rec_inputs():
        import jax
        import jax.numpy as jnp
        _rk = jax.random.key(seed)
        x = 7.22e-05 + 1 * jax.random.normal(jax.random.fold_in(_rk, 1), (8, 512, 512), jnp.float32)
        _lenS = 512 - jax.random.randint(jax.random.fold_in(_rk, 7), (8,), 0, max(1, 512 // 4) + 1, jnp.int32)
        _lenS2 = 120 - jax.random.randint(jax.random.fold_in(_rk, 8), (8,), 0, max(1, 120 // 4) + 1, jnp.int32)
        _ctx_1024P = jax.random.normal(jax.random.fold_in(_rk, 11), (8, 16, 512), jnp.float32)
        _ctx_1024c = jax.random.dirichlet(jax.random.fold_in(_rk, 511), 0.3 * jnp.ones((16,), jnp.float32), (8, 120))
        _ctx_1024t = jnp.einsum('bsk,bkd->bsd', _ctx_1024c, _ctx_1024P)
        _ctx_1024t = _ctx_1024t * jax.lax.rsqrt(jnp.mean(jnp.square(_ctx_1024t)) + 1e-12) * 0.953939
        ctx_1024 = 4.13588e-05 + 0.999923 * (_ctx_1024t + 0.3 * jax.random.normal(jax.random.fold_in(_rk, 611), (8, 120, 512), jnp.float32))
        _validS = jnp.arange(512)[None, :] < _lenS[:, None]
        _validS2 = jnp.arange(120)[None, :] < _lenS2[:, None]
        _causal = jnp.tril(jnp.ones((512, 512), dtype=bool))
        mask_BxS2_ik0 = jnp.where(jnp.broadcast_to(_validS2[:, :], (8, 120)), 0, 1).astype(jnp.int32)
        _g = jax.random.normal(jax.random.fold_in(_rk, 9001), (2, 2), jnp.float32)
        _g = jnp.sign(_g) * jnp.maximum(jnp.abs(_g), 1.0) + (_g == 0) * 1.0
        g_xattn = _g[0]
        g_ffn = _g[1]
        return (x, ctx_1024, mask_BxS2_ik0, g_xattn, g_ffn)
    x, ctx_1024, mask_BxS2_ik0, g_xattn, g_ffn = _rec_inputs()

    def _L0_xattn_setup():
        import jax, jax.numpy as jnp
        import numpy as np
        D_MODEL = 512
        NUM_HEADS = 16
        D_K = D_MODEL // NUM_HEADS

        def _split_heads(x):
            B, S, _ = x.shape
            return x.reshape(B, S, NUM_HEADS, D_K).transpose(0, 2, 1, 3)
        key = jax.random.key(seed)
        ks = jax.random.split(key, 7)
        B, S = (4, 1024)
        scale = 1.0 / np.sqrt(D_MODEL)
        return {'Q': jax.random.normal(ks[0], (B, S, D_MODEL), dtype=jnp.float32), 'K': jax.random.normal(ks[1], (B, S, D_MODEL), dtype=jnp.float32), 'V': jax.random.normal(ks[2], (B, S, D_MODEL), dtype=jnp.float32), 'W_q': jax.random.normal(ks[3], (D_MODEL, D_MODEL), dtype=jnp.float32) * scale, 'W_k': jax.random.normal(ks[4], (D_MODEL, D_MODEL), dtype=jnp.float32) * scale, 'W_v': jax.random.normal(ks[5], (D_MODEL, D_MODEL), dtype=jnp.float32) * scale, 'W_o': jax.random.normal(ks[6], (D_MODEL, D_MODEL), dtype=jnp.float32) * scale}
    _L0_xattn_all = _L0_xattn_setup()
    _L0_xattn_in = {k: v for k, v in _L0_xattn_all.items() if k in ('W_q', 'W_k', 'W_v', 'W_o')}
    del _L0_xattn_all

    def _L0_ffn_setup():
        import jax, jax.numpy as jnp
        import numpy as np
        DM, NEXPERTS, SETS, ESIZE = (512, 32, 4, 32)
        B, S = (2, 4096)
        key = jax.random.key(seed)
        ks = jax.random.split(key, 7)
        sc = 0.02
        return {'x': jax.random.normal(ks[0], (B, S, DM), jnp.float32), 'Wc': jax.random.normal(ks[1], (DM, NEXPERTS, SETS), jnp.float32) * sc, 'bc': jax.random.normal(ks[2], (NEXPERTS, SETS), jnp.float32) * sc, 'W1': jax.random.normal(ks[3], (NEXPERTS, SETS, DM, ESIZE), jnp.float32) * sc, 'b1': jax.random.normal(ks[4], (NEXPERTS, SETS, ESIZE), jnp.float32) * sc, 'W2': jax.random.normal(ks[5], (NEXPERTS, SETS, DM, ESIZE), jnp.float32) * sc, 'b2': jax.random.normal(ks[6], (NEXPERTS, SETS, DM), jnp.float32) * sc}
    _L0_ffn_all = _L0_ffn_setup()
    _L0_ffn_in = {k: v for k, v in _L0_ffn_all.items() if k in ('Wc', 'bc', 'W1', 'b1', 'W2', 'b2')}
    del _L0_ffn_all

    def _L1_xattn_setup():
        import jax, jax.numpy as jnp
        import numpy as np
        D = 512
        H = 16
        HD = D // H

        def _split_heads(x):
            B, L, _ = x.shape
            return x.reshape(B, L, H, HD).transpose(0, 2, 1, 3)
        key = jax.random.key(seed)
        ks = jax.random.split(key, 12)
        B, Lq, Lk = (2, 1024, 1024)
        scale = 1.0 / np.sqrt(D)
        inp = {'query_input': jax.random.normal(ks[0], (B, Lq, D), jnp.float32), 'key_input': jax.random.normal(ks[1], (B, Lk, D), jnp.float32), 'value_input': jax.random.normal(ks[2], (B, Lk, D), jnp.float32), 'key_mask': jax.random.randint(ks[3], (B, Lk), 0, 2, jnp.int32), 'Wq': jax.random.normal(ks[4], (D, D), jnp.float32) * scale, 'bq': jnp.zeros((D,), jnp.float32), 'Wk': jax.random.normal(ks[5], (D, D), jnp.float32) * scale, 'bk': jnp.zeros((D,), jnp.float32), 'Wv': jax.random.normal(ks[6], (D, D), jnp.float32) * scale, 'bv': jnp.zeros((D,), jnp.float32), 'Wo': jax.random.normal(ks[7], (D, D), jnp.float32) * scale, 'bo': jnp.zeros((D,), jnp.float32)}
        return inp
    _L1_xattn_all = _L1_xattn_setup()
    _L1_xattn_in = {k: v for k, v in _L1_xattn_all.items() if k in ('Wq', 'bq', 'Wk', 'bk', 'Wv', 'bv', 'Wo', 'bo')}
    del _L1_xattn_all

    def _L1_ffn_setup():
        import jax, jax.numpy as jnp
        import numpy as np
        DIM = 512

        def _reference_tuple_inner(x, W_r, W_k, W_v, mu_r, mu_k):
            B, T, C = x.shape
            x_prev = jnp.concatenate([jnp.zeros((B, 1, C), x.dtype), x[:, :-1, :]], axis=1)
            xr = mu_r * x + (1.0 - mu_r) * x_prev
            xk = mu_k * x + (1.0 - mu_k) * x_prev
            r = jax.nn.sigmoid(jnp.einsum('btc,dc->btd', xr, W_r))
            k = jnp.einsum('btc,dc->btd', xk, W_k)
            k_act = jnp.square(jax.nn.relu(k))
            out = r * jnp.einsum('btc,dc->btd', k_act, W_v)
            new_state = x[:, -1, :]
            return (out, new_state)
        key = jax.random.key(seed)
        ks = jax.random.split(key, 6)
        B, T, C = (8, 1024, DIM)
        x = jax.random.normal(ks[0], (B, T, C), dtype=jnp.float32)
        s = 1.0 / np.sqrt(C)
        W_r = jax.random.uniform(ks[1], (C, C), jnp.float32, -s, s)
        W_k = jax.random.uniform(ks[2], (C, C), jnp.float32, -s, s)
        W_v = jax.random.uniform(ks[3], (C, C), jnp.float32, -s, s)
        mu_r = jax.random.uniform(ks[4], (C,), jnp.float32)
        mu_k = jax.random.uniform(ks[5], (C,), jnp.float32)
        return {'x': x, 'W_r': W_r, 'W_k': W_k, 'W_v': W_v, 'mu_r': mu_r, 'mu_k': mu_k}
    _L1_ffn_all = _L1_ffn_setup()
    _L1_ffn_in = {k: v for k, v in _L1_ffn_all.items() if k in ('W_r', 'W_k', 'W_v', 'mu_r', 'mu_k')}
    del _L1_ffn_all
    return {'x': x, 'ctx_1024': ctx_1024, 'mask_BxS2_ik0': mask_BxS2_ik0, 'g_xattn': g_xattn, 'g_ffn': g_ffn, 'L0_xattn_W_q': _L0_xattn_in['W_q'], 'L0_xattn_W_k': _L0_xattn_in['W_k'], 'L0_xattn_W_v': _L0_xattn_in['W_v'], 'L0_xattn_W_o': _L0_xattn_in['W_o'], 'L0_ffn_Wc': _L0_ffn_in['Wc'], 'L0_ffn_bc': _L0_ffn_in['bc'], 'L0_ffn_W1': _L0_ffn_in['W1'], 'L0_ffn_b1': _L0_ffn_in['b1'], 'L0_ffn_W2': _L0_ffn_in['W2'], 'L0_ffn_b2': _L0_ffn_in['b2'], 'L1_xattn_Wq': _L1_xattn_in['Wq'], 'L1_xattn_bq': _L1_xattn_in['bq'], 'L1_xattn_Wk': _L1_xattn_in['Wk'], 'L1_xattn_bk': _L1_xattn_in['bk'], 'L1_xattn_Wv': _L1_xattn_in['Wv'], 'L1_xattn_bv': _L1_xattn_in['bv'], 'L1_xattn_Wo': _L1_xattn_in['Wo'], 'L1_xattn_bo': _L1_xattn_in['bo'], 'L1_ffn_W_r': _L1_ffn_in['W_r'], 'L1_ffn_W_k': _L1_ffn_in['W_k'], 'L1_ffn_W_v': _L1_ffn_in['W_v'], 'L1_ffn_mu_r': _L1_ffn_in['mu_r'], 'L1_ffn_mu_k': _L1_ffn_in['mu_k']}

def reference(x, ctx_1024, mask_BxS2_ik0, g_xattn, g_ffn, L0_xattn_W_q, L0_xattn_W_k, L0_xattn_W_v, L0_xattn_W_o, L0_ffn_Wc, L0_ffn_bc, L0_ffn_W1, L0_ffn_b1, L0_ffn_W2, L0_ffn_b2, L1_xattn_Wq, L1_xattn_bq, L1_xattn_Wk, L1_xattn_bk, L1_xattn_Wv, L1_xattn_bv, L1_xattn_Wo, L1_xattn_bo, L1_ffn_W_r, L1_ffn_W_k, L1_ffn_W_v, L1_ffn_mu_r, L1_ffn_mu_k):
    import jax
    import jax.numpy as jnp

    def _L0_xattn_ref(Q, K, V, W_q, W_k, W_v, W_o):
        import jax, jax.numpy as jnp
        import numpy as np
        D_MODEL = 512
        NUM_HEADS = 16
        D_K = D_MODEL // NUM_HEADS

        def _split_heads(x):
            B, S, _ = x.shape
            return x.reshape(B, S, NUM_HEADS, D_K).transpose(0, 2, 1, 3)
        q = _split_heads(Q @ W_q.T)
        k = _split_heads(K @ W_k.T)
        v = _split_heads(V @ W_v.T)
        scores = jnp.einsum('bhqd,bhkd->bhqk', q, k) / jnp.sqrt(jnp.float32(D_K))
        probs = jax.nn.softmax(scores, axis=-1)
        out = jnp.einsum('bhqk,bhkd->bhqd', probs, v)
        B, H, S, dk = out.shape
        out = out.transpose(0, 2, 1, 3).reshape(B, S, H * dk)
        return out @ W_o.T

    def _L0_ffn_ref(x, Wc, bc, W1, b1, W2, b2):
        import jax, jax.numpy as jnp
        import numpy as np
        DM, NEXPERTS, SETS, ESIZE = (512, 32, 4, 32)
        B, S = (2, 4096)
        b, s, d = x.shape
        g = Wc.shape[1]
        grouped = x.reshape(b, s // g, g, d)
        logits = jnp.einsum('bntd,des->bntes', grouped, Wc) + bc
        tie = jnp.linspace(0.0, 1e-06, g, dtype=x.dtype).reshape(-1, 1, 1)
        logits = logits + tie
        perm = (logits == jnp.max(logits, axis=-3, keepdims=True)).astype(x.dtype)
        permuted = jnp.einsum('bntd,bntes->bnesd', grouped, perm)
        inner = jax.nn.relu(jnp.einsum('bnesd,esdf->bnesf', permuted, W1) + b1)
        result_permuted = jnp.einsum('bnesf,esdf->bnesd', inner, W2) + b2
        result = jnp.einsum('bnesd,bntes->bntd', result_permuted, perm)
        return result.reshape(b, s, d)

    def _L1_xattn_ref(query_input, key_input, value_input, key_mask, Wq, bq, Wk, bk, Wv, bv, Wo, bo):
        import jax, jax.numpy as jnp
        import numpy as np
        D = 512
        H = 16
        HD = D // H

        def _split_heads(x):
            B, L, _ = x.shape
            return x.reshape(B, L, H, HD).transpose(0, 2, 1, 3)
        B = query_input.shape[0]
        q = _split_heads(query_input @ Wq.T + bq)
        k = _split_heads(key_input @ Wk.T + bk)
        v = _split_heads(value_input @ Wv.T + bv)
        scores = jnp.einsum('bhqd,bhkd->bhqk', q, k) / jnp.sqrt(jnp.float32(HD))
        mask = key_mask[:, None, None, :]
        scores = jnp.where(mask == 0, jnp.float32(-1e+30), scores)
        attn = jax.nn.softmax(scores, axis=-1)
        ctx = jnp.einsum('bhqk,bhkd->bhqd', attn, v)
        ctx = ctx.transpose(0, 2, 1, 3).reshape(B, -1, D)
        return ctx @ Wo.T + bo

    def _L1_ffn_ref(x, W_r, W_k, W_v, mu_r, mu_k):
        import jax, jax.numpy as jnp
        import numpy as np
        DIM = 512

        def _reference_tuple_inner(x, W_r, W_k, W_v, mu_r, mu_k):
            B, T, C = x.shape
            x_prev = jnp.concatenate([jnp.zeros((B, 1, C), x.dtype), x[:, :-1, :]], axis=1)
            xr = mu_r * x + (1.0 - mu_r) * x_prev
            xk = mu_k * x + (1.0 - mu_k) * x_prev
            r = jax.nn.sigmoid(jnp.einsum('btc,dc->btd', xr, W_r))
            k = jnp.einsum('btc,dc->btd', xk, W_k)
            k_act = jnp.square(jax.nn.relu(k))
            out = r * jnp.einsum('btc,dc->btd', k_act, W_v)
            new_state = x[:, -1, :]
            return (out, new_state)
        return _reference_tuple_inner(x, W_r, W_k, W_v, mu_r, mu_k)[0]
    x = x + jnp.tanh(g_xattn[0]) * _L0_xattn_ref(_layernorm(x, axis=-1), ctx_1024, ctx_1024, L0_xattn_W_q, L0_xattn_W_k, L0_xattn_W_v, L0_xattn_W_o)
    x = x + jnp.tanh(g_ffn[0]) * _L0_ffn_ref(_layernorm(x, axis=-1), L0_ffn_Wc, L0_ffn_bc, L0_ffn_W1, L0_ffn_b1, L0_ffn_W2, L0_ffn_b2)
    x = x + jnp.tanh(g_xattn[1]) * _L1_xattn_ref(_layernorm(x, axis=-1), ctx_1024, ctx_1024, mask_BxS2_ik0, L1_xattn_Wq, L1_xattn_bq, L1_xattn_Wk, L1_xattn_bk, L1_xattn_Wv, L1_xattn_bv, L1_xattn_Wo, L1_xattn_bo)
    x = x + jnp.tanh(g_ffn[1]) * _L1_ffn_ref(_layernorm(x, axis=-1), L1_ffn_W_r, L1_ffn_W_k, L1_ffn_W_v, L1_ffn_mu_r, L1_ffn_mu_k)
    return x

_drawn_inputs = setup_inputs


def setup_inputs(seed=0):
    import zlib

    import numpy as np

    out = dict(_drawn_inputs(seed))
    spreads = {'g_ffn': (-1.0, 0.6),
     'L1_xattn_bq': (0.0, 0.355),
     'L1_xattn_bk': (0.0, 2.0),
     'L1_xattn_bv': (0.0, 0.1),
     'L1_xattn_bo': (0.0, 0.1)}
    factors = {'L0_ffn_b1': 30.245, 'L1_ffn_W_r': 3.919, 'L1_ffn_mu_r': 8.0}
    for name, (base, spread) in spreads.items():
        noise = np.random.default_rng([zlib.crc32(name.encode()), seed]).standard_normal(out[name].shape)
        drawn = base * np.exp(spread * noise) if base else spread * noise
        out[name] = jnp.asarray(drawn.astype(out[name].dtype))
    for name, factor in factors.items():
        out[name] = (out[name] * factor).astype(out[name].dtype)
    return out
```

```python
from contextlib import ExitStack

import concourse.bass as bass
import numpy as np
from concourse import mybir

ALU = mybir.AluOpType
ACT = mybir.ActivationFunctionType
AX = mybir.AxisListType
F32 = mybir.dt.float32
F32R = mybir.dt.float32r
I32 = mybir.dt.int32

P = 128
B, T, D = 8, 512, 512
S2 = 120
H, DK = 16, 32
C = D // P
NT = T // P
HJ = P // DK
ES, EF, G = 128, 32, 32
NG = B * T // G
GB = T // G
GT = P // G
NTILE = B * NT
EJ = P // EF
EK = ES // EJ
EPS = 1e-5
SCALE = 1.0 / float(np.sqrt(np.float32(DK)))
BIG = 1e30
RG = 2
RING = 8
STACK = 3 * DK + 1


def f(ap):
    return ap.bitcast(F32)


LN_STEPS = 4


class Steps:

    def __init__(self, eng, sem, base=0):
        self.eng, self.sem, self.base, self.n = eng, sem, base, 0

    def count(self, ins):
        ins.then_inc(self.sem, 1)
        self.n += 1

    def link(self, ins):
        self.count(ins)
        self.eng.wait_ge(self.sem, self.base + self.n)


def tools(nc, ctx):
    def sb(name, shape, dt=F32):
        return ctx.enter_context(nc.sbuf_tensor(name, shape, dt))

    def banks(*names):
        return {n: ctx.enter_context(nc.psum_tensor(n, [P, 512], F32)) for n in names}

    sems = []

    def sem(name):
        sems.append(nc.alloc_semaphore(name=name))
        return sems[-1]

    def clear():
        nc.clear_and_free_semaphores(sems)
        nc.all_engine_barrier()

    ctx.callback(clear)
    return sb, banks, sem


def three_passes(pe, out, lhs, rhs):
    for c in range(C):
        (ah, al), (bh, bl) = lhs(c), rhs(c)
        pe.matmul(out, ah, bh, start=(c == 0), stop=False)
        pe.matmul(out, ah, bl, start=False, stop=False)
        last = pe.matmul(out, al, bh, start=False, stop=(c == C - 1))
    return last


def keys_and_values(nc, ctx_t, weights, biases, kh_d, kl_d, v_d):
    N = B * S2
    HALF = N // 2
    with ExitStack() as ctx:
        sb, banks, sem = tools(nc, ctx)
        raw = sb("kv_raw", [P, 4, C, D])
        wh, wl = sb("kv_wh", [P, 4, C, D], F32R), sb("kv_wl", [P, 4, C, D], F32R)
        craw = sb("kv_craw", [P, C, N])
        ch, cl = sb("kv_ch", [P, C, N], F32R), sb("kv_cl", [P, C, N], F32R)
        bk, bv = sb("kv_bk", [P, C]), sb("kv_bv", [S2, D])
        kh, kl = sb("kv_kh", [P, 2, HALF], F32R), sb("kv_kl", [P, 2, HALF], F32R)
        vo = sb("kv_vo", [S2, 2, D])
        ps = banks("kv_p0", "kv_p1")
        full, free = [sem(f"kv_full{i}") for i in range(2)], [sem(f"kv_free{i}") for i in range(2)]
        ctx_in, bias_in = sem("kv_ctx_in"), sem("kv_bias_in")
        w_in = [sem(f"kv_w_in{i}") for i in range(4)]
        hi_done, lo_done, k_hi = sem("kv_hi_done"), sem("kv_lo_done"), sem("kv_k_hi")
        k_st, v_st = [sem(f"kv_k_st{i}") for i in range(2)], [sem(f"kv_v_st{i}") for i in range(2)]
        bank = [ps["kv_p0"], ps["kv_p1"]]
        units = [(lay, kind, u) for lay in range(2) for kind in "kv" for u in range(8)]

        with nc.Block() as block:
            @block.sync
            def _(sp):
                sp.dma_start(craw[:, :, :], ctx_t.rearrange("(c p) n -> p c n", p=P)).then_inc(ctx_in, 16)
                for i, w in enumerate(weights):
                    sp.dma_start(raw[:, i], w.rearrange("(c p) n -> p c n", p=P)).then_inc(w_in[i], 16)
                sp.dma_start(bk[:, :], biases[0]).then_inc(bias_in, 16)
                sp.dma_start(bv[:, :], biases[1].partition_broadcast(S2)).then_inc(bias_in, 16)
                nk = nv = 0
                for n, (lay, kind, u) in enumerate(units):
                    sp.wait_ge(free[n % 2], n // 2 + 1)
                    if kind == "k":
                        m, half = u // 2, u % 2
                        rows, cols = slice(m * P, (m + 1) * P), slice(half * HALF, (half + 1) * HALF)
                        sp.dma_start(kh_d[lay][rows, cols], f(kh[:, nk % 2, :])).then_inc(k_st[nk % 2], 16)
                        sp.dma_start(kl_d[lay][rows, cols], f(kl[:, nk % 2, :])).then_inc(k_st[nk % 2], 16)
                        nk += 1
                    else:
                        sp.dma_start(v_d[lay][u * S2:(u + 1) * S2, :], vo[:, nv % 2, :]).then_inc(v_st[nv % 2], 16)
                        nv += 1
                for i in range(2):
                    sp.wait_ge(k_st[i], 32 * nk // 2)
                    sp.wait_ge(v_st[i], 16 * nv // 2)

            @block.scalar
            def _(act):
                act.wait_ge(ctx_in, 16)
                for c in range(C):
                    act.activation(ch[:, c], craw[:, c], ACT.Copy).then_inc(hi_done, 1)
                for i in range(4):
                    act.wait_ge(w_in[i], 16)
                    for c in range(C):
                        act.activation(wh[:, i, c], raw[:, i, c], ACT.Copy).then_inc(hi_done, 1)
                act.wait_ge(bias_in, 32)
                nk = 0
                for n, (lay, kind, u) in enumerate(units):
                    if kind == "k":
                        act.wait_ge(full[n % 2], n // 2 + 1)
                        if nk >= 2:
                            act.wait_ge(k_st[nk % 2], 32 * (nk // 2))
                        bias = bk[:, u // 2:u // 2 + 1] if lay else 0.0
                        act.activation(kh[:, nk % 2, :], bank[n % 2][:, 0:HALF], ACT.Identity, bias=bias)\
                           .then_inc(k_hi, 1)
                        nk += 1

            @block.vector
            def _(dve):
                for i in range(5):
                    for c in range(C):
                        dve.wait_ge(hi_done, C * i + c + 1)
                        if i == 0:
                            dve.tensor_tensor(cl[:, c], craw[:, c], f(ch[:, c]), ALU.subtract).then_inc(lo_done, 1)
                        else:
                            dve.tensor_tensor(wl[:, i - 1, c], raw[:, i - 1, c], f(wh[:, i - 1, c]),
                                              ALU.subtract).then_inc(lo_done, 1)
                dve.wait_ge(bias_in, 32)
                nk = nv = 0
                for n, (lay, kind, u) in enumerate(units):
                    src = bank[n % 2]
                    if kind == "k":
                        dve.wait_ge(k_hi, nk + 1)
                        if nk >= 2:
                            dve.wait_ge(k_st[nk % 2], 32 * (nk // 2))
                        bias = bk[:, u // 2:u // 2 + 1] if lay else 0.0
                        dve.scalar_tensor_tensor(out=kl[:, nk % 2, :], in0=src[:, 0:HALF], scalar=bias,
                                                 in1=f(kh[:, nk % 2, :]), op0=ALU.add, op1=ALU.subtract)\
                           .then_inc(free[n % 2], 1)
                        nk += 1
                    else:
                        dve.wait_ge(full[n % 2], n // 2 + 1)
                        if nv >= 2:
                            dve.wait_ge(v_st[nv % 2], 16 * (nv // 2))
                        if lay:
                            dve.tensor_tensor(vo[:, nv % 2, :], src[0:S2, :], bv[:, :], ALU.add)\
                               .then_inc(free[n % 2], 1)
                        else:
                            dve.tensor_copy(vo[:, nv % 2, :], src[0:S2, :])\
                               .then_inc(free[n % 2], 1)
                        nv += 1

            @block.tensor
            def _(pe):
                for n, (lay, kind, u) in enumerate(units):
                    i = 2 * lay + (kind == "v")
                    pe.wait_ge(lo_done, C * (i + 2))
                    pe.wait_ge(free[n % 2], n // 2)
                    if kind == "k":
                        m, half = u // 2, u % 2
                        cols = slice(half * HALF, (half + 1) * HALF)
                        last = three_passes(
                            pe, bank[n % 2][:, 0:HALF],
                            lambda c: (wh[:, i, c, m * P:(m + 1) * P], wl[:, i, c, m * P:(m + 1) * P]),
                            lambda c: (ch[:, c, cols], cl[:, c, cols]))
                    else:
                        cols = slice(u * S2, (u + 1) * S2)
                        last = three_passes(pe, bank[n % 2][0:S2, :],
                                            lambda c: (ch[:, c, cols], cl[:, c, cols]),
                                            lambda c: (wh[:, i, c, :], wl[:, i, c, :]))
                    last.then_inc(full[n % 2], 1)


class Uses:

    def __init__(self, before, turn, last):
        self.before, self.turn, self.last = before, turn, last

    def n(self, i, kind, k):
        names = self.before if i is None else self.last if isinstance(i, int) and i == B - 1 else self.turn
        at = [x for x, name in enumerate(names) if name == kind][k]
        return at if i is None else i * len(self.turn) + (len(self.before) + at)


def attention(nc, lay, io):
    route, merge = lay == 0, lay == 1
    if route:
        TP = Uses(["ln1"] * 2, ["ln1"] * 2 + ["bc"] * 2 + ["ln2"] * 2 + ["bd"] * 2,
                  ["bc"] * 2 + ["ln2"] * 2 + ["bd"] * 2)
        PJ = Uses(["q"] * 2, ["pv"] * 2 + ["q"] * 2 + ["o"] * 2, ["pv"] * 2 + ["o"] * 2)
        SM = Uses([], ["sum", "logits"], ["sum", "logits"])
    else:
        TP = Uses(["ln1"] * 2, ["ln1"] * 2 + ["bc"] * 2, ["bc"] * 2)
        PJ = Uses(["merge", "merge", "q", "q"], ["merge", "pv", "merge", "pv", "q", "q", "o", "o"],
                  ["pv", "pv", "o", "o"])
        SM = Uses([], ["sum"], ["sum"])
    SC = Uses(["max"] * 8, ["score"] * 8 + ["max"] * 8, ["score"] * 8)
    MT = Uses(["mt"], ["mt"], [])

    with ExitStack() as ctx:
        sb, banks, sem = tools(nc, ctx)
        n_ = lambda s: f"a{lay}_{s}"
        wqh, wql = sb(n_("wqh"), [P, C, D], F32R), sb(n_("wql"), [P, C, D], F32R)
        woh, wol = sb(n_("woh"), [P, C, D], F32R), sb(n_("wol"), [P, C, D], F32R)
        ident, mhalf = sb(n_("ident"), [P, P]), sb(n_("mhalf"), [P, NT])
        gate = sb(n_("gate"), [P, 2])
        x2 = sb(n_("x2"), [P, 2, NT, D])
        xn = sb(n_("xn"), [P, NT, D])
        stats, mv = sb(n_("stats"), [P, NT, 6]), sb(n_("mv"), [P, NT, 2])
        mark = sb(n_("mark"), [P, 1])
        ve, rstd = sb(n_("ve"), [P, 2, NT]), sb(n_("rstd"), [P, 2, NT])
        xth, xtl = sb(n_("xth"), [P, C, T], F32R), sb(n_("xtl"), [P, C, T], F32R)
        qh, ql = sb(n_("qh"), [P, C, T], F32R), sb(n_("ql"), [P, C, T], F32R)
        qs = sb(n_("qs"), [STACK, H, T], F32R)
        ks = sb(n_("ks"), [STACK, H, S2], F32R)
        kbd = sb(n_("kbd"), [P, C, HJ * S2], F32R)
        v = sb(n_("v"), [S2, D])
        pick = sb(n_("pick"), [S2, HJ, DK])
        bc = sb(n_("bc"), [P, C, P], F32R)
        part = sb(n_("part"), [P, 1])
        pr = sb(n_("pr"), [S2, RING, T])
        mx, mt = sb(n_("mx"), [P, NT, H]), sb(n_("mt"), [H, T], F32R)
        rs, rx = sb(n_("rs"), [P, T]), sb(n_("rx"), [P, T], F32R)
        pvs, ao = sb(n_("pvs"), [P, C, T]), sb(n_("ao"), [P, 2, T])
        ath, atl = sb(n_("ath"), [P, C, T], F32R), sb(n_("atl"), [P, C, T], F32R)
        if route:
            wch, wcl = sb(n_("wch"), [P, C, ES], F32R), sb(n_("wcl"), [P, C, ES], F32R)
            bcol, tie = sb(n_("bcol"), [P, 1]), sb(n_("tie"), [P, G])
            lg, gmax = sb(n_("lg"), [P, T]), sb(n_("gmax"), [P, GB])
            perm = sb(n_("perm"), [P, T])
            gmask = sb(n_("gmask"), [P, GT])
            bd = sb(n_("bd"), [P, 2, ES, GT], F32R)
        else:
            bq = sb(n_("bq"), [P, C])
            mcol_i = sb(n_("mcol_i"), [S2, B], I32)
            mall_i = pvs[0:S2].rearrange("p c t -> p (c t)")[:, 0:B * S2].bitcast(I32)
            mall_f = pr[:, :, :].rearrange("p h t -> p (h t)")[:, 0:B * S2]
            rows_, ones = sb(n_("rows"), [DK + 1, 2 * D], F32R), sb(n_("ones"), [DK + 1, P], F32R)
            mrow = rows_[0:1, 0:B * S2].rearrange("p (b s) -> p b s", b=B)
            bo = rows_[DK:DK + 1, :].rearrange("p (a n) -> p a n", a=2)
            bo_raw = xn[DK:DK + 1, 0, :]
            mall = sb(n_("mall"), [S2, B])
            kscale, kbias, kcur = sb(n_("kscale"), [S2, B]), sb(n_("kbias"), [S2, B]), sb(n_("kcur"), [S2, 2])
            rp = sb(n_("rp"), [ES, 2, RG, D])
            permb = sb(n_("permb"), [ES, T])
            b2 = sb(n_("b2"), [ES, D])

        ps = banks(*(n_(b) for b in ("sc0", "sc1", "tp0", "tp1", "pj0", "pj1", "sm", "x")))
        bank = {k: ps[n_(k)] for k in ("sc0", "sc1", "tp0", "tp1", "pj0", "pj1", "sm", "x")}
        full = {k: sem(n_("full_" + k)) for k in bank}
        free = {k: sem(n_("free_" + k)) for k in bank}
        x_in, x_st = sem(n_("x_in")), sem(n_("x_st"))
        k_in, kbd_in, v_in = sem(n_("k_in")), sem(n_("kbd_in")), sem(n_("v_in"))
        w_in = [sem(n_(f"w_in{i}")) for i in range(3)]
        c_in = sem(n_("c_in"))
        w_hi, w_lo, const = sem(n_("w_hi")), sem(n_("w_lo")), sem(n_("const"))
        ve_done, rstd_done = sem(n_("ve_done")), sem(n_("rstd_done"))
        xn1, xn2 = sem(n_("xn1")), sem(n_("xn2"))
        xt_hi, q_hi, a_hi, a_lo = sem(n_("xt_hi")), sem(n_("q_hi")), sem(n_("a_hi")), sem(n_("a_lo"))
        q_stacked, m_stacked = sem(n_("q_stacked")), sem(n_("m_stacked"))
        exps, dchain, fchain = sem(n_("exps")), sem(n_("dchain")), sem(n_("fchain"))
        if route:
            xn_st, perm_st = sem(n_("xn_st")), sem(n_("perm_st"))
            bd_st = [sem(n_(f"bd_st{i}")) for i in range(2)]
            permed = sem(n_("permed"))
        else:
            kcur_done = sem(n_("kcur_done"))
            rp_in, permb_in = [sem(n_(f"rp_in{i}")) for i in range(2)], sem(n_("permb_in"))

        last_turn = lambda i: isinstance(i, int) and i == B - 1

        def xt_base(i, which):
            per = 2 * C if route else C
            if which == 1:
                return 0 if i is None else C + per * i
            return C + per * i + (0 if last_turn(i) else C)

        with nc.Block() as block:
            @block.sync
            def _(sp):
                rows = lambda w: w.rearrange("(c p) n -> p c n", p=P)
                sp.dma_start(x2[:, 0], rows(io["wq"])).then_inc(w_in[0], 16)
                sp.dma_start(x2[:, 1], rows(io["wo"])).then_inc(w_in[1], 16)
                n_const = 2
                sp.dma_start(gate[:, 0:1], io["gate"].partition_broadcast(P)).then_inc(c_in, 16)
                sp.dma_start(gate[:, 1:2], io["gate_before"].partition_broadcast(P)).then_inc(c_in, 16)
                if route:
                    sp.dma_start(xn[:, 0, :].rearrange("p (c n) -> p c n", c=C), rows(io["wc"])).then_inc(w_in[2], 16)
                    sp.dma_start(bcol[:, :], io["bc"].rearrange("(p a) -> p a", a=1)).then_inc(c_in, 16)
                    sp.dma_start(tie[:, :], io["tie"].partition_broadcast(P)).then_inc(c_in, 16)
                    n_const += 2
                else:
                    sp.dma_start(bq[:, :], io["bq"]).then_inc(c_in, 16)
                    sp.dma_start(bo_raw, io["bo"].rearrange("(a n) -> a n", a=1)).then_inc(c_in, 16)
                    sp.dma_start(mcol_i[:, :], io["mask_t"]).then_inc(c_in, 16)
                    sp.dma_start(mall_i, io["mask"].rearrange("b s -> (b s)").partition_broadcast(S2))\
                      .then_inc(c_in, 16)
                    sp.dma_start(b2[:, :], io["b2"]).then_inc(c_in, 16)
                    n_const += 5

                def load_x(j):
                    sp.dma_start(x2[:, j % 2], io["x"][j].rearrange("(t p) d -> p t d", p=P)).then_inc(x_in, 16)

                def load_keys(j):
                    cols = bass.ds(j * S2, S2)
                    for r, k in enumerate((io["kh"], io["kl"], io["kh"])):
                        sp.dma_start(f(ks[r * DK:(r + 1) * DK]), k.rearrange("(h p) s -> p h s", p=DK)[:, :, cols])\
                          .then_inc(k_in, 16)

                def load_max_keys(j):
                    cols = bass.ds(j * S2, S2)
                    src = io["kh"].rearrange("(c j p) s -> j p c s", p=DK, j=HJ)
                    for a in range(HJ):
                        sp.dma_start(f(kbd[a * DK:(a + 1) * DK, :, a * S2:(a + 1) * S2]), src[a][:, :, cols])\
                          .then_inc(kbd_in, 16)

                def load_v(j):
                    sp.dma_start(v[:, :], io["v"][bass.ds(j * S2, S2), :]).then_inc(v_in, 16)

                def load_experts(j, t):
                    for a in range(2):
                        sp.dma_start(rp[:, a], io["rp"][bass.ds(j * GB + t * GT + a * RG, RG)].rearrange(
                            "n e d -> e n d")).then_inc(rp_in[a], 16)

                def load_perm(j):
                    sp.dma_start(permb[:, :], io["perm"][:, bass.ds(j * T, T)]).then_inc(permb_in, 16)

                def stack_queries(i, j):
                    for k in range(2):
                        sp.wait_ge(free[f"pj{k}"], PJ.n(i, "q", 1) + 1)
                    for r, q in enumerate((qh, qh, ql)):
                        for a in range(HJ):
                            sp.dma_start(f(qs[r * DK:(r + 1) * DK]).rearrange("p (c a) t -> p c a t", a=HJ)[:, :, a],
                                         f(q[a * DK:(a + 1) * DK])).then_inc(q_stacked, 16)

                def stack_max(i):
                    sp.wait_ge(free["x"], MT.n(i, "mt", 0) + 1)
                    sp.dma_start(f(qs[3 * DK:STACK]).rearrange('a h t -> a (h t)'), f(mt[:, :])).then_inc(m_stacked, 16)

                sp.wait_ge(w_lo, 2 * C + (1 if route else 1))
                load_x(0)
                load_keys(0)
                sp.wait_ge(const, 1)
                load_max_keys(0)
                load_v(0)
                if merge:
                    load_perm(0)
                    for t in range(NT):
                        if t:
                            sp.wait_ge(full[f"pj{(t - 1) % 2}"], PJ.n(None, "merge", (t - 1) // 2) + 1)
                        load_experts(0, t)
                stack_queries(None, 0)
                stack_max(None)
                if merge:
                    sp.wait_ge(full["pj1"], PJ.n(None, "merge", 1) + 1)
                    load_perm(1)
                    load_experts(1, 0)

                def turn(i):
                    last = last_turn(i)
                    if not last:
                        if not (isinstance(i, int) and i == 0):
                            sp.wait_ge(x_st, 16 * i)
                        load_x(i + 1)
                        load_max_keys(i + 1)
                        if merge:
                            for t in range(1, NT):
                                sp.wait_ge(full[f"pj{(t - 1) % 2}"], PJ.n(i, "merge", (t - 1) // 2) + 1)
                                load_experts(i + 1, t)
                        for k in range(2):
                            sp.wait_ge(full[f"sc{k}"], SC.n(i, "score", 7) + 1)
                        load_keys(i + 1)
                        for k in range(2):
                            sp.wait_ge(full[f"pj{k}"], PJ.n(i, "pv", 1) + 1)
                        load_v(i + 1)
                        stack_queries(i, i + 1)
                        stack_max(i)
                    for k in range(2):
                        sp.wait_ge(free[f"pj{k}"], PJ.n(i, "o", 1) + 1)
                    sp.dma_start(io["x_out"][i].rearrange("(t p) d -> p t d", p=P), x2[:, i % 2]).then_inc(x_st, 16)
                    if merge and not last:
                        sp.wait_ge(full["pj1"], PJ.n(i, "merge", 1) + 1)
                        if not (isinstance(i, int) and i == B - 2):
                            load_perm(i + 2)
                            load_experts(i + 2, 0)
                    if route:
                        sp.wait_ge(xn2, NT * (i + 1))
                        sp.dma_start(io["xn_out"][i].rearrange("(t p) d -> p t d", p=P), xn[:, :, :])\
                          .then_inc(xn_st, 16)
                        sp.wait_ge(permed, i + 1)
                        sp.dma_start(io["perm"][:, bass.ds(i * T, T)], perm[:, :]).then_inc(perm_st, 16)
                        for t in range(NT):
                            sp.wait_ge(free[f"tp{t % 2}"], TP.n(i, "bd", t // 2) + 1)
                            sp.dma_start(io["bd"][:, i * NT + t], f(bd[:, t % 2])).then_inc(bd_st[t % 2], 16)

                if merge:
                    with sp.Fori(0, B - 2) as i:
                        turn(i)
                    turn(B - 2)
                else:
                    with sp.Fori(0, B - 1) as i:
                        turn(i)
                turn(B - 1)
                sp.wait_ge(x_st, 16 * B)
                if route:
                    sp.wait_ge(xn_st, 16 * B)
                    sp.wait_ge(perm_st, 16 * B)
                    for k in range(2):
                        sp.wait_ge(bd_st[k], 16 * B * NT // 2)

            @block.gpsimd
            def _(pool):
                steps = Steps(pool, fchain)
                steps.link(pool.memset(ident[:, :], 0.0))
                steps.link(pool.affine_select(out=ident[:, :], in_=ident[:, :], compare_op=ALU.not_equal, fill=1.0,
                                              base=0, pattern=[[-1, P]], channel_multiplier=1))
                steps.link(pool.memset(f(kbd[:, :, :]), 0.0))
                steps.link(pool.memset(f(ks[3 * DK:STACK]), 1.0))
                steps.link(pool.memset(mhalf[:, :], -0.5))
                steps.link(pool.memset(pick[:, :, :], 0.0))
                for g in range(HJ):
                    steps.link(pool.memset(pick[:, g].rearrange("p (a b) -> p a b", b=HJ)[:, :, g:g + 1], 1.0))
                steps.link(pool.memset(part[:, :], -1.0))
                for j in range(HJ):
                    steps.link(pool.memset(part[j * DK:j * DK + C], 0.0))
                spread = ao[:, 0, :].rearrange("p (g c) -> p g c", g=C)
                steps.link(pool.memset(spread, 0.0))
                for g in range(C):
                    view = spread[:, g].rearrange("p (j i) -> p j i", i=DK)
                    for row in (g, C + g):
                        steps.link(pool.affine_select(out=view, in_=view, compare_op=ALU.not_equal, fill=1.0,
                                                      base=-row, pattern=[[-DK, HJ], [0, DK]],
                                                      channel_multiplier=1))
                steps.link(pool.tensor_copy(bc[:, :, :], spread))
                if route:
                    steps.link(pool.memset(gmask[:, :], 0.0))
                    for a in range(GT):
                        steps.link(pool.memset(gmask[a * G:(a + 1) * G, a:a + 1], 1.0))
                else:
                    pool.memset(f(ones[:, :]), 1.0)
                pool.drain().then_inc(const, 1)

                def power(done, which, count):
                    pool.wait_ge(ve_done, count + 1)
                    pool.tensor_tensor(rstd[:, which, :], ve[:, which, :], mhalf[:, :], ALU.pow).then_inc(rstd_done, 1)

                per = 2 if route else 1
                power(rstd_done, 0, 0)
                if merge:
                    pool.wait_ge(w_lo, 2 * C + 1)

                def turn(i):
                    last = last_turn(i)
                    if merge:
                        pool.tensor_copy(kcur[:, 0:1], kscale[:, bass.ds(i, 1)]).then_inc(kcur_done, 1)
                        pool.tensor_copy(kcur[:, 1:2], kbias[:, bass.ds(i, 1)]).then_inc(kcur_done, 1)
                    if not last:
                        power(rstd_done, 0, 1 + per * i)
                    for g in range(C):
                        pool.wait_ge(a_hi, C * i + g + 1)
                        pool.tensor_tensor(atl[:, g], ao[:, g % 2], f(ath[:, g]), ALU.subtract).then_inc(a_lo, 1)
                    if route:
                        power(rstd_done, 1, 1 + per * i + (0 if last else 1))

                with pool.Fori(0, B - 1) as i:
                    turn(i)
                turn(B - 1)

            @block.scalar
            def _(act):
                for i, (hi, raw) in enumerate(((wqh, x2[:, 0]), (woh, x2[:, 1]))):
                    act.wait_ge(w_in[i], 16)
                    for c in range(C):
                        act.activation(hi[:, c], raw[:, c], ACT.Copy).then_inc(w_hi, 1)
                if route:
                    act.wait_ge(w_in[2], 16)
                    act.activation(wch[:, :, :], xn[:, 0, :].rearrange("p (c n) -> p c n", c=C), ACT.Copy)\
                       .then_inc(w_hi, 1)
                act.wait_ge(c_in, 16 * (4 if route else 7))
                if merge:
                    act.activation(bo[:, 0, :], bo_raw, ACT.Copy).then_inc(w_hi, 1)
                act.activation(gate[:, :], gate[:, :], ACT.Tanh).then_inc(w_hi, 1)

                def transposed(i, which):
                    for c in range(C):
                        kind = "ln1" if which == 1 else "ln2"
                        act.wait_ge(full[f"tp{c % 2}"], TP.n(i, kind, c // 2) + 1)
                        act.activation(xth[:, c], bank[f"tp{c % 2}"][:, :], ACT.Copy).then_inc(xt_hi, 1)

                def queries(i, j, ms):
                    for m in ms:
                        act.wait_ge(full[f"pj{m % 2}"], PJ.n(i, "q", m // 2) + 1)
                        act.activation(qh[:, m], bank[f"pj{m % 2}"][:, :], ACT.Identity,
                                       bias=bq[:, m:m + 1] if merge else 0.0).then_inc(q_hi, 1)

                def negated_max(i):
                    act.wait_ge(full["x"], MT.n(i, "mt", 0) + 1)
                    act.activation(mt[:, :], bank["x"][0:H, :], ACT.Copy, scale=-1.0).then_inc(free["x"], 1)

                act.wait_ge(w_lo, 2 * C + 1)
                transposed(None, 1)
                queries(None, 0, range(C))
                negated_max(None)

                def turn(i):
                    last = last_turn(i)

                    def exp(h):
                        act.wait_ge(full[f"sc{h % 2}"], SC.n(i, "score", h // 2) + 1)
                        if h >= RING:
                            g = (h - RING) // HJ
                            act.wait_ge(full[f"pj{g % 2}"], PJ.n(i, "pv", g // 2) + 1)
                        src = bank[f"sc{h % 2}"][0:S2, :]
                        if merge:
                            act.activation(pr[:, h % RING, :], src, ACT.Exp, scale=kcur[:, 0:1], bias=kcur[:, 1:2]).then_inc(free[f"sc{h % 2}"], 1)
                        else:
                            act.activation(pr[:, h % RING, :], src, ACT.Exp, scale=SCALE)\
                               .then_inc(free[f"sc{h % 2}"], 1)

                    def values(g):
                        act.wait_ge(full[f"pj{g % 2}"], PJ.n(i, "pv", g // 2) + 1)
                        act.activation(pvs[:, g], bank[f"pj{g % 2}"][:, :], ACT.Copy).then_inc(free[f"pj{g % 2}"], 1)

                    if merge:
                        act.wait_ge(kcur_done, 2 * (i + 1))
                    for h in range(8):
                        exp(h)
                    values(0)
                    for h in range(8, 12):
                        exp(h)
                    values(1)
                    for h in range(12, 16):
                        exp(h)
                    values(2)
                    values(3)
                    if not last:
                        transposed(i, 1)
                        queries(i, i + 1, range(2))
                    for g in range(C):
                        act.wait_ge(free[f"tp{g % 2}"], TP.n(i, "bc", g // 2) + 1)
                        act.activation(ath[:, g], ao[:, g % 2], ACT.Copy).then_inc(a_hi, 1)
                    if not last:
                        queries(i, i + 1, range(2, C))
                        negated_max(i)
                    if route:
                        transposed(i, 2)

                with act.Fori(0, B - 1) as i:
                    turn(i)
                turn(B - 1)

            @block.vector
            def _(dve):
                steps = Steps(dve, dchain)
                for i, (hi, lo, raw) in enumerate(((wqh, wql, x2[:, 0]), (woh, wol, x2[:, 1]))):
                    for c in range(C):
                        dve.wait_ge(w_hi, C * i + c + 1)
                        dve.tensor_tensor(lo[:, c], raw[:, c], f(hi[:, c]), ALU.subtract).then_inc(w_lo, 1)
                dve.wait_ge(w_hi, 2 * C + 2)
                if route:
                    dve.tensor_tensor(wcl[:, :, :], xn[:, 0, :].rearrange("p (c n) -> p c n", c=C), f(wch[:, :, :]),
                                      ALU.subtract).then_inc(w_lo, 1)
                else:
                    dve.tensor_scalar(mrow, mall_i[0:1].rearrange("a (b s) -> a b s", b=B), 0.0, -BIG,
                                      ALU.is_equal, ALU.mult)
                    steps.link(dve.tensor_scalar(mall_f, mall_i, 0.0, None, ALU.is_equal))
                    steps.link(dve.tensor_reduce(mall[:, :], mall_f.rearrange("p (b s) -> p b s", b=B), AX.X,
                                                 ALU.min))
                    steps.link(dve.tensor_scalar(mall[:, :], mall[:, :], BIG, -BIG, ALU.mult, ALU.add))
                    steps.link(dve.tensor_scalar(kbias[:, :], mcol_i[:, :], 0.0, None, ALU.is_equal))
                    steps.link(dve.tensor_scalar(kscale[:, :], kbias[:, :], -SCALE, SCALE, ALU.mult, ALU.add))
                    steps.link(dve.tensor_tensor(kbias[:, :], kbias[:, :], mall[:, :], ALU.mult))
                    dve.tensor_tensor(bo[:, 1, :], bo_raw, f(bo[:, 0, :]), ALU.subtract).then_inc(w_lo, 1)
                dve.wait_ge(const, 1)
                LN1, LN2, LOG = LN_STEPS, (LN_STEPS if route else 0), (1 if route else 0)
                TURN = LN1 + LN2 + LOG + 2

                def norm(steps, x, which, count, done):
                    steps.count(dve.memset(mark[:, :], 0.0))
                    for t in range(NT):
                        ins = dve.bn_stats(stats[:, t, :], x[:, t, :])
                    steps.link(ins)
                    steps.count(dve.memset(mark[:, :], 0.0))
                    for t in range(NT):
                        ins = dve.bn_aggr(mv[:, t, :], stats[:, t, :])
                    steps.link(ins)
                    dve.tensor_scalar(ve[:, which, :], mv[:, :, 1], EPS, None, ALU.add).then_inc(ve_done, 1)
                    dve.wait_ge(rstd_done, count + 1)
                    for t in range(NT):
                        dve.tensor_scalar(xn[:, t, :], x[:, t, :], mv[:, t, 0:1], rstd[:, which, t:t + 1],
                                          ALU.subtract, ALU.mult).then_inc(done, 1)

                def merged(i, j, t):
                    dve.wait_ge(full[f"pj{t % 2}"], PJ.n(i, "merge", t // 2) + 1)
                    xt = x2[:, j % 2, t]
                    dve.scalar_tensor_tensor(out=xt, in0=bank[f"pj{t % 2}"][:, :], scalar=gate[:, 1:2], in1=xt,
                                             op0=ALU.mult, op1=ALU.add).then_inc(free[f"pj{t % 2}"], 1)

                def transposed(i, which):
                    kind = "ln1" if which == 1 else "ln2"
                    for c in range(C):
                        dve.wait_ge(xt_hi, xt_base(i, which) + c + 1)
                        dve.tensor_tensor(xtl[:, c], bank[f"tp{c % 2}"][:, :], f(xth[:, c]), ALU.subtract)\
                           .then_inc(free[f"tp{c % 2}"], 1)

                def queries(i, j, ms):
                    for m in ms:
                        dve.wait_ge(q_hi, C * j + m + 1)
                        src, dst = bank[f"pj{m % 2}"][:, :], ql[:, m]
                        if merge:
                            ins = dve.scalar_tensor_tensor(out=dst, in0=src, scalar=bq[:, m:m + 1], in1=f(qh[:, m]),
                                                           op0=ALU.add, op1=ALU.subtract)
                        else:
                            ins = dve.tensor_tensor(dst, src, f(qh[:, m]), ALU.subtract)
                        ins.then_inc(free[f"pj{m % 2}"], 1)

                def maxima(i, k):
                    m, t = k // NT, k % NT
                    dve.wait_ge(full[f"sc{k % 2}"], SC.n(i, "max", k // 2) + 1)
                    dve.tensor_reduce(mx[:, t, m * HJ:(m + 1) * HJ],
                                      bank[f"sc{k % 2}"][:, 0:HJ * S2].rearrange("p (a s) -> p a s", a=HJ), AX.X,
                                      ALU.max).then_inc(free[f"sc{k % 2}"], 1)

                dve.wait_ge(x_in, 16)
                if merge:
                    for t in range(NT):
                        merged(None, 0, t)
                    for k in range(2):
                        dve.wait_ge(free[f"pj{k}"], PJ.n(None, "merge", 1) + 1)
                norm(steps, x2[:, 0], 0, 0, xn1)
                transposed(None, 1)
                queries(None, 0, range(C))
                for k in range(4 * NT):
                    maxima(None, k)
                BEFORE = steps.n

                def turn(i):
                    last = last_turn(i)
                    steps = Steps(dve, dchain, BEFORE + TURN * i)
                    per = 2 if route else 1
                    if not last:
                        j = i + 1
                        dve.wait_ge(x_in, 16 * (j + 1))
                        if merge:
                            for t in range(NT):
                                merged(i, j, t)
                            for k in range(2):
                                dve.wait_ge(free[f"pj{k}"], PJ.n(i, "merge", 1) + 1)
                        if route and not (isinstance(i, int) and i == 0):
                            dve.wait_ge(xn_st, 16 * i)
                        norm(steps, x2[:, j % 2], 0, 1 + per * i, xn1)
                        transposed(i, 1)
                    dve.wait_ge(full["sm"], SM.n(i, "sum", 0) + 1)
                    steps.link(dve.reciprocal(rs[:, :], bank["sm"][:, :]))
                    steps.link(dve.tensor_copy(rx[:, :], rs[:, :]))
                    dve.scalar_tensor_tensor(out=rx[:, :], in0=f(rx[:, :]), scalar=part[:, 0:1], in1=rs[:, :],
                                             op0=ALU.mult, op1=ALU.add).then_inc(free["sm"], 1)
                    if not last:
                        queries(i, j, range(2))
                    for g in range(C):
                        dve.wait_ge(full[f"tp{g % 2}"], TP.n(i, "bc", g // 2) + 1)
                        dve.wait_ge(free[f"pj{g % 2}"], PJ.n(i, "pv", g // 2) + 1)
                        if g >= 2:
                            dve.wait_ge(a_lo, C * i + g - 1)
                        dve.tensor_tensor(ao[:, g % 2], bank[f"tp{g % 2}"][:, :], pvs[:, g], ALU.mult)\
                           .then_inc(free[f"tp{g % 2}"], 1)
                    if not last:
                        queries(i, j, range(2, C))
                    for t in range(NT):
                        if not last:
                            for m in range(C):
                                maxima(i, NT * t + m)
                        dve.wait_ge(full[f"pj{t % 2}"], PJ.n(i, "o", t // 2) + 1)
                        xt = x2[:, i % 2, t]
                        dve.scalar_tensor_tensor(out=xt, in0=bank[f"pj{t % 2}"][:, :], scalar=gate[:, 0:1], in1=xt,
                                                 op0=ALU.mult, op1=ALU.add).then_inc(free[f"pj{t % 2}"], 1)
                    if route:
                        for k in range(2):
                            dve.wait_ge(free[f"pj{k}"], PJ.n(i, "o", 1) + 1)
                        norm(steps, x2[:, i % 2], 1, 1 + per * i + (0 if last else 1), xn2)
                        transposed(i, 2)
                        dve.wait_ge(full["sm"], SM.n(i, "logits", 0) + 1)
                        grouped = lambda a: a.rearrange("p (n t) -> p n t", t=G)
                        dve.scalar_tensor_tensor(out=grouped(lg[:, :]), in0=grouped(bank["sm"][:, :]),
                                                 scalar=bcol[:, 0:1],
                                                 in1=tie[:, :].unsqueeze(1).broadcast_to([P, GB, G]),
                                                 op0=ALU.add, op1=ALU.add).then_inc(free["sm"], 1)
                        dve.wait_ge(free["sm"], SM.n(i, "logits", 0) + 1)
                        steps.link(dve.tensor_reduce(gmax[:, :], grouped(lg[:, :]), AX.X, ALU.max))
                        if not (isinstance(i, int) and i == 0):
                            dve.wait_ge(perm_st, 16 * i)
                        dve.tensor_tensor(grouped(perm[:, :]), grouped(lg[:, :]),
                                          gmax[:, :].unsqueeze(2).broadcast_to([P, GB, G]), ALU.is_equal)\
                           .then_inc(permed, 1)
                        for t in range(NT):
                            dve.wait_ge(full[f"tp{t % 2}"], TP.n(i, "bd", t // 2) + 1)
                            count = NT // 2 * i + t // 2
                            if not (isinstance(count, int) and count == 0):
                                dve.wait_ge(bd_st[t % 2], 16 * count)
                            dve.tensor_tensor(bd[:, t % 2],
                                              bank[f"tp{t % 2}"][:, 0:ES].unsqueeze(2).broadcast_to([P, ES, GT]),
                                              gmask[:, :].unsqueeze(1).broadcast_to([P, ES, GT]), ALU.mult)\
                               .then_inc(free[f"tp{t % 2}"], 1)

                with dve.Fori(0, B - 1) as i:
                    turn(i)
                turn(B - 1)

            @block.tensor
            def _(pe):
                pe.wait_ge(const, 1)
                pe.wait_ge(w_lo, 2 * C + 1)

                def transposes(i, which):
                    kind = "ln1" if which == 1 else "ln2"
                    if which == 1:
                        pe.wait_ge(xn1, NT * (1 if i is None else i + 2))
                    else:
                        pe.wait_ge(xn2, NT * (i + 1))
                    for c in range(C):
                        u = TP.n(i, kind, c // 2)
                        pe.wait_ge(free[f"tp{c % 2}"], u)
                        for t in range(NT):
                            last = pe.transpose(bank[f"tp{c % 2}"][:, t * P:(t + 1) * P], xn[:, t, c * P:(c + 1) * P],
                                                ident[:, :])
                        last.then_inc(full[f"tp{c % 2}"], 1)

                def transposed_ready(i, kind):
                    for k in range(2):
                        pe.wait_ge(free[f"tp{k}"], TP.n(i, kind, 1) + 1)

                def queries(i, ms):
                    for m in ms:
                        pe.wait_ge(free[f"pj{m % 2}"], PJ.n(i, "q", m // 2))
                        cols = slice(m * P, (m + 1) * P)
                        three_passes(pe, bank[f"pj{m % 2}"][:, :],
                                     lambda c: (wqh[:, c, cols], wql[:, c, cols]),
                                     lambda c: (xth[:, c, :], xtl[:, c, :])).then_inc(full[f"pj{m % 2}"], 1)

                def max_tile(i, j, k):
                    m, t = k // NT, k % NT
                    pe.wait_ge(free[f"sc{k % 2}"], SC.n(i, "max", k // 2))
                    if t == 0:
                        pe.wait_ge(q_hi, C * j + m + 1)
                    out = bank[f"sc{k % 2}"][:, 0:HJ * S2]
                    last = pe.matmul(out, qh[:, m, t * P:(t + 1) * P], kbd[:, m, :], start=True, stop=not merge)
                    if merge:
                        last = pe.matmul(out.rearrange("p (a s) -> p a s", a=HJ), ones[0:1, :],
                                         mrow[:, bass.ds(j, 1), :].broadcast_to([1, HJ, S2]), start=False, stop=True)
                    last.then_inc(full[f"sc{k % 2}"], 1)

                def max_rows(i):
                    for k in range(2):
                        pe.wait_ge(free[f"sc{k}"], SC.n(i, "max", 7) + 1)
                    pe.wait_ge(free["x"], MT.n(i, "mt", 0))
                    for t in range(NT):
                        last = pe.transpose(bank["x"][0:H, t * P:(t + 1) * P], mx[:, t, :], ident[:, :])
                    last.then_inc(full["x"], 1)

                def merge_tile(i, j, t):
                    pe.wait_ge(permb_in, 16 * (j + 1))
                    pe.wait_ge(free[f"pj{t % 2}"], PJ.n(i, "merge", t // 2))
                    out = bank[f"pj{t % 2}"]
                    pe.matmul(out[:, :], permb[:, t * P:(t + 1) * P], b2[:, :], start=True, stop=False,
                              skip_group_check=True)
                    for a in range(GT):
                        if a % RG == 0:
                            pe.wait_ge(rp_in[a // RG], 16 * (NT * j + t + 1))
                        col = t * P + a * G
                        last = pe.matmul(out[a * G:(a + 1) * G, :], permb[:, col:col + G], rp[:, a // RG, a % RG, :],
                                         start=False, stop=True, skip_group_check=True)
                    last.then_inc(full[f"pj{t % 2}"], 1)

                if merge:
                    for t in range(NT):
                        merge_tile(None, 0, t)
                transposes(None, 1)
                transposed_ready(None, "ln1")
                queries(None, range(C))
                pe.wait_ge(kbd_in, 16 * HJ)
                for k in range(C * NT):
                    max_tile(None, 0, k)
                max_rows(None)

                def turn(i):
                    last_ = last_turn(i)

                    def score(h):
                        pe.wait_ge(free[f"sc{h % 2}"], SC.n(i, "score", h // 2))
                        pe.matmul(bank[f"sc{h % 2}"][0:S2, :], ks[:, h, :], qs[:, h, :], start=True, stop=True)\
                          .then_inc(full[f"sc{h % 2}"], 1)

                    def values(g):
                        h = HJ * g + HJ - 1
                        for k in range(2):
                            pe.wait_ge(free[f"sc{k}"], SC.n(i, "score", h // 2) + 1)
                        pe.wait_ge(free[f"pj{g % 2}"], PJ.n(i, "pv", g // 2))
                        if g == 0:
                            pe.wait_ge(free["sm"], SM.n(i, "sum", 0))
                        for a in range(HJ):
                            ins = pe.matmul(bank["sm"][a * DK:(a + 1) * DK, :], pick[:, g, :],
                                            pr[:, (HJ * g + a) % RING, :], start=(g == 0), stop=(g == C - 1),
                                            skip_group_check=True)
                        if g == C - 1:
                            ins.then_inc(full["sm"], 1)
                        for a in range(HJ):
                            h = HJ * g + a
                            ins = pe.matmul(bank[f"pj{g % 2}"][a * DK:(a + 1) * DK, :], v[:, h * DK:(h + 1) * DK],
                                            pr[:, h % RING, :], start=True, stop=True)
                        ins.then_inc(full[f"pj{g % 2}"], 1)

                    def spread(g):
                        pe.wait_ge(free[f"tp{g % 2}"], TP.n(i, "bc", g // 2))
                        if g == 0:
                            pe.wait_ge(free["sm"], SM.n(i, "sum", 0) + 1)
                        pe.matmul(bank[f"tp{g % 2}"][:, :], bc[:, g, :], rx[:, :], start=True, stop=True)\
                          .then_inc(full[f"tp{g % 2}"], 1)

                    if merge and not last_:
                        merge_tile(i, i + 1, 0)
                        merge_tile(i, i + 1, 1)
                    pe.wait_ge(k_in, 48 * (i + 1))
                    pe.wait_ge(q_stacked, 16 * 3 * HJ * (i + 1))
                    pe.wait_ge(m_stacked, 16 * (i + 1))
                    for h in range(8):
                        score(h)
                    pe.wait_ge(v_in, 16 * (i + 1))
                    values(0)
                    for h in range(8, 12):
                        score(h)
                    values(1)
                    if merge and not last_:
                        merge_tile(i, i + 1, 2)
                        merge_tile(i, i + 1, 3)
                    for h in range(12, 16):
                        score(h)
                    values(2)
                    values(3)
                    if not last_:
                        transposes(i, 1)
                        transposed_ready(i, "ln1")
                        queries(i, range(2))
                    for g in range(C):
                        spread(g)
                    if not last_:
                        queries(i, range(2, C))
                        pe.wait_ge(kbd_in, 16 * HJ * (i + 2))
                    pe.wait_ge(a_lo, C * (i + 1))
                    for t in range(NT):
                        pe.wait_ge(free[f"pj{t % 2}"], PJ.n(i, "o", t // 2))
                        out, cols = bank[f"pj{t % 2}"][:, :], slice(t * P, (t + 1) * P)
                        if merge:
                            pe.matmul(out, ones[DK:DK + 1, :], bo[:, 0, :], start=True, stop=False)
                            pe.matmul(out, ones[DK:DK + 1, :], bo[:, 1, :], start=False, stop=False)
                        for m in range(C):
                            pe.matmul(out, ath[:, m, cols], woh[:, m, :], start=(route and m == 0), stop=False)
                            pe.matmul(out, ath[:, m, cols], wol[:, m, :], start=False, stop=False)
                            ins = pe.matmul(out, atl[:, m, cols], woh[:, m, :], start=False, stop=(m == C - 1))
                            if m == C - 1:
                                ins.then_inc(full[f"pj{t % 2}"], 1)
                            if not last_:
                                max_tile(i, i + 1, NT * t + m)
                    if not last_:
                        max_rows(i)
                    if route:
                        transposes(i, 2)
                        transposed_ready(i, "ln2")
                        pe.wait_ge(free["sm"], SM.n(i, "logits", 0))
                        three_passes(pe, bank["sm"][:, :], lambda c: (wch[:, c, :], wcl[:, c, :]),
                                     lambda c: (xth[:, c, :], xtl[:, c, :])).then_inc(full["sm"], 1)
                        pe.wait_ge(permed, i + 1)
                        for t in range(NT):
                            pe.wait_ge(free[f"tp{t % 2}"], TP.n(i, "bd", t // 2))
                            pe.transpose(bank[f"tp{t % 2}"][:, 0:ES], perm[:, t * P:(t + 1) * P], ident[:, :])\
                              .then_inc(full[f"tp{t % 2}"], 1)

                with pe.Fori(0, B - 1) as i:
                    turn(i)
                turn(B - 1)


def experts(nc, io):
    XQ = NTILE // 4
    NG4, NW = 4, 2
    WG = EK // 4
    with ExitStack() as outer:
        inner = outer.enter_context(nc.sbuf_tensor("e_inner", [P, EK, NG], F32))
        with ExitStack() as ctx:
            sb, banks, sem = tools(nc, ctx)
            bd = sb("e_bd", [P, NTILE, ES * GT], F32R)
            gt = sb("e_gt", [P, ES, NG])
            raw = sb("e_raw", [P, 2, XQ, P])
            xh, xl = sb("e_xh", [P, NTILE, P], F32R), sb("e_xl", [P, NTILE, P], F32R)
            w1 = sb("e_w1", [P, ES, EF])
            b1 = sb("e_b1", [P, EK])
            names = [f"e_g{i}" for i in range(NG4)] + [f"e_h{i}" for i in range(NW)]
            bank = banks(*names)
            full, free = {k: sem(k + "_full") for k in names}, {k: sem(k + "_free") for k in names}
            raw_in, w1_in, b1_in = [sem(f"e_raw_in{i}") for i in range(2)], sem("e_w1_in"), sem("e_b1_in")
            bd_in = [sem(f"e_bd_in{i}") for i in range(4)]
            x_hi, x_lo, init = sem("e_x_hi"), sem("e_x_lo"), sem("e_init")
            GU, WU = NTILE // NG4, WG // NW

            with nc.Block() as block:
                @block.sync
                def _(sp):
                    sp.dma_start(b1[:, :], io["b1"]).then_inc(b1_in, 16)

                    def load_tokens(c, q):
                        sp.dma_start(raw[:, q % 2], io["xn"][q * XQ:(q + 1) * XQ].rearrange("n p d -> p n d")[
                            :, :, bass.ds(c * P, P)]).then_inc(raw_in[q % 2], 16)

                    def load_choices(q):
                        sp.dma_start(f(bd[:, q * XQ:(q + 1) * XQ]), io["bd"].rearrange("p n e g -> p n (e g)")[
                            :, q * XQ:(q + 1) * XQ]).then_inc(bd_in[q], 16)

                    def load_w1(c):
                        sp.dma_start(w1[:, :, :], io["w1"][bass.ds(c * P, P), :].rearrange(
                            "p (e f) -> p e f", f=EF)).then_inc(w1_in, 16)

                    load_tokens(0, 0)
                    load_tokens(0, 1)
                    for q in range(4):
                        load_choices(q)
                        if q >= 2:
                            sp.wait_ge(x_lo, q - 1)
                            load_tokens(0, q)
                    load_w1(0)
                    with sp.Fori(0, C - 1) as c:
                        for q in range(4):
                            sp.wait_ge(x_lo, 4 * c + q + 3)
                            load_tokens(c + 1, q)
                        for w in range(NW):
                            sp.wait_ge(full[f"e_h{w}"], WU * (c + 1))
                        load_w1(c + 1)

                @block.scalar
                def _(act):
                    with act.Fori(0, C) as c:
                        for g in range(NG4):
                            act.wait_ge(full[f"e_g{g}"], GU * c)
                        for q in range(4):
                            act.wait_ge(raw_in[q % 2], 16 * (2 * c + q // 2 + 1))
                            act.activation(xh[:, q * XQ:(q + 1) * XQ], raw[:, q % 2], ACT.Copy).then_inc(x_hi, 1)
                        for w in range(NW):
                            act.wait_ge(full[f"e_h{w}"], WU * c)
                        for n in range(0, NTILE, 2):
                            k = n % NG4
                            act.wait_ge(full[f"e_g{k}"], GU * c + n // NG4 + 1)
                            act.activation(gt[:, :, n * GT:(n + 1) * GT],
                                           bank[f"e_g{k}"][:, :].rearrange("p (e g) -> p e g", g=GT), ACT.Copy)\
                               .then_inc(free[f"e_g{k}"], 1)

                @block.gpsimd
                def _(pool):
                    with pool.Fori(0, C) as c:
                        for q in range(4):
                            pool.wait_ge(x_hi, 4 * c + q + 1)
                            pool.tensor_tensor(xl[:, q * XQ:(q + 1) * XQ], raw[:, q % 2],
                                               f(xh[:, q * XQ:(q + 1) * XQ]), ALU.subtract).then_inc(x_lo, 1)

                @block.vector
                def _(dve):
                    dve.wait_ge(b1_in, 16)
                    dve.tensor_copy(inner[:, :, :], b1[:, :].unsqueeze(2).broadcast_to([P, EK, NG])).then_inc(init, 1)
                    dve.wait_ge(init, 1)
                    with dve.Fori(0, C) as c:
                        for w in range(NW):
                            dve.wait_ge(full[f"e_h{w}"], WU * c)
                        for n in range(1, NTILE, 2):
                            k = n % NG4
                            dve.wait_ge(full[f"e_g{k}"], GU * c + n // NG4 + 1)
                            dve.tensor_copy(gt[:, :, n * GT:(n + 1) * GT],
                                            bank[f"e_g{k}"][:, :].rearrange("p (e g) -> p e g", g=GT))\
                               .then_inc(free[f"e_g{k}"], 1)
                        for w in range(WG):
                            k = w % NW
                            dve.wait_ge(full[f"e_h{k}"], WU * c + w // NW + 1)
                            part = inner[:, 4 * w:4 * w + 4, :]
                            dve.tensor_tensor(part, bank[f"e_h{k}"][:, :].rearrange("p (k n) -> p k n", n=NG), part,
                                              ALU.add).then_inc(free[f"e_h{k}"], 1)

                @block.tensor
                def _(pe):
                    with pe.Fori(0, C) as c:
                        for n in range(NTILE):
                            k = n % NG4
                            if n % XQ == 0:
                                pe.wait_ge(bd_in[n // XQ], 16)
                                pe.wait_ge(x_lo, 4 * c + n // XQ + 1)
                            pe.wait_ge(free[f"e_g{k}"], GU * c + n // NG4)
                            pe.matmul(bank[f"e_g{k}"][:, :], xh[:, n, :], bd[:, n, :], start=True, stop=False)
                            pe.matmul(bank[f"e_g{k}"][:, :], xl[:, n, :], bd[:, n, :], start=False, stop=True)\
                              .then_inc(full[f"e_g{k}"], 1)
                        pe.wait_ge(w1_in, 16 * (c + 1))
                        for k in range(NG4):
                            pe.wait_ge(free[f"e_g{k}"], GU * (c + 1))
                        for w in range(WG):
                            k = w % NW
                            pe.wait_ge(free[f"e_h{k}"], WU * c + w // NW)
                            for b in range(4):
                                for a in range(EJ):
                                    e = (4 * w + b) * EJ + a
                                    ins = pe.matmul(bank[f"e_h{k}"][a * EF:(a + 1) * EF, b * NG:(b + 1) * NG],
                                                    w1[:, e, :], gt[:, e, :], start=True, stop=True,
                                                    skip_group_check=True)
                            ins.then_inc(full[f"e_h{k}"], 1)

        with ExitStack() as ctx:
            sb, banks, sem = tools(nc, ctx)
            diag = sb("o_diag", [P, 2, 4, EJ, NG])
            w2 = sb("o_w2", [P, 2, 4, D])
            out = sb("o_out", [NG, 4, EJ, D])
            names = [f"o_p{i}" for i in range(8)]
            bank = banks(*names)
            full, free = [sem(k + "_full") for k in names], [sem(k + "_free") for k in names]
            w2_in, out_st = [sem(f"o_w2_in{i}") for i in range(2)], [sem(f"o_out_st{i}") for i in range(4)]
            zero, diag_done = sem("o_zero"), sem("o_diag_done")
            NE = 16
            TURNS = WG // 2

            with nc.Block() as block:
                @block.sync
                def _(sp):
                    def load(g, s, first):
                        if not first:
                            for k in range(8):
                                sp.wait_ge(full[k], 4 * (g // 2) + 2 * s)
                        sp.dma_start(w2[:, s], io["w2"].rearrange("(k p) d -> p k d", p=P)[:, bass.ds(g * 4, 4)])\
                          .then_inc(w2_in[s], 16)

                    for s in range(2):
                        sp.dma_start(w2[:, s], io["w2"].rearrange("(k p) d -> p k d", p=P)[:, s * 4:s * 4 + 4])\
                          .then_inc(w2_in[s], 16)

                    def turn(u, last):
                        for s in range(2):
                            for q in range(4):
                                for k in range(4):
                                    sp.wait_ge(free[(4 * q + k) % 8], 4 * u + 2 * s + q // 2 + 1)
                                sp.dma_start(io["rp"][:, bass.ds(u * 2 * NE + s * NE + 4 * q, 4), :], out[:, q])\
                                  .then_inc(out_st[q], 16)
                            if not last:
                                for k in range(8):
                                    sp.wait_ge(full[k], 4 * u + 2 * s + 2)
                                sp.dma_start(w2[:, s], io["w2"].rearrange("(k p) d -> p k d", p=P)[
                                    :, bass.ds(u * 8 + 8 + s * 4, 4)]).then_inc(w2_in[s], 16)

                    with sp.Fori(0, TURNS - 1) as u:
                        turn(u, False)
                    turn(TURNS - 1, True)
                    for q in range(4):
                        sp.wait_ge(out_st[q], 16 * WG)

                def read_out(eng, copy, u, s, parity):
                    for e in range(parity, NE, 2):
                        k, q = e % 8, e // 4
                        eng.wait_ge(full[k], 4 * u + 2 * s + e // 8 + 1)
                        if e % 4 == parity:
                            eng.wait_ge(out_st[q], 16 * (2 * u + s))
                        copy(out[:, q, e % 4], bank[names[k]][:, :]).then_inc(free[k], 1)

                @block.gpsimd
                def _(pool):
                    pool.memset(diag[:, :, :, :, :], 0.0).then_inc(zero, 1)

                @block.scalar
                def _(act):
                    with act.Fori(0, TURNS) as u:
                        for s in range(2):
                            read_out(act, lambda o, x: act.activation(o, x, ACT.Copy), u, s, 0)

                @block.vector
                def _(dve):
                    dve.wait_ge(zero, 1)

                    def spread(u, s):
                        for a in range(EJ):
                            rows = slice(a * EF, (a + 1) * EF)
                            dve.tensor_scalar(diag[rows, s, :, a, :], inner[rows, bass.ds(u * 8 + s * 4, 4), :], 0.0,
                                              None, ALU.max).then_inc(diag_done, 1)

                    spread(0, 0)

                    def turn(u, last):
                        for s in range(2):
                            if s == 0:
                                for k in range(8):
                                    dve.wait_ge(full[k], 4 * u)
                                spread(u, 1)
                            elif not last:
                                for k in range(8):
                                    dve.wait_ge(full[k], 4 * u + 2)
                                spread(u + 1, 0)
                            read_out(dve, dve.tensor_copy, u, s, 1)

                    with dve.Fori(0, TURNS - 1) as u:
                        turn(u, False)
                    turn(TURNS - 1, True)

                @block.tensor
                def _(pe):
                    with pe.Fori(0, TURNS) as u:
                        for s in range(2):
                            pe.wait_ge(diag_done, EJ * (2 * u + s + 1))
                            pe.wait_ge(w2_in[s], 16 * (u + 1))
                            for e in range(NE):
                                k = e % 8
                                pe.wait_ge(free[k], 4 * u + 2 * s + e // 8)
                                pe.matmul(bank[names[k]][:, :], diag[:, s, e // EJ, e % EJ, :], w2[:, s, e // EJ, :],
                                          start=True, stop=True).then_inc(full[k], 1)


def feed_forward(nc, io):
    TP = Uses(["t"] * 2, ["t"] * 2, [])
    last_turn = lambda i: isinstance(i, int) and i == B - 1
    with ExitStack() as ctx:
        sb, banks, sem = tools(nc, ctx)
        wh, wl = sb("f_wh", [P, 3, C, D], F32R), sb("f_wl", [P, 3, C, D], F32R)
        ident, mhalf = sb("f_ident", [P, P]), sb("f_mhalf", [P, NT])
        mu, gate = sb("f_mu", [P, 2, C]), sb("f_gate", [P, 1])
        x4 = sb("f_x4", [P, 4, NT, D])
        xn = sb("f_xn", [P, NT, D])
        stats, mv = sb("f_stats", [P, NT, 6]), sb("f_mv", [P, NT, 2])
        mark = sb("f_mark", [P, 1])
        ve, rstd = sb("f_ve", [P, NT]), sb("f_rstd", [P, NT])
        xt, dif = sb("f_xt", [P, C, T + 1]), sb("f_dif", [P, C, T])
        mix = sb("f_mix", [P, 2, 2, T])
        xm = [[sb(f"f_xm{a}{b}", [P, C, T], F32R) for b in "hl"] for a in "kr"]
        ka, kk = sb("f_ka", [P, 2, T]), sb("f_kk", [P, 2, T])
        kh, kl = sb("f_kh", [P, C, T], F32R), sb("f_kl", [P, C, T], F32R)
        th, tmp = sb("f_th", [P, NT, D]), sb("f_tmp", [P, 2, D])
        names = [f"f_{a}{b}" for a in "tkrv" for b in range(2)]
        bank = banks(*names)
        full, free = {k: sem(k + "_full") for k in names}, {k: sem(k + "_free") for k in names}
        w_in, c_in, x_in, x_st = [sem(f"f_w_in{i}") for i in range(3)], sem("f_c_in"), sem("f_x_in"), sem("f_x_st")
        w_hi, w_lo, const, gated = sem("f_w_hi"), sem("f_w_lo"), sem("f_const"), sem("f_gated")
        ve_done, rstd_done, xn_done = sem("f_ve_done"), sem("f_rstd_done"), sem("f_xn_done")
        stored = sem("f_stored")
        mixed, mix_hi, mix_lo = ([sem(f"f_{n}{a}") for a in "kr"] for n in ("mixed", "mix_hi", "mix_lo"))
        squared, k_hi, k_lo = sem("f_squared"), sem("f_k_hi"), sem("f_k_lo")
        dchain, fchain, out_done = sem("f_dchain"), sem("f_fchain"), sem("f_out_done")

        with nc.Block() as block:
            @block.sync
            def _(sp):
                raws = (x4[:, 2], x4[:, 3], xn[:, :, :])
                for i in range(3):
                    sp.dma_start(raws[i], io["w"][i].rearrange("(c p) n -> p c n", p=P)).then_inc(w_in[i], 16)
                for i in range(2):
                    sp.dma_start(mu[:, i, :], io["mu"][i]).then_inc(c_in, 16)
                sp.dma_start(gate[:, :], io["gate"].partition_broadcast(P)).then_inc(c_in, 16)

                def load_x(j):
                    sp.dma_start(x4[:, j % 4], io["x"][j].rearrange("(t p) d -> p t d", p=P)).then_inc(x_in, 16)

                load_x(0)
                sp.wait_ge(x_in, 16)
                load_x(1)

                def turn(i):
                    if not isinstance(i, int):
                        sp.wait_ge(x_st, 16 * i)
                        sp.sem_inc(stored, 1)
                        sp.wait_ge(xn_done, NT * (i + 2))
                        load_x(i + 2)
                    sp.wait_ge(out_done, NT * (i + 1))
                    sp.dma_start(io["out"][i].rearrange("(t p) d -> p t d", p=P), x4[:, i % 4]).then_inc(x_st, 16)

                with sp.Fori(0, B - 2) as i:
                    turn(i)
                turn(B - 2)
                turn(B - 1)
                sp.wait_ge(x_st, 16 * B)

            @block.gpsimd
            def _(pool):
                steps = Steps(pool, fchain)
                steps.link(pool.memset(ident[:, :], 0.0))
                pool.affine_select(out=ident[:, :], in_=ident[:, :], compare_op=ALU.not_equal, fill=1.0, base=0,
                                   pattern=[[-1, P]], channel_multiplier=1)
                steps.link(pool.memset(mhalf[:, :], -0.5))
                pool.memset(xt[:, :, 0:1], 0.0)
                pool.drain().then_inc(const, 1)

                def power(j):
                    pool.wait_ge(ve_done, j + 1)
                    pool.tensor_tensor(rstd[:, :], ve[:, :], mhalf[:, :], ALU.pow).then_inc(rstd_done, 1)

                def mixes(j, a):
                    for c in range(C):
                        pool.wait_ge(mix_hi[a], C * j + c + 1)
                        pool.tensor_tensor(xm[a][1][:, c], mix[:, a, c % 2], f(xm[a][0][:, c]), ALU.subtract)\
                            .then_inc(mix_lo[a], 1)

                power(0)
                mixes(0, 0)
                mixes(0, 1)

                def turn(i):
                    if not last_turn(i):
                        power(i + 1)
                    for m in range(C):
                        pool.wait_ge(free[f"f_k{m % 2}"], 2 * i + m // 2 + 1)
                        if m >= 2:
                            pool.wait_ge(k_lo, C * i + m - 1)
                        pool.tensor_tensor(kk[:, m % 2], ka[:, m % 2], ka[:, m % 2], ALU.mult).then_inc(squared, 1)
                    if not last_turn(i):
                        mixes(i + 1, 0)
                        mixes(i + 1, 1)

                with pool.Fori(0, B - 1) as i:
                    turn(i)
                turn(B - 1)

            @block.scalar
            def _(act):
                raws = (x4[:, 2], x4[:, 3], xn[:, :, :])
                for i in range(3):
                    act.wait_ge(w_in[i], 16)
                    for c in range(C):
                        act.activation(wh[:, i, c], raws[i][:, c], ACT.Copy).then_inc(w_hi, 1)
                act.wait_ge(c_in, 48)
                act.activation(gate[:, :], gate[:, :], ACT.Tanh).then_inc(gated, 1)
                act.wait_ge(const, 1)

                def transposed(i):
                    for c in range(C):
                        act.wait_ge(full[f"f_t{c % 2}"], TP.n(i, "t", c // 2) + 1)
                        act.activation(xt[:, c, 1:T + 1], bank[f"f_t{c % 2}"][:, :], ACT.Copy)\
                           .then_inc(free[f"f_t{c % 2}"], 1)

                def mixes(j, a):
                    for c in range(C):
                        act.wait_ge(mixed[a], C * j + c + 1)
                        act.activation(xm[a][0][:, c], mix[:, a, c % 2], ACT.Copy).then_inc(mix_hi[a], 1)

                transposed(None)
                mixes(0, 0)
                mixes(0, 1)

                def turn(i):
                    def relu(m):
                        act.wait_ge(full[f"f_k{m % 2}"], 2 * i + m // 2 + 1)
                        if m >= 2:
                            act.wait_ge(squared, C * i + m - 1)
                        act.activation(ka[:, m % 2], bank[f"f_k{m % 2}"][:, :], ACT.Relu)\
                           .then_inc(free[f"f_k{m % 2}"], 1)

                    def high(m):
                        act.wait_ge(squared, C * i + m + 1)
                        act.activation(kh[:, m], kk[:, m % 2], ACT.Copy).then_inc(k_hi, 1)

                    relu(0)
                    relu(1)
                    high(0)
                    relu(2)
                    high(1)
                    relu(3)
                    high(2)
                    high(3)
                    if not last_turn(i):
                        transposed(i)
                        mixes(i + 1, 0)
                    for t in range(NT):
                        act.wait_ge(full[f"f_r{t % 2}"], 2 * i + t // 2 + 1)
                        for k in range(2):
                            act.wait_ge(free[f"f_v{k}"], 2 * i)
                        act.activation(th[:, t], bank[f"f_r{t % 2}"][:, :], ACT.Tanh, scale=0.5)\
                           .then_inc(free[f"f_r{t % 2}"], 1)
                    if not last_turn(i):
                        mixes(i + 1, 1)

                with act.Fori(0, B - 1) as i:
                    turn(i)
                turn(B - 1)

            @block.vector
            def _(dve):
                raws = (x4[:, 2], x4[:, 3], xn[:, :, :])
                for i in range(3):
                    for c in range(C):
                        dve.wait_ge(w_hi, C * i + c + 1)
                        dve.tensor_tensor(wl[:, i, c], raws[i][:, c], f(wh[:, i, c]), ALU.subtract).then_inc(w_lo, 1)
                dve.wait_ge(const, 1)
                steps = Steps(dve, dchain)
                dve.wait_ge(gated, 1)
                steps.link(dve.tensor_scalar(gate[:, :], gate[:, :], 0.5, None, ALU.mult))

                def norm(steps, x, j):
                    steps.count(dve.memset(mark[:, :], 0.0))
                    for t in range(NT):
                        ins = dve.bn_stats(stats[:, t, :], x[:, t, :])
                    steps.link(ins)
                    steps.count(dve.memset(mark[:, :], 0.0))
                    for t in range(NT):
                        ins = dve.bn_aggr(mv[:, t, :], stats[:, t, :])
                    steps.link(ins)
                    dve.tensor_scalar(ve[:, :], mv[:, :, 1], EPS, None, ALU.add).then_inc(ve_done, 1)
                    dve.wait_ge(rstd_done, j + 1)
                    for t in range(NT):
                        dve.tensor_scalar(xn[:, t, :], x[:, t, :], mv[:, t, 0:1], rstd[:, t:t + 1],
                                          ALU.subtract, ALU.mult).then_inc(xn_done, 1)

                def mixes(steps, i, j, a):
                    for c in range(C):
                        if a == 0:
                            dve.wait_ge(free[f"f_t{c % 2}"], TP.n(i, "t", c // 2) + 1)
                            steps.link(dve.tensor_tensor(dif[:, c], xt[:, c, 1:T + 1], xt[:, c, 0:T], ALU.subtract))
                        if c >= 2:
                            dve.wait_ge(mix_lo[a], C * j + c - 1)
                        dve.scalar_tensor_tensor(out=mix[:, a, c % 2], in0=dif[:, c], scalar=mu[:, a, c:c + 1],
                                                 in1=xt[:, c, 0:T], op0=ALU.mult, op1=ALU.add).then_inc(mixed[a], 1)

                dve.wait_ge(x_in, 16)
                dve.wait_ge(c_in, 48)
                norm(steps, x4[:, 0], 0)
                mixes(steps, None, 0, 0)
                mixes(steps, None, 0, 1)
                BEFORE = steps.n

                def turn(i):
                    steps = Steps(dve, dchain, BEFORE + TURN * i)
                    if not last_turn(i):
                        dve.wait_ge(x_in, 16 * (i + 2))
                        norm(steps, x4[:, (i + 1) % 4], i + 1)
                    for m in range(C):
                        dve.wait_ge(k_hi, C * i + m + 1)
                        dve.tensor_tensor(kl[:, m], kk[:, m % 2], f(kh[:, m]), ALU.subtract).then_inc(k_lo, 1)
                    if not last_turn(i):
                        mixes(steps, i, i + 1, 0)
                        for k in range(2):
                            dve.wait_ge(full[f"f_r{k}"], 2 * i + 2)
                        mixes(steps, i, i + 1, 1)
                    for t in range(NT):
                        dve.wait_ge(free[f"f_r{t % 2}"], 2 * i + t // 2 + 1)
                        dve.wait_ge(full[f"f_v{t % 2}"], 2 * i + t // 2 + 1)
                        dve.scalar_tensor_tensor(out=tmp[:, t % 2], in0=th[:, t], scalar=1.0,
                                                 in1=bank[f"f_v{t % 2}"][:, :], op0=ALU.add, op1=ALU.mult)\
                           .then_inc(free[f"f_v{t % 2}"], 1)
                        dve.wait_ge(free[f"f_v{t % 2}"], 2 * i + t // 2 + 1)
                        xt_ = x4[:, i % 4, t]
                        dve.scalar_tensor_tensor(out=xt_, in0=tmp[:, t % 2], scalar=gate[:, 0:1], in1=xt_,
                                                 op0=ALU.mult, op1=ALU.add).then_inc(out_done, 1)

                TURN = LN_STEPS + C
                with dve.Fori(0, B - 1) as i:
                    turn(i)
                turn(B - 1)

            @block.tensor
            def _(pe):
                pe.wait_ge(const, 1)
                pe.wait_ge(w_lo, 3 * C)

                def transposes(i):
                    pe.wait_ge(xn_done, NT * (1 if i is None else i + 2))
                    for c in range(C):
                        pe.wait_ge(free[f"f_t{c % 2}"], TP.n(i, "t", c // 2))
                        for t in range(NT):
                            last = pe.transpose(bank[f"f_t{c % 2}"][:, t * P:(t + 1) * P],
                                                xn[:, t, c * P:(c + 1) * P], ident[:, :])
                        last.then_inc(full[f"f_t{c % 2}"], 1)

                transposes(None)

                def turn(i):
                    pe.wait_ge(mix_lo[0], C * (i + 1))
                    for m in range(C):
                        cols = slice(m * P, (m + 1) * P)
                        pe.wait_ge(free[f"f_k{m % 2}"], 2 * i + m // 2)
                        three_passes(pe, bank[f"f_k{m % 2}"][:, :],
                                     lambda c: (wh[:, 0, c, cols], wl[:, 0, c, cols]),
                                     lambda c: (xm[0][0][:, c], xm[0][1][:, c])).then_inc(full[f"f_k{m % 2}"], 1)
                    if not last_turn(i):
                        transposes(i)
                    pe.wait_ge(mix_lo[1], C * (i + 1))
                    for t in range(NT):
                        cols = slice(t * P, (t + 1) * P)
                        pe.wait_ge(free[f"f_r{t % 2}"], 2 * i + t // 2)
                        three_passes(pe, bank[f"f_r{t % 2}"][:, :],
                                     lambda c: (xm[1][0][:, c, cols], xm[1][1][:, c, cols]),
                                     lambda c: (wh[:, 1, c], wl[:, 1, c])).then_inc(full[f"f_r{t % 2}"], 1)
                    pe.wait_ge(k_lo, C * (i + 1))
                    for t in range(NT):
                        cols = slice(t * P, (t + 1) * P)
                        pe.wait_ge(free[f"f_v{t % 2}"], 2 * i + t // 2)
                        three_passes(pe, bank[f"f_v{t % 2}"][:, :],
                                     lambda c: (kh[:, c, cols], kl[:, c, cols]),
                                     lambda c: (wh[:, 2, c], wl[:, 2, c])).then_inc(full[f"f_v{t % 2}"], 1)

                with pe.Fori(0, B - 1) as i:
                    turn(i)
                turn(B - 1)


def build(nc, a, out):
    def dram(name, shape, dt=F32):
        return nc.dram_tensor(name, shape, dt).ap()

    N = B * S2
    kh_d = [dram(f"s_kh{i}", (D, N)) for i in range(2)]
    kl_d = [dram(f"s_kl{i}", (D, N)) for i in range(2)]
    v_d = [dram(f"s_v{i}", (N, D)) for i in range(2)]
    x1_d, x3_d, xn_d = dram("s_x1", (B, T, D)), dram("s_x3", (B, T, D)), dram("s_xn", (B, T, D))
    perm_d = dram("s_perm", (ES, B * T))
    bd_d = dram("s_bd", (P, NTILE, ES, GT))
    rp_d = dram("s_rp", (NG, ES, D))
    keys_and_values(nc, a["ctx_t"], [a["k0"], a["v0"], a["k1"], a["v1"]], [a["bk"], a["bv"]], kh_d, kl_d, v_d)
    attention(nc, 0, dict(x=a["x"], wq=a["q0"], wo=a["o0"], gate=a["g_xattn"][0:1], gate_before=a["g_ffn"][0:1],
                          wc=a["wc"], bc=a["bc"], tie=a["tie"], kh=kh_d[0], kl=kl_d[0], v=v_d[0], x_out=x1_d,
                          xn_out=xn_d, perm=perm_d, bd=bd_d))
    experts(nc, dict(bd=bd_d, xn=xn_d.rearrange("b (t p) d -> (b t) p d", p=P), w1=a["w1"], b1=a["b1"], w2=a["w2"],
                     rp=rp_d))
    attention(nc, 1, dict(x=x1_d, wq=a["q1"], wo=a["o1"], gate=a["g_xattn"][1:2], gate_before=a["g_ffn"][0:1],
                          bq=a["bq"], bo=a["bo"], mask=a["mask"], mask_t=a["mask_t"], kh=kh_d[1], kl=kl_d[1],
                          v=v_d[1], x_out=x3_d, perm=perm_d, rp=rp_d, b2=a["b2"]))
    feed_forward(nc, dict(w=[a["wk"], a["wr"], a["wv"]], mu=[a["mu_k"], a["mu_r"]], gate=a["g_ffn"][1:2], x=x3_d,
                          out=out))


def kernel(**inputs):
    import concourse.bacc as bacc
    from concourse.bass_utils import run_bass_kernel_spmd

    g = {k: np.asarray(v) for k, v in inputs.items()}
    columns = lambda a: a.reshape(C, P).T
    arrays = dict(
        x=g["x"], ctx_t=g["ctx_1024"].reshape(B * S2, D).T, mask=g["mask_BxS2_ik0"], mask_t=g["mask_BxS2_ik0"].T,
        g_xattn=g["g_xattn"], g_ffn=g["g_ffn"],
        q0=g["L0_xattn_W_q"].T, k0=g["L0_xattn_W_k"].T, v0=g["L0_xattn_W_v"].T, o0=g["L0_xattn_W_o"].T,
        wc=g["L0_ffn_Wc"].reshape(D, ES), bc=g["L0_ffn_bc"].reshape(ES),
        w1=g["L0_ffn_W1"].reshape(ES, D, EF).transpose(1, 0, 2).reshape(D, ES * EF),
        b1=g["L0_ffn_b1"].reshape(EK, P).T,
        w2=g["L0_ffn_W2"].reshape(ES, D, EF).transpose(0, 2, 1).reshape(ES * EF, D),
        b2=g["L0_ffn_b2"].reshape(ES, D),
        q1=g["L1_xattn_Wq"].T, k1=g["L1_xattn_Wk"].T, v1=g["L1_xattn_Wv"].T, o1=g["L1_xattn_Wo"].T,
        bq=columns(g["L1_xattn_bq"]), bk=columns(g["L1_xattn_bk"]), bv=g["L1_xattn_bv"], bo=g["L1_xattn_bo"],
        wr=g["L1_ffn_W_r"].T, wk=g["L1_ffn_W_k"].T, wv=g["L1_ffn_W_v"].T,
        mu_r=columns(g["L1_ffn_mu_r"]), mu_k=columns(g["L1_ffn_mu_k"]),
        tie=np.linspace(0.0, 1e-6, G, dtype=np.float32),
    )
    nc = bacc.Bacc("TRN2", target_bir_lowering=False, num_devices=1)
    feed, aps = {}, {}
    for name, value in arrays.items():
        feed["in_" + name] = np.ascontiguousarray(value)
        aps[name] = nc.dram_tensor("in_" + name, value.shape, mybir.dt.from_np(value.dtype), kind="ExternalInput").ap()
    out = nc.dram_tensor("out", (B, T, D), F32, kind="ExternalOutput").ap()
    build(nc, aps, out)
    return run_bass_kernel_spmd(nc, [feed], core_ids=[0]).results[0]["out"]
```

```python
from contextlib import ExitStack

import concourse.bass as bass
import numpy as np
from concourse import mybir

ALU = mybir.AluOpType
ACT = mybir.ActivationFunctionType
AX = mybir.AxisListType
F32 = mybir.dt.float32
F32R = mybir.dt.float32r
I32 = mybir.dt.int32

P = 128
B, T, D = 8, 512, 512
S2 = 120
H, DK = 16, 32
C = D // P
NT = T // P
HJ = P // DK
ES, EF, G = 128, 32, 32
NG = B * T // G
GB = T // G
GT = P // G
NTILE = B * NT
EJ = P // EF
EK = ES // EJ
EPS = 1e-5
SCALE = 1.0 / float(np.sqrt(np.float32(DK)))
BIG = 1e30
RG = 2
RING = 8
STACK = 3 * DK + 1


def f(ap):
    return ap.bitcast(F32)


LN_STEPS = 4


class Steps:

    def __init__(self, eng, sem, base=0):
        self.eng, self.sem, self.base, self.n = eng, sem, base, 0

    def count(self, ins):
        ins.then_inc(self.sem, 1)
        self.n += 1

    def link(self, ins):
        self.count(ins)
        self.eng.wait_ge(self.sem, self.base + self.n)


def tools(nc, ctx):
    def sb(name, shape, dt=F32):
        return ctx.enter_context(nc.sbuf_tensor(name, shape, dt))

    def banks(*names):
        return {n: ctx.enter_context(nc.psum_tensor(n, [P, 512], F32)) for n in names}

    sems = []

    def sem(name):
        sems.append(nc.alloc_semaphore(name=name))
        return sems[-1]

    def clear():
        nc.clear_and_free_semaphores(sems)
        nc.all_engine_barrier()

    ctx.callback(clear)
    return sb, banks, sem


def three_passes(pe, out, lhs, rhs, ready=None):
    for c in range(C):
        if ready is not None:
            ready(c)
        (ah, al), (bh, bl) = lhs(c), rhs(c)
        pe.matmul(out, ah, bh, start=(c == 0), stop=False)
        pe.matmul(out, ah, bl, start=False, stop=False)
        last = pe.matmul(out, al, bh, start=False, stop=(c == C - 1))
    return last


def keys_and_values(nc, ctx_t, weights, biases, kh_d, kl_d, v_d):
    N = B * S2
    HALF = N // 2
    with ExitStack() as ctx:
        sb, banks, sem = tools(nc, ctx)
        raw = sb("kv_raw", [P, 4, C, D])
        wh, wl = sb("kv_wh", [P, 4, C, D], F32R), sb("kv_wl", [P, 4, C, D], F32R)
        craw = sb("kv_craw", [P, C, N])
        ch, cl = sb("kv_ch", [P, C, N], F32R), sb("kv_cl", [P, C, N], F32R)
        bk, bv = sb("kv_bk", [P, C]), sb("kv_bv", [S2, D])
        kh, kl = sb("kv_kh", [P, 2, HALF], F32R), sb("kv_kl", [P, 2, HALF], F32R)
        vo = sb("kv_vo", [S2, 2, D])
        ps = banks("kv_p0", "kv_p1")
        full, free = [sem(f"kv_full{i}") for i in range(2)], [sem(f"kv_free{i}") for i in range(2)]
        ctx_in, bias_in = sem("kv_ctx_in"), sem("kv_bias_in")
        w_in = [sem(f"kv_w_in{i}") for i in range(4)]
        hi_done, lo_done, k_hi = sem("kv_hi_done"), sem("kv_lo_done"), sem("kv_k_hi")
        k_st, v_st = [sem(f"kv_k_st{i}") for i in range(2)], [sem(f"kv_v_st{i}") for i in range(2)]
        bank = [ps["kv_p0"], ps["kv_p1"]]
        units = [(lay, kind, u) for lay in range(2) for kind in "kv" for u in range(8)]

        with nc.Block() as block:
            @block.sync
            def _(sp):
                sp.dma_start(craw[:, :, :], ctx_t.rearrange("(c p) n -> p c n", p=P)).then_inc(ctx_in, 16)
                for i, w in enumerate(weights):
                    sp.dma_start(raw[:, i], w.rearrange("(c p) n -> p c n", p=P)).then_inc(w_in[i], 16)
                sp.dma_start(bk[:, :], biases[0]).then_inc(bias_in, 16)
                sp.dma_start(bv[:, :], biases[1].partition_broadcast(S2)).then_inc(bias_in, 16)
                nk = nv = 0
                for n, (lay, kind, u) in enumerate(units):
                    sp.wait_ge(free[n % 2], n // 2 + 1)
                    if kind == "k":
                        m, half = u // 2, u % 2
                        rows, cols = slice(m * P, (m + 1) * P), slice(half * HALF, (half + 1) * HALF)
                        sp.dma_start(kh_d[lay][rows, cols], f(kh[:, nk % 2, :])).then_inc(k_st[nk % 2], 16)
                        sp.dma_start(kl_d[lay][rows, cols], f(kl[:, nk % 2, :])).then_inc(k_st[nk % 2], 16)
                        nk += 1
                    else:
                        sp.dma_start(v_d[lay][u * S2:(u + 1) * S2, :], vo[:, nv % 2, :]).then_inc(v_st[nv % 2], 16)
                        nv += 1
                for i in range(2):
                    sp.wait_ge(k_st[i], 32 * nk // 2)
                    sp.wait_ge(v_st[i], 16 * nv // 2)

            @block.scalar
            def _(act):
                act.wait_ge(ctx_in, 16)
                for c in range(C):
                    act.activation(ch[:, c], craw[:, c], ACT.Copy).then_inc(hi_done, 1)
                for i in range(4):
                    act.wait_ge(w_in[i], 16)
                    for c in range(C):
                        act.activation(wh[:, i, c], raw[:, i, c], ACT.Copy).then_inc(hi_done, 1)
                act.wait_ge(bias_in, 32)
                nk = 0
                for n, (lay, kind, u) in enumerate(units):
                    if kind == "k":
                        act.wait_ge(full[n % 2], n // 2 + 1)
                        if nk >= 2:
                            act.wait_ge(k_st[nk % 2], 32 * (nk // 2))
                        bias = bk[:, u // 2:u // 2 + 1] if lay else 0.0
                        act.activation(kh[:, nk % 2, :], bank[n % 2][:, 0:HALF], ACT.Identity, bias=bias)\
                           .then_inc(k_hi, 1)
                        nk += 1

            @block.vector
            def _(dve):
                for i in range(5):
                    for c in range(C):
                        dve.wait_ge(hi_done, C * i + c + 1)
                        if i == 0:
                            dve.tensor_tensor(cl[:, c], craw[:, c], f(ch[:, c]), ALU.subtract).then_inc(lo_done, 1)
                        else:
                            dve.tensor_tensor(wl[:, i - 1, c], raw[:, i - 1, c], f(wh[:, i - 1, c]),
                                              ALU.subtract).then_inc(lo_done, 1)
                dve.wait_ge(bias_in, 32)
                nk = nv = 0
                for n, (lay, kind, u) in enumerate(units):
                    src = bank[n % 2]
                    if kind == "k":
                        dve.wait_ge(k_hi, nk + 1)
                        if nk >= 2:
                            dve.wait_ge(k_st[nk % 2], 32 * (nk // 2))
                        bias = bk[:, u // 2:u // 2 + 1] if lay else 0.0
                        dve.scalar_tensor_tensor(out=kl[:, nk % 2, :], in0=src[:, 0:HALF], scalar=bias,
                                                 in1=f(kh[:, nk % 2, :]), op0=ALU.add, op1=ALU.subtract)\
                           .then_inc(free[n % 2], 1)
                        nk += 1
                    else:
                        dve.wait_ge(full[n % 2], n // 2 + 1)
                        if nv >= 2:
                            dve.wait_ge(v_st[nv % 2], 16 * (nv // 2))
                        if lay:
                            dve.tensor_tensor(vo[:, nv % 2, :], src[0:S2, :], bv[:, :], ALU.add)\
                               .then_inc(free[n % 2], 1)
                        else:
                            dve.tensor_copy(vo[:, nv % 2, :], src[0:S2, :])\
                               .then_inc(free[n % 2], 1)
                        nv += 1

            @block.tensor
            def _(pe):
                for n, (lay, kind, u) in enumerate(units):
                    i = 2 * lay + (kind == "v")
                    pe.wait_ge(lo_done, C * (i + 2))
                    pe.wait_ge(free[n % 2], n // 2)
                    if kind == "k":
                        m, half = u // 2, u % 2
                        cols = slice(half * HALF, (half + 1) * HALF)
                        last = three_passes(
                            pe, bank[n % 2][:, 0:HALF],
                            lambda c: (wh[:, i, c, m * P:(m + 1) * P], wl[:, i, c, m * P:(m + 1) * P]),
                            lambda c: (ch[:, c, cols], cl[:, c, cols]))
                    else:
                        cols = slice(u * S2, (u + 1) * S2)
                        last = three_passes(pe, bank[n % 2][0:S2, :],
                                            lambda c: (ch[:, c, cols], cl[:, c, cols]),
                                            lambda c: (wh[:, i, c, :], wl[:, i, c, :]))
                    last.then_inc(full[n % 2], 1)


class Uses:

    def __init__(self, before, turn, last, after=(), first=None):
        self.before, self.turn, self.last, self.after = before, turn, last, after
        self.first = turn if first is None else first

    def n(self, i, kind, k):
        known = i is None or isinstance(i, int)
        names = {None: self.before, 0: self.first, B - 1: self.last, B: self.after}.get(i, self.turn) \
            if known else self.turn
        at = [x for x, name in enumerate(names) if name == kind][k]
        if i is None:
            return at
        at += len(self.before)
        if known and i == 0:
            return at
        if known and i == B:
            return at + len(self.first) + len(self.turn) * (B - 2) + len(self.last)
        return i * len(self.turn) + (at + len(self.first) - len(self.turn))


def attention(nc, lay, io):
    route, merge = lay == 0, lay == 1
    if route:
        TP = Uses(["ln1"] * 2, ["ln2"] * 2 + ["ln1"] * 2 + ["bc"] * 2 + ["bd"] * 2,
                  ["ln2"] * 2 + ["bc"] * 2 + ["bd"] * 2, ["ln2"] * 2 + ["bd"] * 2, ["ln1"] * 2 + ["bc"] * 2)
        PJ = Uses(["q"] * 2, ["pv"] * 2 + ["q"] * 2 + ["o"] * 2, ["pv"] * 2 + ["o"] * 2)
        MT = Uses(["mt"], ["logits", "mt"], ["logits"], ["logits"], ["mt"])
    else:
        TP = Uses(["ln1"] * 2, ["ln1"] * 2 + ["bc"] * 2, ["bc"] * 2)
        PJ = Uses(["merge", "merge", "q", "q"], ["merge", "pv", "merge", "pv", "q", "q", "o", "o"],
                  ["pv", "pv", "o", "o"])
        MT = Uses(["mt"], ["mt"], [])
    SC = Uses(["max"] * 8, ["score"] * 8 + ["max"] * 8, ["score"] * 8)
    SM = Uses([], ["sum"], ["sum"])
    MAXES = (range(0, 6), range(6, 11), range(11, C * NT), range(0))
    BDS = ((0,), (1,), (), (2, 3))

    with ExitStack() as ctx:
        sb, banks, sem = tools(nc, ctx)
        n_ = lambda s: f"a{lay}_{s}"
        wqh, wql = sb(n_("wqh"), [P, C, D], F32R), sb(n_("wql"), [P, C, D], F32R)
        woh, wol = sb(n_("woh"), [P, C, D], F32R), sb(n_("wol"), [P, C, D], F32R)
        ident, mhalf = sb(n_("ident"), [P, P]), sb(n_("mhalf"), [P, NT])
        gate = sb(n_("gate"), [P, 2])
        x2 = sb(n_("x2"), [P, 2, NT, D])
        xn = sb(n_("xn"), [P, NT, D])
        stats, mv = sb(n_("stats"), [P, NT, 6]), sb(n_("mv"), [P, NT, 2])
        mark = sb(n_("mark"), [P, NT + 1])
        ve, rstd = sb(n_("ve"), [P, 2, NT]), sb(n_("rstd"), [P, 2, NT])
        xth, xtl = sb(n_("xth"), [P, C, T], F32R), sb(n_("xtl"), [P, C, T], F32R)
        qh, ql = sb(n_("qh"), [P, C, T], F32R), sb(n_("ql"), [P, C, T], F32R)
        qs = sb(n_("qs"), [STACK, H, T], F32R)
        ks = sb(n_("ks"), [STACK, H, S2], F32R)
        kbd = sb(n_("kbd"), [P, C, HJ * S2], F32R)
        v = sb(n_("v"), [S2, D])
        pick = sb(n_("pick"), [S2, HJ, DK])
        bc = sb(n_("bc"), [P, C, P], F32R)
        part = sb(n_("part"), [P, 1])
        pr = sb(n_("pr"), [S2, RING, T])
        mx, mt = sb(n_("mx"), [P, NT, H]), sb(n_("mt"), [H, T], F32R)
        rs, rx = sb(n_("rs"), [P, T]), sb(n_("rx"), [P, T], F32R)
        pvs, ao = sb(n_("pvs"), [P, C, T]), sb(n_("ao"), [P, 2, T])
        ath, atl = sb(n_("ath"), [P, C, T], F32R), sb(n_("atl"), [P, C, T], F32R)
        if route:
            wch, wcl = sb(n_("wch"), [P, C, ES], F32R), sb(n_("wcl"), [P, C, ES], F32R)
            bcol, tie = sb(n_("bcol"), [P, 1]), sb(n_("tie"), [P, G])
            lg, gmax = sb(n_("lg"), [P, T]), sb(n_("gmax"), [P, GB])
            perm = sb(n_("perm"), [P, T])
            gmask = sb(n_("gmask"), [P, GT])
            bd = sb(n_("bd"), [P, 2, ES, GT], F32R)
        else:
            bq = sb(n_("bq"), [P, C])
            mcol_i = sb(n_("mcol_i"), [S2, B], I32)
            mall_i = pvs[0:S2].rearrange("p c t -> p (c t)")[:, 0:B * S2].bitcast(I32)
            mall_f = pr[:, :, :].rearrange("p h t -> p (h t)")[:, 0:B * S2]
            rows_, ones = sb(n_("rows"), [DK + 1, 2 * D], F32R), sb(n_("ones"), [DK + 1, P], F32R)
            mrow = rows_[0:1, 0:B * S2].rearrange("p (b s) -> p b s", b=B)
            bo = rows_[DK:DK + 1, :].rearrange("p (a n) -> p a n", a=2)
            bo_raw = xn[DK:DK + 1, 0, :]
            mall = sb(n_("mall"), [S2, B])
            kscale, kbias, kcur = sb(n_("kscale"), [S2, B]), sb(n_("kbias"), [S2, B]), sb(n_("kcur"), [S2, 2])
            rp = sb(n_("rp"), [ES, 2, RG, D])
            permb = sb(n_("permb"), [ES, T])
            b2 = sb(n_("b2"), [ES, D])

        ps = banks(*(n_(b) for b in ("sc0", "sc1", "tp0", "tp1", "pj0", "pj1", "sm", "x")))
        bank = {k: ps[n_(k)] for k in ("sc0", "sc1", "tp0", "tp1", "pj0", "pj1", "sm", "x")}
        full = {k: sem(n_("full_" + k)) for k in bank}
        free = {k: sem(n_("free_" + k)) for k in bank}
        x_in, x_st = ([sem(n_(f"{k}{t}")) for t in range(NT if merge else 1)] for k in ("x_in", "x_st"))
        k_in, kbd_in, v_in = sem(n_("k_in")), sem(n_("kbd_in")), sem(n_("v_in"))
        w_in = [sem(n_(f"w_in{i}")) for i in range(3)]
        c_in = sem(n_("c_in"))
        w_hi, w_lo, const = sem(n_("w_hi")), sem(n_("w_lo")), sem(n_("const"))
        ve_done, rstd_done = sem(n_("ve_done")), sem(n_("rstd_done"))
        xn1, xn2 = sem(n_("xn1")), sem(n_("xn2"))
        xt_hi, q_hi, a_hi, a_lo = sem(n_("xt_hi")), sem(n_("q_hi")), sem(n_("a_hi")), sem(n_("a_lo"))
        q_stacked, m_stacked = sem(n_("q_stacked")), sem(n_("m_stacked"))
        exps, dchain, fchain = sem(n_("exps")), sem(n_("dchain")), sem(n_("fchain"))
        if route:
            xn_st, perm_st = sem(n_("xn_st")), sem(n_("perm_st"))
            bd_st = [sem(n_(f"bd_st{i}")) for i in range(2)]
            permed, step = sem(n_("permed")), sem(n_("step"))
        else:
            kcur_done = sem(n_("kcur_done"))
            rp_in, permb_in = [sem(n_(f"rp_in{i}")) for i in range(2)], sem(n_("permb_in"))

        last_turn = lambda i: isinstance(i, int) and i == B - 1
        first_turn = lambda i: isinstance(i, int) and i == 0

        def norms_before(i, which):
            if which == 1:
                return 0 if i is None else 2 * i + 1 if route else i + 1
            return 2 * B - 1 if isinstance(i, int) and i == B else 2 * i

        def turns(eng, turn, last=1):
            if route:
                turn(0)
            with eng.Fori(1 if route else 0, B - last) as i:
                turn(i)
            for i in range(B - last, B):
                turn(i)

        def xt_base(i, which):
            return 0 if i is None else C * norms_before(i, which)

        with nc.Block() as block:
            @block.sync
            def _(sp):
                rows = lambda w: w.rearrange("(c p) n -> p c n", p=P)
                sp.dma_start(x2[:, 0], rows(io["wq"])).then_inc(w_in[0], 16)
                sp.dma_start(x2[:, 1], rows(io["wo"])).then_inc(w_in[1], 16)
                n_const = 2
                sp.dma_start(gate[:, 0:1], io["gate"].partition_broadcast(P)).then_inc(c_in, 16)
                sp.dma_start(gate[:, 1:2], io["gate_before"].partition_broadcast(P)).then_inc(c_in, 16)
                if route:
                    sp.dma_start(xn[:, 0, :].rearrange("p (c n) -> p c n", c=C), rows(io["wc"])).then_inc(w_in[2], 16)
                    sp.dma_start(bcol[:, :], io["bc"].rearrange("(p a) -> p a", a=1)).then_inc(c_in, 16)
                    sp.dma_start(tie[:, :], io["tie"].partition_broadcast(P)).then_inc(c_in, 16)
                    n_const += 2
                else:
                    sp.dma_start(bq[:, :], io["bq"]).then_inc(c_in, 16)
                    sp.dma_start(bo_raw, io["bo"].rearrange("(a n) -> a n", a=1)).then_inc(c_in, 16)
                    sp.dma_start(mcol_i[:, :], io["mask_t"]).then_inc(c_in, 16)
                    sp.dma_start(mall_i, io["mask"].rearrange("b s -> (b s)").partition_broadcast(S2))\
                      .then_inc(c_in, 16)
                    sp.dma_start(b2[:, :], io["b2"]).then_inc(c_in, 16)
                    n_const += 5

                def load_x(j):
                    for t, x_in_ in enumerate(x_in):
                        ts = slice(t, t + 1) if merge else slice(0, NT)
                        sp.dma_start(x2[:, j % 2, ts], io["x"][j].rearrange("(t p) d -> p t d", p=P)[:, ts])\
                          .then_inc(x_in_, 16)

                def load_keys(j):
                    cols = bass.ds(j * S2, S2)
                    for r, k in enumerate((io["kh"], io["kl"], io["kh"])):
                        sp.dma_start(f(ks[r * DK:(r + 1) * DK]), k.rearrange("(h p) s -> p h s", p=DK)[:, :, cols])\
                          .then_inc(k_in, 16)

                def load_max_keys(j):
                    cols = bass.ds(j * S2, S2)
                    src = io["kh"].rearrange("(c j p) s -> j p c s", p=DK, j=HJ)
                    for a in range(HJ):
                        sp.dma_start(f(kbd[a * DK:(a + 1) * DK, :, a * S2:(a + 1) * S2]), src[a][:, :, cols])\
                          .then_inc(kbd_in, 16)

                def load_v(j):
                    sp.dma_start(v[:, :], io["v"][bass.ds(j * S2, S2), :]).then_inc(v_in, 16)

                def load_experts(j, t):
                    for a in range(2):
                        sp.dma_start(rp[:, a], io["rp"][bass.ds(j * GB + t * GT + a * RG, RG)].rearrange(
                            "n e d -> e n d")).then_inc(rp_in[a], 16)

                def load_perm(j):
                    sp.dma_start(permb[:, :], io["perm"][:, bass.ds(j * T, T)]).then_inc(permb_in, 16)

                def stack_queries(i, j):
                    for k in range(2):
                        sp.wait_ge(free[f"pj{k}"], PJ.n(i, "q", 1) + 1)
                    for r, q in enumerate((qh, qh, ql)):
                        for a in range(HJ):
                            sp.dma_start(f(qs[r * DK:(r + 1) * DK]).rearrange("p (c a) t -> p c a t", a=HJ)[:, :, a],
                                         f(q[a * DK:(a + 1) * DK])).then_inc(q_stacked, 16)

                def stack_max(i):
                    sp.wait_ge(free["x"], MT.n(i, "mt", 0) + 1)
                    sp.dma_start(f(qs[3 * DK:STACK]).rearrange('a h t -> a (h t)'), f(mt[:, :])).then_inc(m_stacked, 16)

                load_keys(0)
                load_v(0)
                if merge:
                    load_perm(0)
                    load_experts(0, 0)
                sp.wait_ge(const, 1)
                load_max_keys(0)
                sp.wait_ge(w_lo, C)
                load_x(0)
                if merge:
                    for t in range(1, NT):
                        sp.wait_ge(full[f"pj{(t - 1) % 2}"], PJ.n(None, "merge", (t - 1) // 2) + 1)
                        load_experts(0, t)
                sp.wait_ge(w_lo, 2 * C + (1 if route else 1))
                if merge:
                    load_x(1)
                    sp.wait_ge(full["pj1"], PJ.n(None, "merge", 1) + 1)
                    load_perm(1)
                    load_experts(1, 0)
                stack_queries(None, 0)
                stack_max(None)

                def store_normed(i):
                    sp.wait_ge(xn2, NT * i)
                    sp.dma_start(io["xn_out"][i - 1].rearrange("(t p) d -> p t d", p=P), xn[:, :, :])\
                      .then_inc(xn_st, 16)

                def store_perm(i):
                    sp.wait_ge(permed, i)
                    sp.dma_start(io["perm"][:, bass.ds((i - 1) * T, T)], perm[:, :]).then_inc(perm_st, 16)

                def store_bd(i, ts):
                    for t in ts:
                        sp.wait_ge(free[f"tp{t % 2}"], TP.n(i, "bd", t // 2) + 1)
                        sp.dma_start(io["bd"][:, (i - 1) * NT + t], f(bd[:, t % 2])).then_inc(bd_st[t % 2], 16)

                def turn(i):
                    last, tail = last_turn(i), route and not first_turn(i)
                    if route and not last:
                        if tail:
                            sp.wait_ge(xn2, NT * i)
                            sp.sem_inc(step, 1)
                            sp.wait_ge(x_st[0], 16 * i)
                        load_x(i + 1)
                    if tail:
                        store_normed(i)
                    if not last:
                        load_max_keys(i + 1)
                        if merge:
                            for t in range(1, NT):
                                sp.wait_ge(full[f"pj{(t - 1) % 2}"], PJ.n(i, "merge", (t - 1) // 2) + 1)
                                load_experts(i + 1, t)
                    if tail:
                        store_perm(i)
                    if not last:
                        for k in range(2):
                            sp.wait_ge(full[f"sc{k}"], SC.n(i, "score", 7) + 1)
                        load_keys(i + 1)
                        if merge and not (isinstance(i, int) and i == B - 2):
                            sp.wait_ge(full["pj1"], PJ.n(i, "merge", 1) + 1)
                            load_perm(i + 2)
                            load_experts(i + 2, 0)
                        for k in range(2):
                            sp.wait_ge(full[f"pj{k}"], PJ.n(i, "pv", 1) + 1)
                        load_v(i + 1)
                        stack_queries(i, i + 1)
                    if tail:
                        store_bd(i, (0, 1))
                    if route:
                        if not last:
                            stack_max(i)
                        if tail:
                            store_bd(i, (2, 3))
                        for k in range(2):
                            sp.wait_ge(free[f"pj{k}"], PJ.n(i, "o", 1) + 1)
                        sp.dma_start(io["x_out"][i].rearrange("(t p) d -> p t d", p=P), x2[:, i % 2])\
                          .then_inc(x_st[0], 16)
                    else:
                        for t in range(NT):
                            if t == NT - 1 and not last:
                                stack_max(i)
                            sp.wait_ge(free[f"pj{t % 2}"], PJ.n(i, "o", t // 2) + 1)
                            sp.dma_start(io["x_out"][i].rearrange("(t p) d -> p t d", p=P)[:, t], x2[:, i % 2, t])\
                              .then_inc(x_st[t], 16)
                        if not last and not (isinstance(i, int) and i == B - 2):
                            for t in range(NT):
                                sp.wait_ge(x_st[t], 16 * (i + 1))
                                sp.dma_start(x2[:, i % 2, t], io["x"][i + 2].rearrange("(t p) d -> p t d", p=P)[:, t])\
                                  .then_inc(x_in[t], 16)

                turns(sp, turn, 2 if merge else 1)
                if route:
                    store_normed(B)
                    store_perm(B)
                    store_bd(B, range(NT))
                for stored in x_st:
                    sp.wait_ge(stored, 16 * B)
                if route:
                    sp.wait_ge(xn_st, 16 * B)
                    sp.wait_ge(perm_st, 16 * B)
                    for k in range(2):
                        sp.wait_ge(bd_st[k], 16 * B * NT // 2)

            @block.gpsimd
            def _(pool):
                steps = Steps(pool, fchain)
                steps.link(pool.memset(ident[:, :], 0.0))
                steps.link(pool.affine_select(out=ident[:, :], in_=ident[:, :], compare_op=ALU.not_equal, fill=1.0,
                                              base=0, pattern=[[-1, P]], channel_multiplier=1))
                steps.link(pool.memset(f(kbd[:, :, :]), 0.0))
                steps.link(pool.memset(f(ks[3 * DK:STACK]), 1.0))
                steps.link(pool.memset(mhalf[:, :], -0.5))
                steps.link(pool.memset(pick[:, :, :], 0.0))
                for g in range(HJ):
                    steps.link(pool.memset(pick[:, g].rearrange("p (a b) -> p a b", b=HJ)[:, :, g:g + 1], 1.0))
                steps.link(pool.memset(part[:, :], -1.0))
                for j in range(HJ):
                    steps.link(pool.memset(part[j * DK:j * DK + C], 0.0))
                spread = ao[:, 0, :].rearrange("p (g c) -> p g c", g=C)
                steps.link(pool.memset(spread, 0.0))
                for g in range(C):
                    view = spread[:, g].rearrange("p (j i) -> p j i", i=DK)
                    for row in (g, C + g):
                        steps.link(pool.affine_select(out=view, in_=view, compare_op=ALU.not_equal, fill=1.0,
                                                      base=-row, pattern=[[-DK, HJ], [0, DK]],
                                                      channel_multiplier=1))
                steps.link(pool.tensor_copy(bc[:, :, :], spread))
                if route:
                    steps.link(pool.memset(gmask[:, :], 0.0))
                    for a in range(GT):
                        steps.link(pool.memset(gmask[a * G:(a + 1) * G, a:a + 1], 1.0))
                else:
                    pool.memset(f(ones[:, :]), 1.0)
                pool.drain().then_inc(const, 1)

                def power(done, which, count):
                    pool.wait_ge(ve_done, count + 1)
                    pool.tensor_tensor(rstd[:, which, :], ve[:, which, :], mhalf[:, :], ALU.pow).then_inc(rstd_done, 1)

                power(rstd_done, 0, 0)
                if merge:
                    pool.wait_ge(w_lo, 2 * C + 1)

                def turn(i):
                    last = last_turn(i)
                    if merge:
                        pool.tensor_copy(kcur[:, 0:1], kscale[:, bass.ds(i, 1)]).then_inc(kcur_done, 1)
                        pool.tensor_copy(kcur[:, 1:2], kbias[:, bass.ds(i, 1)]).then_inc(kcur_done, 1)
                    if route and not first_turn(i):
                        power(rstd_done, 1, norms_before(i, 2))
                    if not last:
                        power(rstd_done, 0, norms_before(i, 1))
                    for g in range(C):
                        pool.wait_ge(a_hi, C * i + g + 1)
                        pool.tensor_tensor(atl[:, g], ao[:, g % 2], f(ath[:, g]), ALU.subtract).then_inc(a_lo, 1)

                turns(pool, turn)
                if route:
                    power(rstd_done, 1, norms_before(B, 2))

            @block.scalar
            def _(act):
                for i, (hi, raw) in enumerate(((wqh, x2[:, 0]), (woh, x2[:, 1]))):
                    act.wait_ge(w_in[i], 16)
                    for c in range(C):
                        act.activation(hi[:, c], raw[:, c], ACT.Copy).then_inc(w_hi, 1)
                if route:
                    act.wait_ge(w_in[2], 16)
                    act.activation(wch[:, :, :], xn[:, 0, :].rearrange("p (c n) -> p c n", c=C), ACT.Copy)\
                       .then_inc(w_hi, 1)
                act.wait_ge(c_in, 16 * (4 if route else 7))
                if merge:
                    act.activation(bo[:, 0, :], bo_raw, ACT.Copy).then_inc(w_hi, 1)
                act.activation(gate[:, :], gate[:, :], ACT.Tanh).then_inc(w_hi, 1)

                def transposed(i, which):
                    for c in range(C):
                        kind = "ln1" if which == 1 else "ln2"
                        act.wait_ge(full[f"tp{c % 2}"], TP.n(i, kind, c // 2) + 1)
                        act.activation(xth[:, c], bank[f"tp{c % 2}"][:, :], ACT.Copy).then_inc(xt_hi, 1)

                def queries(i, j, ms):
                    for m in ms:
                        act.wait_ge(full[f"pj{m % 2}"], PJ.n(i, "q", m // 2) + 1)
                        act.activation(qh[:, m], bank[f"pj{m % 2}"][:, :], ACT.Identity,
                                       bias=bq[:, m:m + 1] if merge else 0.0).then_inc(q_hi, 1)

                def negated_max(i):
                    act.wait_ge(full["x"], MT.n(i, "mt", 0) + 1)
                    act.activation(mt[:, :], bank["x"][0:H, :], ACT.Copy, scale=-1.0).then_inc(free["x"], 1)

                act.wait_ge(w_lo, 2 * C + 1)
                transposed(None, 1)
                queries(None, 0, range(C))
                negated_max(None)

                def turn(i):
                    last = last_turn(i)

                    def exp(h):
                        act.wait_ge(full[f"sc{h % 2}"], SC.n(i, "score", h // 2) + 1)
                        if h >= RING:
                            g = (h - RING) // HJ
                            act.wait_ge(full[f"pj{g % 2}"], PJ.n(i, "pv", g // 2) + 1)
                        src = bank[f"sc{h % 2}"][0:S2, :]
                        if merge:
                            act.activation(pr[:, h % RING, :], src, ACT.Exp, scale=kcur[:, 0:1], bias=kcur[:, 1:2]).then_inc(free[f"sc{h % 2}"], 1)
                        else:
                            act.activation(pr[:, h % RING, :], src, ACT.Exp, scale=SCALE)\
                               .then_inc(free[f"sc{h % 2}"], 1)

                    def values(g):
                        act.wait_ge(full[f"pj{g % 2}"], PJ.n(i, "pv", g // 2) + 1)
                        act.activation(pvs[:, g], bank[f"pj{g % 2}"][:, :], ACT.Copy).then_inc(free[f"pj{g % 2}"], 1)

                    if merge:
                        act.wait_ge(kcur_done, 2 * (i + 1))
                    for h in range(6):
                        exp(h)
                    values(0)
                    for h in range(6, 10):
                        exp(h)
                    if route and not first_turn(i):
                        transposed(i, 2)
                    values(1)
                    for h in range(10, 14):
                        exp(h)
                    values(2)
                    for h in range(14, 16):
                        exp(h)
                    values(3)
                    if not last:
                        transposed(i, 1)
                    for g in range(C):
                        if not last and g % 2 == 0:
                            queries(i, i + 1, (g // 2,))
                        act.wait_ge(free[f"tp{g % 2}"], TP.n(i, "bc", g // 2) + 1)
                        act.activation(ath[:, g], ao[:, g % 2], ACT.Copy).then_inc(a_hi, 1)
                    if not last:
                        queries(i, i + 1, range(2, C))
                        negated_max(i)

                turns(act, turn)
                if route:
                    transposed(B, 2)

            @block.vector
            def _(dve):
                steps = Steps(dve, dchain)
                for i, (hi, lo, raw) in enumerate(((wqh, wql, x2[:, 0]), (woh, wol, x2[:, 1]))):
                    for c in range(C):
                        dve.wait_ge(w_hi, C * i + c + 1)
                        dve.tensor_tensor(lo[:, c], raw[:, c], f(hi[:, c]), ALU.subtract).then_inc(w_lo, 1)
                dve.wait_ge(w_hi, 2 * C + 2)
                if route:
                    dve.tensor_tensor(wcl[:, :, :], xn[:, 0, :].rearrange("p (c n) -> p c n", c=C), f(wch[:, :, :]),
                                      ALU.subtract).then_inc(w_lo, 1)
                else:
                    dve.tensor_scalar(mrow, mall_i[0:1].rearrange("a (b s) -> a b s", b=B), 0.0, -BIG,
                                      ALU.is_equal, ALU.mult)
                    steps.link(dve.tensor_scalar(mall_f, mall_i, 0.0, None, ALU.is_equal))
                    steps.link(dve.tensor_reduce(mall[:, :], mall_f.rearrange("p (b s) -> p b s", b=B), AX.X,
                                                 ALU.min))
                    steps.link(dve.tensor_scalar(mall[:, :], mall[:, :], BIG, -BIG, ALU.mult, ALU.add))
                    steps.link(dve.tensor_scalar(kbias[:, :], mcol_i[:, :], 0.0, None, ALU.is_equal))
                    steps.link(dve.tensor_scalar(kscale[:, :], kbias[:, :], -SCALE, SCALE, ALU.mult, ALU.add))
                    steps.link(dve.tensor_tensor(kbias[:, :], kbias[:, :], mall[:, :], ALU.mult))
                    dve.tensor_tensor(bo[:, 1, :], bo_raw, f(bo[:, 0, :]), ALU.subtract).then_inc(w_lo, 1)
                dve.wait_ge(const, 1)
                LN1, LN2, LOG = LN_STEPS + (NT - 1 if merge else 0), (LN_STEPS if route else 0), (1 if route else 0)
                FIRST = LN1 + 2
                TURN = FIRST + LN2 + LOG

                def statistics(steps, x, t):
                    steps.count(dve.memset(mark[:, t:t + 1], 0.0))
                    return dve.bn_stats(stats[:, t, :], x[:, t, :])

                def norm(steps, x, which, count, done, stored=None, ins=None):
                    if ins is None:
                        ins = statistics(steps, x, 0)
                        for t in range(1, NT):
                            ins = dve.bn_stats(stats[:, t, :], x[:, t, :])
                    steps.link(ins)
                    steps.count(dve.memset(mark[:, NT:NT + 1], 0.0))
                    for t in range(NT):
                        ins = dve.bn_aggr(mv[:, t, :], stats[:, t, :])
                    steps.link(ins)
                    dve.tensor_scalar(ve[:, which, :], mv[:, :, 1], EPS, None, ALU.add).then_inc(ve_done, 1)
                    if stored is not None:
                        dve.wait_ge(xn_st, stored)
                    dve.wait_ge(rstd_done, count + 1)
                    for t in range(NT):
                        dve.tensor_scalar(xn[:, t, :], x[:, t, :], mv[:, t, 0:1], rstd[:, which, t:t + 1],
                                          ALU.subtract, ALU.mult).then_inc(done, 1)

                def merged(steps, i, j, t):
                    dve.wait_ge(x_in[t], 16 * (j + 1))
                    dve.wait_ge(full[f"pj{t % 2}"], PJ.n(i, "merge", t // 2) + 1)
                    xt = x2[:, j % 2, t]
                    dve.scalar_tensor_tensor(out=xt, in0=bank[f"pj{t % 2}"][:, :], scalar=gate[:, 1:2], in1=xt,
                                             op0=ALU.mult, op1=ALU.add).then_inc(free[f"pj{t % 2}"], 1)
                    dve.wait_ge(free[f"pj{t % 2}"], PJ.n(i, "merge", t // 2) + 1)
                    return statistics(steps, x2[:, j % 2], t)

                def transposed(i, which):
                    kind = "ln1" if which == 1 else "ln2"
                    for c in range(C):
                        dve.wait_ge(xt_hi, xt_base(i, which) + c + 1)
                        dve.tensor_tensor(xtl[:, c], bank[f"tp{c % 2}"][:, :], f(xth[:, c]), ALU.subtract)\
                           .then_inc(free[f"tp{c % 2}"], 1)

                def queries(i, j, ms):
                    for m in ms:
                        dve.wait_ge(q_hi, C * j + m + 1)
                        src, dst = bank[f"pj{m % 2}"][:, :], ql[:, m]
                        if merge:
                            ins = dve.scalar_tensor_tensor(out=dst, in0=src, scalar=bq[:, m:m + 1], in1=f(qh[:, m]),
                                                           op0=ALU.add, op1=ALU.subtract)
                        else:
                            ins = dve.tensor_tensor(dst, src, f(qh[:, m]), ALU.subtract)
                        ins.then_inc(free[f"pj{m % 2}"], 1)

                def maxima(i, k):
                    m, t = k // NT, k % NT
                    dve.wait_ge(full[f"sc{k % 2}"], SC.n(i, "max", k // 2) + 1)
                    dve.tensor_reduce(mx[:, t, m * HJ:(m + 1) * HJ],
                                      bank[f"sc{k % 2}"][:, 0:HJ * S2].rearrange("p (a s) -> p a s", a=HJ), AX.X,
                                      ALU.max).then_inc(free[f"sc{k % 2}"], 1)

                if route:
                    dve.wait_ge(x_in[0], 16)
                ins = [merged(steps, None, 0, t) for t in range(NT)][-1] if merge else None
                norm(steps, x2[:, 0], 0, 0, xn1, ins=ins)
                transposed(None, 1)
                queries(None, 0, range(C))
                for k in range(4 * NT):
                    maxima(None, k)
                BEFORE = steps.n

                def normed_tail(steps, i):
                    for k in range(2):
                        dve.wait_ge(free[f"pj{k}"], PJ.n(i - 1, "o", 1) + 1)
                    norm(steps, x2[:, (i - 1) % 2], 1, norms_before(i, 2), xn2)
                    transposed(i, 2)

                def choose(steps, i):
                    dve.wait_ge(full["x"], MT.n(i, "logits", 0) + 1)
                    grouped = lambda a: a.rearrange("p (n t) -> p n t", t=G)
                    dve.scalar_tensor_tensor(out=grouped(lg[:, :]), in0=grouped(bank["x"][:, :]),
                                             scalar=bcol[:, 0:1],
                                             in1=tie[:, :].unsqueeze(1).broadcast_to([P, GB, G]),
                                             op0=ALU.add, op1=ALU.add).then_inc(free["x"], 1)
                    dve.wait_ge(free["x"], MT.n(i, "logits", 0) + 1)
                    steps.link(dve.tensor_reduce(gmax[:, :], grouped(lg[:, :]), AX.X, ALU.max))
                    if not (isinstance(i, int) and i == 1):
                        dve.wait_ge(perm_st, 16 * (i - 1))
                    dve.tensor_tensor(grouped(perm[:, :]), grouped(lg[:, :]),
                                      gmax[:, :].unsqueeze(2).broadcast_to([P, GB, G]), ALU.is_equal)\
                       .then_inc(permed, 1)

                def choices(i, ts):
                    for t in ts:
                        dve.wait_ge(full[f"tp{t % 2}"], TP.n(i, "bd", t // 2) + 1)
                        count = NT // 2 * (i - 1) + t // 2
                        if not (isinstance(count, int) and count == 0):
                            dve.wait_ge(bd_st[t % 2], 16 * count)
                        dve.tensor_tensor(bd[:, t % 2],
                                          bank[f"tp{t % 2}"][:, 0:ES].unsqueeze(2).broadcast_to([P, ES, GT]),
                                          gmask[:, :].unsqueeze(1).broadcast_to([P, ES, GT]), ALU.mult)\
                           .then_inc(free[f"tp{t % 2}"], 1)

                def turn(i):
                    last, tail = last_turn(i), route and not first_turn(i)
                    steps = Steps(dve, dchain, BEFORE if first_turn(i) else TURN * i + (BEFORE + FIRST - TURN))
                    if tail:
                        normed_tail(steps, i)
                    if not last:
                        j = i + 1
                        if route:
                            dve.wait_ge(x_in[0], 16 * (j + 1))
                        ins = [merged(steps, i, j, t) for t in range(NT)][-1] if merge else None
                        norm(steps, x2[:, j % 2], 0, norms_before(i, 1), xn1, 16 * i if tail else None, ins)
                    if tail:
                        choose(steps, i)
                    if not last:
                        transposed(i, 1)
                    dve.wait_ge(full["sm"], SM.n(i, "sum", 0) + 1)
                    steps.link(dve.reciprocal(rs[:, :], bank["sm"][:, :]))
                    steps.link(dve.tensor_copy(rx[:, :], rs[:, :]))
                    dve.scalar_tensor_tensor(out=rx[:, :], in0=f(rx[:, :]), scalar=part[:, 0:1], in1=rs[:, :],
                                             op0=ALU.mult, op1=ALU.add).then_inc(free["sm"], 1)
                    for g in range(C):
                        if not last and g % 2 == 0:
                            queries(i, j, (g // 2,))
                        dve.wait_ge(full[f"tp{g % 2}"], TP.n(i, "bc", g // 2) + 1)
                        dve.wait_ge(free[f"pj{g % 2}"], PJ.n(i, "pv", g // 2) + 1)
                        if g >= 2:
                            dve.wait_ge(a_lo, C * i + g - 1)
                        dve.tensor_tensor(ao[:, g % 2], bank[f"tp{g % 2}"][:, :], pvs[:, g], ALU.mult)\
                           .then_inc(free[f"tp{g % 2}"], 1)
                    if not last:
                        queries(i, j, range(2, C))
                    for t in range(NT):
                        if tail:
                            choices(i, BDS[t])
                        if not last:
                            for k in MAXES[t]:
                                maxima(i, k)
                        dve.wait_ge(full[f"pj{t % 2}"], PJ.n(i, "o", t // 2) + 1)
                        xt = x2[:, i % 2, t]
                        dve.scalar_tensor_tensor(out=xt, in0=bank[f"pj{t % 2}"][:, :], scalar=gate[:, 0:1], in1=xt,
                                                 op0=ALU.mult, op1=ALU.add).then_inc(free[f"pj{t % 2}"], 1)

                turns(dve, turn)
                if route:
                    steps = Steps(dve, dchain, BEFORE + FIRST + TURN * (B - 1) - LN1)
                    normed_tail(steps, B)
                    choose(steps, B)
                    choices(B, range(NT))

            @block.tensor
            def _(pe):
                pe.wait_ge(const, 1)
                pe.wait_ge(w_lo, 2 * C + 1)

                def transposes(i, which):
                    kind = "ln1" if which == 1 else "ln2"
                    if which == 1:
                        pe.wait_ge(xn1, NT * (1 if i is None else i + 2))
                    else:
                        pe.wait_ge(xn2, NT * i)
                    for c in range(C):
                        u = TP.n(i, kind, c // 2)
                        pe.wait_ge(free[f"tp{c % 2}"], u)
                        for t in range(NT):
                            last = pe.transpose(bank[f"tp{c % 2}"][:, t * P:(t + 1) * P], xn[:, t, c * P:(c + 1) * P],
                                                ident[:, :])
                        last.then_inc(full[f"tp{c % 2}"], 1)

                def transposed(i, kind):
                    return lambda c: pe.wait_ge(free[f"tp{c % 2}"], TP.n(i, kind, c // 2) + 1)

                def queries(i, ms):
                    for m in ms:
                        pe.wait_ge(free[f"pj{m % 2}"], PJ.n(i, "q", m // 2))
                        cols = slice(m * P, (m + 1) * P)
                        three_passes(pe, bank[f"pj{m % 2}"][:, :],
                                     lambda c: (wqh[:, c, cols], wql[:, c, cols]),
                                     lambda c: (xth[:, c, :], xtl[:, c, :]),
                                     transposed(i, "ln1") if m == 0 else None).then_inc(full[f"pj{m % 2}"], 1)

                def max_tile(i, j, k):
                    m, t = k // NT, k % NT
                    pe.wait_ge(free[f"sc{k % 2}"], SC.n(i, "max", k // 2))
                    if t == 0:
                        pe.wait_ge(q_hi, C * j + m + 1)
                    out = bank[f"sc{k % 2}"][:, 0:HJ * S2]
                    last = pe.matmul(out, qh[:, m, t * P:(t + 1) * P], kbd[:, m, :], start=True, stop=not merge)
                    if merge:
                        last = pe.matmul(out.rearrange("p (a s) -> p a s", a=HJ), ones[0:1, :],
                                         mrow[:, bass.ds(j, 1), :].broadcast_to([1, HJ, S2]), start=False, stop=True)
                    last.then_inc(full[f"sc{k % 2}"], 1)

                def max_rows(i):
                    for k in range(2):
                        pe.wait_ge(free[f"sc{k}"], SC.n(i, "max", 7) + 1)
                    pe.wait_ge(free["x"], MT.n(i, "mt", 0))
                    for t in range(NT):
                        last = pe.transpose(bank["x"][0:H, t * P:(t + 1) * P], mx[:, t, :], ident[:, :])
                    last.then_inc(full["x"], 1)

                def merge_tile(i, j, t):
                    pe.wait_ge(permb_in, 16 * (j + 1))
                    pe.wait_ge(free[f"pj{t % 2}"], PJ.n(i, "merge", t // 2))
                    out = bank[f"pj{t % 2}"]
                    pe.matmul(out[:, :], permb[:, t * P:(t + 1) * P], b2[:, :], start=True, stop=False,
                              skip_group_check=True)
                    for a in range(GT):
                        if a % RG == 0:
                            pe.wait_ge(rp_in[a // RG], 16 * (NT * j + t + 1))
                        col = t * P + a * G
                        last = pe.matmul(out[a * G:(a + 1) * G, :], permb[:, col:col + G], rp[:, a // RG, a % RG, :],
                                         start=False, stop=True, skip_group_check=True)
                    last.then_inc(full[f"pj{t % 2}"], 1)

                if merge:
                    for t in range(NT):
                        merge_tile(None, 0, t)
                transposes(None, 1)
                queries(None, range(C))
                pe.wait_ge(kbd_in, 16 * HJ)
                for k in range(C * NT):
                    max_tile(None, 0, k)
                max_rows(None)

                def logits(i):
                    pe.wait_ge(free["x"], MT.n(i, "logits", 0))
                    three_passes(pe, bank["x"][:, :], lambda c: (wch[:, c, :], wcl[:, c, :]),
                                 lambda c: (xth[:, c, :], xtl[:, c, :]),
                                 transposed(i, "ln2")).then_inc(full["x"], 1)

                def choices(i, ts):
                    for t in ts:
                        pe.wait_ge(permed, i)
                        pe.wait_ge(free[f"tp{t % 2}"], TP.n(i, "bd", t // 2))
                        pe.transpose(bank[f"tp{t % 2}"][:, 0:ES], perm[:, t * P:(t + 1) * P], ident[:, :])\
                          .then_inc(full[f"tp{t % 2}"], 1)

                def turn(i):
                    last_, tail = last_turn(i), route and not first_turn(i)

                    def score(h):
                        pe.wait_ge(free[f"sc{h % 2}"], SC.n(i, "score", h // 2))
                        pe.matmul(bank[f"sc{h % 2}"][0:S2, :], ks[:, h, :], qs[:, h, :], start=True, stop=True)\
                          .then_inc(full[f"sc{h % 2}"], 1)

                    def values(g):
                        h = HJ * g + HJ - 1
                        for k in range(2):
                            pe.wait_ge(free[f"sc{k}"], SC.n(i, "score", h // 2) + 1)
                        pe.wait_ge(free[f"pj{g % 2}"], PJ.n(i, "pv", g // 2))
                        if g == 0:
                            pe.wait_ge(free["sm"], SM.n(i, "sum", 0))
                        for a in range(HJ):
                            ins = pe.matmul(bank["sm"][a * DK:(a + 1) * DK, :], pick[:, g, :],
                                            pr[:, (HJ * g + a) % RING, :], start=(g == 0), stop=(g == C - 1),
                                            skip_group_check=True)
                        if g == C - 1:
                            ins.then_inc(full["sm"], 1)
                        for a in range(HJ):
                            h = HJ * g + a
                            ins = pe.matmul(bank[f"pj{g % 2}"][a * DK:(a + 1) * DK, :], v[:, h * DK:(h + 1) * DK],
                                            pr[:, h % RING, :], start=True, stop=True)
                        ins.then_inc(full[f"pj{g % 2}"], 1)

                    def spread(g):
                        pe.wait_ge(free[f"tp{g % 2}"], TP.n(i, "bc", g // 2))
                        if g == 0:
                            pe.wait_ge(free["sm"], SM.n(i, "sum", 0) + 1)
                        pe.matmul(bank[f"tp{g % 2}"][:, :], bc[:, g, :], rx[:, :], start=True, stop=True)\
                          .then_inc(full[f"tp{g % 2}"], 1)

                    merging = merge and not last_
                    if merging:
                        merge_tile(i, i + 1, 0)
                    pe.wait_ge(k_in, 48 * (i + 1))
                    pe.wait_ge(q_stacked, 16 * 3 * HJ * (i + 1))
                    pe.wait_ge(m_stacked, 16 * (i + 1))
                    for h in range(6):
                        score(h)
                    pe.wait_ge(v_in, 16 * (i + 1))
                    values(0)
                    if merging:
                        merge_tile(i, i + 1, 1)
                    for h in range(6, 10):
                        score(h)
                    if tail:
                        transposes(i, 2)
                    values(1)
                    if merging:
                        merge_tile(i, i + 1, 2)
                    for h in range(10, 14):
                        score(h)
                    values(2)
                    if tail:
                        logits(i)
                    if merging:
                        merge_tile(i, i + 1, 3)
                    for h in range(14, 16):
                        score(h)
                    values(3)
                    if not last_:
                        transposes(i, 1)
                    for g in range(0, C, 2):
                        if not last_:
                            queries(i, (g // 2,))
                        spread(g)
                        spread(g + 1)
                    if not last_:
                        queries(i, range(2, C))
                        pe.wait_ge(kbd_in, 16 * HJ * (i + 2))
                    pe.wait_ge(a_lo, C * (i + 1))
                    for t in range(NT):
                        if tail:
                            choices(i, BDS[t])
                        pe.wait_ge(free[f"pj{t % 2}"], PJ.n(i, "o", t // 2))
                        out, cols = bank[f"pj{t % 2}"][:, :], slice(t * P, (t + 1) * P)
                        if merge:
                            pe.matmul(out, ones[DK:DK + 1, :], bo[:, 0, :], start=True, stop=False)
                            pe.matmul(out, ones[DK:DK + 1, :], bo[:, 1, :], start=False, stop=False)
                        ks_ = MAXES[t]
                        for m in range(C):
                            pe.matmul(out, ath[:, m, cols], woh[:, m, :], start=(route and m == 0), stop=False)
                            pe.matmul(out, ath[:, m, cols], wol[:, m, :], start=False, stop=False)
                            ins = pe.matmul(out, atl[:, m, cols], woh[:, m, :], start=False, stop=(m == C - 1))
                            if m == C - 1:
                                ins.then_inc(full[f"pj{t % 2}"], 1)
                            if not last_:
                                for k in ks_[m * len(ks_) // C:(m + 1) * len(ks_) // C]:
                                    max_tile(i, i + 1, k)
                                if t == NT - 1 and m == 1:
                                    max_rows(i)

                turns(pe, turn)
                if route:
                    transposes(B, 2)
                    logits(B)
                    pe.wait_ge(permed, B)
                    choices(B, range(NT))


def experts(nc, io):
    XQ = NTILE // 4
    NG4, NW = 4, 2
    WG = EK // 4
    with ExitStack() as outer:
        inner = outer.enter_context(nc.sbuf_tensor("e_inner", [P, EK, NG], F32))
        with ExitStack() as ctx:
            sb, banks, sem = tools(nc, ctx)
            bd = sb("e_bd", [P, NTILE, ES * GT], F32R)
            gt = sb("e_gt", [P, ES, NG])
            raw = sb("e_raw", [P, 2, XQ, P])
            xh, xl = sb("e_xh", [P, NTILE, P], F32R), sb("e_xl", [P, NTILE, P], F32R)
            w1 = sb("e_w1", [P, ES, EF])
            b1 = sb("e_b1", [P, EK])
            names = [f"e_g{i}" for i in range(NG4)] + [f"e_h{i}" for i in range(NW)]
            bank = banks(*names)
            full, free = {k: sem(k + "_full") for k in names}, {k: sem(k + "_free") for k in names}
            raw_in, w1_in, b1_in = [sem(f"e_raw_in{i}") for i in range(2)], sem("e_w1_in"), sem("e_b1_in")
            bd_in = [sem(f"e_bd_in{i}") for i in range(4)]
            x_hi, x_lo, init = sem("e_x_hi"), sem("e_x_lo"), sem("e_init")
            GU, WU = NTILE // NG4, WG // NW

            with nc.Block() as block:
                @block.sync
                def _(sp):
                    sp.dma_start(b1[:, :], io["b1"]).then_inc(b1_in, 16)

                    def load_tokens(c, q):
                        sp.dma_start(raw[:, q % 2], io["xn"][q * XQ:(q + 1) * XQ].rearrange("n p d -> p n d")[
                            :, :, bass.ds(c * P, P)]).then_inc(raw_in[q % 2], 16)

                    def load_choices(q):
                        sp.dma_start(f(bd[:, q * XQ:(q + 1) * XQ]), io["bd"].rearrange("p n e g -> p n (e g)")[
                            :, q * XQ:(q + 1) * XQ]).then_inc(bd_in[q], 16)

                    def load_w1(c):
                        sp.dma_start(w1[:, :, :], io["w1"][bass.ds(c * P, P), :].rearrange(
                            "p (e f) -> p e f", f=EF)).then_inc(w1_in, 16)

                    load_tokens(0, 0)
                    load_tokens(0, 1)
                    for q in range(4):
                        load_choices(q)
                        if q >= 2:
                            sp.wait_ge(x_lo, q - 1)
                            load_tokens(0, q)
                    load_w1(0)
                    with sp.Fori(0, C - 1) as c:
                        for q in range(4):
                            sp.wait_ge(x_lo, 4 * c + q + 3)
                            load_tokens(c + 1, q)
                        for w in range(NW):
                            sp.wait_ge(full[f"e_h{w}"], WU * (c + 1))
                        load_w1(c + 1)

                @block.scalar
                def _(act):
                    with act.Fori(0, C) as c:
                        for g in range(NG4):
                            act.wait_ge(full[f"e_g{g}"], GU * c)
                        for q in range(4):
                            act.wait_ge(raw_in[q % 2], 16 * (2 * c + q // 2 + 1))
                            act.activation(xh[:, q * XQ:(q + 1) * XQ], raw[:, q % 2], ACT.Copy).then_inc(x_hi, 1)
                        for w in range(NW):
                            act.wait_ge(full[f"e_h{w}"], WU * c)
                        for n in range(0, NTILE, 2):
                            k = n % NG4
                            act.wait_ge(full[f"e_g{k}"], GU * c + n // NG4 + 1)
                            act.activation(gt[:, :, n * GT:(n + 1) * GT],
                                           bank[f"e_g{k}"][:, :].rearrange("p (e g) -> p e g", g=GT), ACT.Copy)\
                               .then_inc(free[f"e_g{k}"], 1)

                @block.gpsimd
                def _(pool):
                    with pool.Fori(0, C) as c:
                        for q in range(4):
                            pool.wait_ge(x_hi, 4 * c + q + 1)
                            pool.tensor_tensor(xl[:, q * XQ:(q + 1) * XQ], raw[:, q % 2],
                                               f(xh[:, q * XQ:(q + 1) * XQ]), ALU.subtract).then_inc(x_lo, 1)

                @block.vector
                def _(dve):
                    dve.wait_ge(b1_in, 16)
                    dve.tensor_copy(inner[:, :, :], b1[:, :].unsqueeze(2).broadcast_to([P, EK, NG])).then_inc(init, 1)
                    dve.wait_ge(init, 1)
                    with dve.Fori(0, C) as c:
                        for w in range(NW):
                            dve.wait_ge(full[f"e_h{w}"], WU * c)
                        for n in range(1, NTILE, 2):
                            k = n % NG4
                            dve.wait_ge(full[f"e_g{k}"], GU * c + n // NG4 + 1)
                            dve.tensor_copy(gt[:, :, n * GT:(n + 1) * GT],
                                            bank[f"e_g{k}"][:, :].rearrange("p (e g) -> p e g", g=GT))\
                               .then_inc(free[f"e_g{k}"], 1)
                        for w in range(WG):
                            k = w % NW
                            dve.wait_ge(full[f"e_h{k}"], WU * c + w // NW + 1)
                            part = inner[:, 4 * w:4 * w + 4, :]
                            dve.tensor_tensor(part, bank[f"e_h{k}"][:, :].rearrange("p (k n) -> p k n", n=NG), part,
                                              ALU.add).then_inc(free[f"e_h{k}"], 1)

                @block.tensor
                def _(pe):
                    with pe.Fori(0, C) as c:
                        for n in range(NTILE):
                            k = n % NG4
                            if n % XQ == 0:
                                pe.wait_ge(bd_in[n // XQ], 16)
                                pe.wait_ge(x_lo, 4 * c + n // XQ + 1)
                            pe.wait_ge(free[f"e_g{k}"], GU * c + n // NG4)
                            pe.matmul(bank[f"e_g{k}"][:, :], xh[:, n, :], bd[:, n, :], start=True, stop=False)
                            pe.matmul(bank[f"e_g{k}"][:, :], xl[:, n, :], bd[:, n, :], start=False, stop=True)\
                              .then_inc(full[f"e_g{k}"], 1)
                        pe.wait_ge(w1_in, 16 * (c + 1))
                        for k in range(NG4):
                            pe.wait_ge(free[f"e_g{k}"], GU * (c + 1))
                        for w in range(WG):
                            k = w % NW
                            pe.wait_ge(free[f"e_h{k}"], WU * c + w // NW)
                            for b in range(4):
                                for a in range(EJ):
                                    e = (4 * w + b) * EJ + a
                                    ins = pe.matmul(bank[f"e_h{k}"][a * EF:(a + 1) * EF, b * NG:(b + 1) * NG],
                                                    w1[:, e, :], gt[:, e, :], start=True, stop=True,
                                                    skip_group_check=True)
                            ins.then_inc(full[f"e_h{k}"], 1)

        with ExitStack() as ctx:
            sb, banks, sem = tools(nc, ctx)
            diag = sb("o_diag", [P, 2, 4, EJ, NG])
            w2 = sb("o_w2", [P, 2, 4, D])
            out = sb("o_out", [NG, 4, EJ, D])
            names = [f"o_p{i}" for i in range(8)]
            bank = banks(*names)
            full, free = [sem(k + "_full") for k in names], [sem(k + "_free") for k in names]
            w2_in, out_st = [sem(f"o_w2_in{i}") for i in range(2)], [sem(f"o_out_st{i}") for i in range(4)]
            zero, diag_done = sem("o_zero"), sem("o_diag_done")
            NE = 16
            TURNS = WG // 2

            with nc.Block() as block:
                @block.sync
                def _(sp):
                    def load(g, s, first):
                        if not first:
                            for k in range(8):
                                sp.wait_ge(full[k], 4 * (g // 2) + 2 * s)
                        sp.dma_start(w2[:, s], io["w2"].rearrange("(k p) d -> p k d", p=P)[:, bass.ds(g * 4, 4)])\
                          .then_inc(w2_in[s], 16)

                    for s in range(2):
                        sp.dma_start(w2[:, s], io["w2"].rearrange("(k p) d -> p k d", p=P)[:, s * 4:s * 4 + 4])\
                          .then_inc(w2_in[s], 16)

                    def turn(u, last):
                        for s in range(2):
                            for q in range(4):
                                for k in range(4):
                                    sp.wait_ge(free[(4 * q + k) % 8], 4 * u + 2 * s + q // 2 + 1)
                                sp.dma_start(io["rp"][:, bass.ds(u * 2 * NE + s * NE + 4 * q, 4), :], out[:, q])\
                                  .then_inc(out_st[q], 16)
                            if not last:
                                for k in range(8):
                                    sp.wait_ge(full[k], 4 * u + 2 * s + 2)
                                sp.dma_start(w2[:, s], io["w2"].rearrange("(k p) d -> p k d", p=P)[
                                    :, bass.ds(u * 8 + 8 + s * 4, 4)]).then_inc(w2_in[s], 16)

                    with sp.Fori(0, TURNS - 1) as u:
                        turn(u, False)
                    turn(TURNS - 1, True)
                    for q in range(4):
                        sp.wait_ge(out_st[q], 16 * WG)

                def read_out(eng, copy, u, s, parity):
                    for e in range(parity, NE, 2):
                        k, q = e % 8, e // 4
                        eng.wait_ge(full[k], 4 * u + 2 * s + e // 8 + 1)
                        if e % 4 == parity:
                            eng.wait_ge(out_st[q], 16 * (2 * u + s))
                        copy(out[:, q, e % 4], bank[names[k]][:, :]).then_inc(free[k], 1)

                @block.gpsimd
                def _(pool):
                    pool.memset(diag[:, :, :, :, :], 0.0).then_inc(zero, 1)

                @block.scalar
                def _(act):
                    with act.Fori(0, TURNS) as u:
                        for s in range(2):
                            read_out(act, lambda o, x: act.activation(o, x, ACT.Copy), u, s, 0)

                @block.vector
                def _(dve):
                    dve.wait_ge(zero, 1)

                    def spread(u, s):
                        for a in range(EJ):
                            rows = slice(a * EF, (a + 1) * EF)
                            dve.tensor_scalar(diag[rows, s, :, a, :], inner[rows, bass.ds(u * 8 + s * 4, 4), :], 0.0,
                                              None, ALU.max).then_inc(diag_done, 1)

                    spread(0, 0)

                    def turn(u, last):
                        for s in range(2):
                            if s == 0:
                                for k in range(8):
                                    dve.wait_ge(full[k], 4 * u)
                                spread(u, 1)
                            elif not last:
                                for k in range(8):
                                    dve.wait_ge(full[k], 4 * u + 2)
                                spread(u + 1, 0)
                            read_out(dve, dve.tensor_copy, u, s, 1)

                    with dve.Fori(0, TURNS - 1) as u:
                        turn(u, False)
                    turn(TURNS - 1, True)

                @block.tensor
                def _(pe):
                    with pe.Fori(0, TURNS) as u:
                        for s in range(2):
                            pe.wait_ge(diag_done, EJ * (2 * u + s + 1))
                            pe.wait_ge(w2_in[s], 16 * (u + 1))
                            for e in range(NE):
                                k = e % 8
                                pe.wait_ge(free[k], 4 * u + 2 * s + e // 8)
                                pe.matmul(bank[names[k]][:, :], diag[:, s, e // EJ, e % EJ, :], w2[:, s, e // EJ, :],
                                          start=True, stop=True).then_inc(full[k], 1)


def feed_forward(nc, io):
    TP = Uses(["t"] * 2, ["t"] * 2, [])
    last_turn = lambda i: isinstance(i, int) and i == B - 1
    with ExitStack() as ctx:
        sb, banks, sem = tools(nc, ctx)
        wh, wl = sb("f_wh", [P, 3, C, D], F32R), sb("f_wl", [P, 3, C, D], F32R)
        ident, mhalf = sb("f_ident", [P, P]), sb("f_mhalf", [P, NT])
        mu, gate = sb("f_mu", [P, 2, C]), sb("f_gate", [P, 1])
        x4 = sb("f_x4", [P, 4, NT, D])
        xn = sb("f_xn", [P, NT, D])
        stats, mv = sb("f_stats", [P, NT, 6]), sb("f_mv", [P, NT, 2])
        mark = sb("f_mark", [P, 1])
        ve, rstd = sb("f_ve", [P, NT]), sb("f_rstd", [P, NT])
        xt, dif = sb("f_xt", [P, C, T + 1]), sb("f_dif", [P, C, T])
        mix = sb("f_mix", [P, 2, 2, T])
        xm = [[sb(f"f_xm{a}{b}", [P, C, T], F32R) for b in "hl"] for a in "kr"]
        ka, kk = sb("f_ka", [P, 2, T]), sb("f_kk", [P, 2, T])
        kh, kl = sb("f_kh", [P, C, T], F32R), sb("f_kl", [P, C, T], F32R)
        th, tmp = sb("f_th", [P, NT, D]), sb("f_tmp", [P, 2, D])
        names = [f"f_{a}{b}" for a in "tkrv" for b in range(2)]
        bank = banks(*names)
        full, free = {k: sem(k + "_full") for k in names}, {k: sem(k + "_free") for k in names}
        w_in, c_in, x_in, x_st = [sem(f"f_w_in{i}") for i in range(3)], sem("f_c_in"), sem("f_x_in"), sem("f_x_st")
        w_hi, w_lo, const, gated = sem("f_w_hi"), sem("f_w_lo"), sem("f_const"), sem("f_gated")
        ve_done, rstd_done, xn_done = sem("f_ve_done"), sem("f_rstd_done"), sem("f_xn_done")
        stored = sem("f_stored")
        mixed, mix_hi, mix_lo = ([sem(f"f_{n}{a}") for a in "kr"] for n in ("mixed", "mix_hi", "mix_lo"))
        squared, k_hi, k_lo = sem("f_squared"), sem("f_k_hi"), sem("f_k_lo")
        dchain, fchain, out_done = sem("f_dchain"), sem("f_fchain"), sem("f_out_done")

        with nc.Block() as block:
            @block.sync
            def _(sp):
                raws = (x4[:, 2], x4[:, 3], xn[:, :, :])
                for i in range(3):
                    sp.dma_start(raws[i], io["w"][i].rearrange("(c p) n -> p c n", p=P)).then_inc(w_in[i], 16)
                for i in range(2):
                    sp.dma_start(mu[:, i, :], io["mu"][i]).then_inc(c_in, 16)
                sp.dma_start(gate[:, :], io["gate"].partition_broadcast(P)).then_inc(c_in, 16)

                def load_x(j):
                    sp.dma_start(x4[:, j % 4], io["x"][j].rearrange("(t p) d -> p t d", p=P)).then_inc(x_in, 16)

                load_x(0)
                sp.wait_ge(x_in, 16)
                load_x(1)

                def turn(i):
                    if not isinstance(i, int):
                        sp.wait_ge(x_st, 16 * i)
                        sp.sem_inc(stored, 1)
                        sp.wait_ge(xn_done, NT * (i + 2))
                        load_x(i + 2)
                    sp.wait_ge(out_done, NT * (i + 1))
                    sp.dma_start(io["out"][i].rearrange("(t p) d -> p t d", p=P), x4[:, i % 4]).then_inc(x_st, 16)

                with sp.Fori(0, B - 2) as i:
                    turn(i)
                turn(B - 2)
                turn(B - 1)
                sp.wait_ge(x_st, 16 * B)

            @block.gpsimd
            def _(pool):
                steps = Steps(pool, fchain)
                steps.link(pool.memset(ident[:, :], 0.0))
                pool.affine_select(out=ident[:, :], in_=ident[:, :], compare_op=ALU.not_equal, fill=1.0, base=0,
                                   pattern=[[-1, P]], channel_multiplier=1)
                steps.link(pool.memset(mhalf[:, :], -0.5))
                pool.memset(xt[:, :, 0:1], 0.0)
                pool.drain().then_inc(const, 1)

                def power(j):
                    pool.wait_ge(ve_done, j + 1)
                    pool.tensor_tensor(rstd[:, :], ve[:, :], mhalf[:, :], ALU.pow).then_inc(rstd_done, 1)

                def mixes(j, a):
                    for c in range(C):
                        pool.wait_ge(mix_hi[a], C * j + c + 1)
                        pool.tensor_tensor(xm[a][1][:, c], mix[:, a, c % 2], f(xm[a][0][:, c]), ALU.subtract)\
                            .then_inc(mix_lo[a], 1)

                power(0)
                mixes(0, 0)
                mixes(0, 1)

                def turn(i):
                    if not last_turn(i):
                        power(i + 1)
                    for m in range(C):
                        pool.wait_ge(free[f"f_k{m % 2}"], 2 * i + m // 2 + 1)
                        if m >= 2:
                            pool.wait_ge(k_lo, C * i + m - 1)
                        pool.tensor_tensor(kk[:, m % 2], ka[:, m % 2], ka[:, m % 2], ALU.mult).then_inc(squared, 1)
                    if not last_turn(i):
                        mixes(i + 1, 0)
                        mixes(i + 1, 1)

                with pool.Fori(0, B - 1) as i:
                    turn(i)
                turn(B - 1)

            @block.scalar
            def _(act):
                raws = (x4[:, 2], x4[:, 3], xn[:, :, :])
                for i in range(3):
                    act.wait_ge(w_in[i], 16)
                    for c in range(C):
                        act.activation(wh[:, i, c], raws[i][:, c], ACT.Copy).then_inc(w_hi, 1)
                act.wait_ge(c_in, 48)
                act.activation(gate[:, :], gate[:, :], ACT.Tanh).then_inc(gated, 1)
                act.wait_ge(const, 1)

                def transposed(i):
                    for c in range(C):
                        act.wait_ge(full[f"f_t{c % 2}"], TP.n(i, "t", c // 2) + 1)
                        act.activation(xt[:, c, 1:T + 1], bank[f"f_t{c % 2}"][:, :], ACT.Copy)\
                           .then_inc(free[f"f_t{c % 2}"], 1)

                def mixes(j, a):
                    for c in range(C):
                        act.wait_ge(mixed[a], C * j + c + 1)
                        act.activation(xm[a][0][:, c], mix[:, a, c % 2], ACT.Copy).then_inc(mix_hi[a], 1)

                transposed(None)
                mixes(0, 0)
                mixes(0, 1)

                def turn(i):
                    def relu(m):
                        act.wait_ge(full[f"f_k{m % 2}"], 2 * i + m // 2 + 1)
                        if m >= 2:
                            act.wait_ge(squared, C * i + m - 1)
                        act.activation(ka[:, m % 2], bank[f"f_k{m % 2}"][:, :], ACT.Relu)\
                           .then_inc(free[f"f_k{m % 2}"], 1)

                    def high(m):
                        act.wait_ge(squared, C * i + m + 1)
                        act.activation(kh[:, m], kk[:, m % 2], ACT.Copy).then_inc(k_hi, 1)

                    relu(0)
                    relu(1)
                    high(0)
                    relu(2)
                    high(1)
                    relu(3)
                    high(2)
                    high(3)
                    if not last_turn(i):
                        transposed(i)
                        mixes(i + 1, 0)
                    for t in range(NT):
                        act.wait_ge(full[f"f_r{t % 2}"], 2 * i + t // 2 + 1)
                        for k in range(2):
                            act.wait_ge(free[f"f_v{k}"], 2 * i)
                        act.activation(th[:, t], bank[f"f_r{t % 2}"][:, :], ACT.Tanh, scale=0.5)\
                           .then_inc(free[f"f_r{t % 2}"], 1)
                    if not last_turn(i):
                        mixes(i + 1, 1)

                with act.Fori(0, B - 1) as i:
                    turn(i)
                turn(B - 1)

            @block.vector
            def _(dve):
                raws = (x4[:, 2], x4[:, 3], xn[:, :, :])
                for i in range(3):
                    for c in range(C):
                        dve.wait_ge(w_hi, C * i + c + 1)
                        dve.tensor_tensor(wl[:, i, c], raws[i][:, c], f(wh[:, i, c]), ALU.subtract).then_inc(w_lo, 1)
                dve.wait_ge(const, 1)
                steps = Steps(dve, dchain)
                dve.wait_ge(gated, 1)
                steps.link(dve.tensor_scalar(gate[:, :], gate[:, :], 0.5, None, ALU.mult))

                def norm(steps, x, j):
                    steps.count(dve.memset(mark[:, :], 0.0))
                    for t in range(NT):
                        ins = dve.bn_stats(stats[:, t, :], x[:, t, :])
                    steps.link(ins)
                    steps.count(dve.memset(mark[:, :], 0.0))
                    for t in range(NT):
                        ins = dve.bn_aggr(mv[:, t, :], stats[:, t, :])
                    steps.link(ins)
                    dve.tensor_scalar(ve[:, :], mv[:, :, 1], EPS, None, ALU.add).then_inc(ve_done, 1)
                    dve.wait_ge(rstd_done, j + 1)
                    for t in range(NT):
                        dve.tensor_scalar(xn[:, t, :], x[:, t, :], mv[:, t, 0:1], rstd[:, t:t + 1],
                                          ALU.subtract, ALU.mult).then_inc(xn_done, 1)

                def mixes(steps, i, j, a):
                    for c in range(C):
                        if a == 0:
                            dve.wait_ge(free[f"f_t{c % 2}"], TP.n(i, "t", c // 2) + 1)
                            steps.link(dve.tensor_tensor(dif[:, c], xt[:, c, 1:T + 1], xt[:, c, 0:T], ALU.subtract))
                        if c >= 2:
                            dve.wait_ge(mix_lo[a], C * j + c - 1)
                        dve.scalar_tensor_tensor(out=mix[:, a, c % 2], in0=dif[:, c], scalar=mu[:, a, c:c + 1],
                                                 in1=xt[:, c, 0:T], op0=ALU.mult, op1=ALU.add).then_inc(mixed[a], 1)

                dve.wait_ge(x_in, 16)
                dve.wait_ge(c_in, 48)
                norm(steps, x4[:, 0], 0)
                mixes(steps, None, 0, 0)
                mixes(steps, None, 0, 1)
                BEFORE = steps.n

                def turn(i):
                    steps = Steps(dve, dchain, BEFORE + TURN * i)
                    if not last_turn(i):
                        dve.wait_ge(x_in, 16 * (i + 2))
                        norm(steps, x4[:, (i + 1) % 4], i + 1)
                    for m in range(C):
                        dve.wait_ge(k_hi, C * i + m + 1)
                        dve.tensor_tensor(kl[:, m], kk[:, m % 2], f(kh[:, m]), ALU.subtract).then_inc(k_lo, 1)
                    if not last_turn(i):
                        mixes(steps, i, i + 1, 0)
                        for k in range(2):
                            dve.wait_ge(full[f"f_r{k}"], 2 * i + 2)
                        mixes(steps, i, i + 1, 1)
                    for t in range(NT):
                        dve.wait_ge(free[f"f_r{t % 2}"], 2 * i + t // 2 + 1)
                        dve.wait_ge(full[f"f_v{t % 2}"], 2 * i + t // 2 + 1)
                        dve.scalar_tensor_tensor(out=tmp[:, t % 2], in0=th[:, t], scalar=1.0,
                                                 in1=bank[f"f_v{t % 2}"][:, :], op0=ALU.add, op1=ALU.mult)\
                           .then_inc(free[f"f_v{t % 2}"], 1)
                        dve.wait_ge(free[f"f_v{t % 2}"], 2 * i + t // 2 + 1)
                        xt_ = x4[:, i % 4, t]
                        dve.scalar_tensor_tensor(out=xt_, in0=tmp[:, t % 2], scalar=gate[:, 0:1], in1=xt_,
                                                 op0=ALU.mult, op1=ALU.add).then_inc(out_done, 1)

                TURN = LN_STEPS + C
                with dve.Fori(0, B - 1) as i:
                    turn(i)
                turn(B - 1)

            @block.tensor
            def _(pe):
                pe.wait_ge(const, 1)
                pe.wait_ge(w_lo, 3 * C)

                def transposes(i):
                    pe.wait_ge(xn_done, NT * (1 if i is None else i + 2))
                    for c in range(C):
                        pe.wait_ge(free[f"f_t{c % 2}"], TP.n(i, "t", c // 2))
                        for t in range(NT):
                            last = pe.transpose(bank[f"f_t{c % 2}"][:, t * P:(t + 1) * P],
                                                xn[:, t, c * P:(c + 1) * P], ident[:, :])
                        last.then_inc(full[f"f_t{c % 2}"], 1)

                transposes(None)

                def turn(i):
                    pe.wait_ge(mix_lo[0], C * (i + 1))
                    for m in range(C):
                        cols = slice(m * P, (m + 1) * P)
                        pe.wait_ge(free[f"f_k{m % 2}"], 2 * i + m // 2)
                        three_passes(pe, bank[f"f_k{m % 2}"][:, :],
                                     lambda c: (wh[:, 0, c, cols], wl[:, 0, c, cols]),
                                     lambda c: (xm[0][0][:, c], xm[0][1][:, c])).then_inc(full[f"f_k{m % 2}"], 1)
                    if not last_turn(i):
                        transposes(i)
                    pe.wait_ge(mix_lo[1], C * (i + 1))
                    for t in range(NT):
                        cols = slice(t * P, (t + 1) * P)
                        pe.wait_ge(free[f"f_r{t % 2}"], 2 * i + t // 2)
                        three_passes(pe, bank[f"f_r{t % 2}"][:, :],
                                     lambda c: (xm[1][0][:, c, cols], xm[1][1][:, c, cols]),
                                     lambda c: (wh[:, 1, c], wl[:, 1, c])).then_inc(full[f"f_r{t % 2}"], 1)
                    pe.wait_ge(k_lo, C * (i + 1))
                    for t in range(NT):
                        cols = slice(t * P, (t + 1) * P)
                        pe.wait_ge(free[f"f_v{t % 2}"], 2 * i + t // 2)
                        three_passes(pe, bank[f"f_v{t % 2}"][:, :],
                                     lambda c: (kh[:, c, cols], kl[:, c, cols]),
                                     lambda c: (wh[:, 2, c], wl[:, 2, c])).then_inc(full[f"f_v{t % 2}"], 1)

                with pe.Fori(0, B - 1) as i:
                    turn(i)
                turn(B - 1)


def build(nc, a, out):
    def dram(name, shape, dt=F32):
        return nc.dram_tensor(name, shape, dt).ap()

    N = B * S2
    kh_d = [dram(f"s_kh{i}", (D, N)) for i in range(2)]
    kl_d = [dram(f"s_kl{i}", (D, N)) for i in range(2)]
    v_d = [dram(f"s_v{i}", (N, D)) for i in range(2)]
    x1_d, x3_d, xn_d = dram("s_x1", (B, T, D)), dram("s_x3", (B, T, D)), dram("s_xn", (B, T, D))
    perm_d = dram("s_perm", (ES, B * T))
    bd_d = dram("s_bd", (P, NTILE, ES, GT))
    rp_d = dram("s_rp", (NG, ES, D))
    keys_and_values(nc, a["ctx_t"], [a["k0"], a["v0"], a["k1"], a["v1"]], [a["bk"], a["bv"]], kh_d, kl_d, v_d)
    attention(nc, 0, dict(x=a["x"], wq=a["q0"], wo=a["o0"], gate=a["g_xattn"][0:1], gate_before=a["g_ffn"][0:1],
                          wc=a["wc"], bc=a["bc"], tie=a["tie"], kh=kh_d[0], kl=kl_d[0], v=v_d[0], x_out=x1_d,
                          xn_out=xn_d, perm=perm_d, bd=bd_d))
    experts(nc, dict(bd=bd_d, xn=xn_d.rearrange("b (t p) d -> (b t) p d", p=P), w1=a["w1"], b1=a["b1"], w2=a["w2"],
                     rp=rp_d))
    attention(nc, 1, dict(x=x1_d, wq=a["q1"], wo=a["o1"], gate=a["g_xattn"][1:2], gate_before=a["g_ffn"][0:1],
                          bq=a["bq"], bo=a["bo"], mask=a["mask"], mask_t=a["mask_t"], kh=kh_d[1], kl=kl_d[1],
                          v=v_d[1], x_out=x3_d, perm=perm_d, rp=rp_d, b2=a["b2"]))
    feed_forward(nc, dict(w=[a["wk"], a["wr"], a["wv"]], mu=[a["mu_k"], a["mu_r"]], gate=a["g_ffn"][1:2], x=x3_d,
                          out=out))


def kernel(**inputs):
    import concourse.bacc as bacc
    from concourse.bass_utils import run_bass_kernel_spmd

    g = {k: np.asarray(v) for k, v in inputs.items()}
    columns = lambda a: a.reshape(C, P).T
    arrays = dict(
        x=g["x"], ctx_t=g["ctx_1024"].reshape(B * S2, D).T, mask=g["mask_BxS2_ik0"], mask_t=g["mask_BxS2_ik0"].T,
        g_xattn=g["g_xattn"], g_ffn=g["g_ffn"],
        q0=g["L0_xattn_W_q"].T, k0=g["L0_xattn_W_k"].T, v0=g["L0_xattn_W_v"].T, o0=g["L0_xattn_W_o"].T,
        wc=g["L0_ffn_Wc"].reshape(D, ES), bc=g["L0_ffn_bc"].reshape(ES),
        w1=g["L0_ffn_W1"].reshape(ES, D, EF).transpose(1, 0, 2).reshape(D, ES * EF),
        b1=g["L0_ffn_b1"].reshape(EK, P).T,
        w2=g["L0_ffn_W2"].reshape(ES, D, EF).transpose(0, 2, 1).reshape(ES * EF, D),
        b2=g["L0_ffn_b2"].reshape(ES, D),
        q1=g["L1_xattn_Wq"].T, k1=g["L1_xattn_Wk"].T, v1=g["L1_xattn_Wv"].T, o1=g["L1_xattn_Wo"].T,
        bq=columns(g["L1_xattn_bq"]), bk=columns(g["L1_xattn_bk"]), bv=g["L1_xattn_bv"], bo=g["L1_xattn_bo"],
        wr=g["L1_ffn_W_r"].T, wk=g["L1_ffn_W_k"].T, wv=g["L1_ffn_W_v"].T,
        mu_r=columns(g["L1_ffn_mu_r"]), mu_k=columns(g["L1_ffn_mu_k"]),
        tie=np.linspace(0.0, 1e-6, G, dtype=np.float32),
    )
    nc = bacc.Bacc("TRN2", target_bir_lowering=False, num_devices=1)
    feed, aps = {}, {}
    for name, value in arrays.items():
        feed["in_" + name] = np.ascontiguousarray(value)
        aps[name] = nc.dram_tensor("in_" + name, value.shape, mybir.dt.from_np(value.dtype), kind="ExternalInput").ap()
    out = nc.dram_tensor("out", (B, T, D), F32, kind="ExternalOutput").ap()
    build(nc, aps, out)
    return run_bass_kernel_spmd(nc, [feed], core_ids=[0]).results[0]["out"]
```

```python
from contextlib import ExitStack

import concourse.bass as bass
import numpy as np
from concourse import mybir

ALU = mybir.AluOpType
ACT = mybir.ActivationFunctionType
AX = mybir.AxisListType
F32 = mybir.dt.float32
F32R = mybir.dt.float32r
I32 = mybir.dt.int32

P = 128
B, T, D = 8, 512, 512
S2 = 120
H, DK = 16, 32
C = D // P
NT = T // P
HJ = P // DK
ES, EF, G = 128, 32, 32
NG = B * T // G
GB = T // G
GT = P // G
NTILE = B * NT
EJ = P // EF
EK = ES // EJ
EPS = 1e-5
SCALE = 1.0 / float(np.sqrt(np.float32(DK)))
BIG = 1e30
RG = 2
RING = 8
STACK = 3 * DK + 1


def f(ap):
    return ap.bitcast(F32)


LN_STEPS = 4


class Steps:

    def __init__(self, eng, sem, base=0):
        self.eng, self.sem, self.base, self.n = eng, sem, base, 0

    def count(self, ins):
        ins.then_inc(self.sem, 1)
        self.n += 1

    def link(self, ins):
        self.count(ins)
        self.eng.wait_ge(self.sem, self.base + self.n)


def tools(nc, ctx):
    def sb(name, shape, dt=F32):
        return ctx.enter_context(nc.sbuf_tensor(name, shape, dt))

    def banks(*names):
        return {n: ctx.enter_context(nc.psum_tensor(n, [P, 512], F32)) for n in names}

    sems = []

    def sem(name):
        sems.append(nc.alloc_semaphore(name=name))
        return sems[-1]

    def clear():
        nc.clear_and_free_semaphores(sems)
        nc.all_engine_barrier()

    ctx.callback(clear)
    return sb, banks, sem


def three_passes(pe, out, lhs, rhs, ready=None):
    for c in range(C):
        if ready is not None:
            ready(c)
        (ah, al), (bh, bl) = lhs(c), rhs(c)
        pe.matmul(out, ah, bh, start=(c == 0), stop=False)
        pe.matmul(out, ah, bl, start=False, stop=False)
        last = pe.matmul(out, al, bh, start=False, stop=(c == C - 1))
    return last


def keys_and_values(nc, ctx_t, weights, biases, kh_d, kl_d, v_d):
    N = B * S2
    HALF = N // 2
    with ExitStack() as ctx:
        sb, banks, sem = tools(nc, ctx)
        raw = sb("kv_raw", [P, 4, C, D])
        wh, wl = sb("kv_wh", [P, 4, C, D], F32R), sb("kv_wl", [P, 4, C, D], F32R)
        craw = sb("kv_craw", [P, C, N])
        ch, cl = sb("kv_ch", [P, C, N], F32R), sb("kv_cl", [P, C, N], F32R)
        bk, bv = sb("kv_bk", [P, C]), sb("kv_bv", [S2, D])
        kh, kl = sb("kv_kh", [P, 2, HALF], F32R), sb("kv_kl", [P, 2, HALF], F32R)
        vo = sb("kv_vo", [S2, 2, D])
        ps = banks("kv_p0", "kv_p1")
        full, free = [sem(f"kv_full{i}") for i in range(2)], [sem(f"kv_free{i}") for i in range(2)]
        ctx_in, bias_in = [sem(f"kv_ctx_in{c}") for c in range(C)], sem("kv_bias_in")
        w_in = [sem(f"kv_w_in{i}") for i in range(4)]
        hi_done, lo_done, k_hi = sem("kv_hi_done"), sem("kv_lo_done"), sem("kv_k_hi")
        k_st, v_st = [sem(f"kv_k_st{i}") for i in range(2)], [sem(f"kv_v_st{i}") for i in range(2)]
        bank = [ps["kv_p0"], ps["kv_p1"]]
        units = [(lay, kind, u) for lay in range(2) for kind in "kv" for u in range(8)]
        SPLITS = {4: 1, 8: 2, 16: 3}

        with nc.Block() as block:
            @block.sync
            def _(sp):
                for i, w in enumerate(weights):
                    sp.dma_start(raw[:, i], w.rearrange("(c p) n -> p c n", p=P)).then_inc(w_in[i], 16)
                    for c in range(0 if i else C):
                        sp.dma_start(craw[:, c], ctx_t.rearrange("(c p) n -> p c n", p=P)[:, c]).then_inc(ctx_in[c], 16)
                sp.dma_start(bk[:, :], biases[0]).then_inc(bias_in, 16)
                sp.dma_start(bv[:, :], biases[1].partition_broadcast(S2)).then_inc(bias_in, 16)
                nk = nv = 0
                for n, (lay, kind, u) in enumerate(units):
                    sp.wait_ge(free[n % 2], n // 2 + 1)
                    if kind == "k":
                        m, half = u // 2, u % 2
                        rows, cols = slice(m * P, (m + 1) * P), slice(half * HALF, (half + 1) * HALF)
                        sp.dma_start(kh_d[lay][rows, cols], f(kh[:, nk % 2, :])).then_inc(k_st[nk % 2], 16)
                        sp.dma_start(kl_d[lay][rows, cols], f(kl[:, nk % 2, :])).then_inc(k_st[nk % 2], 16)
                        nk += 1
                    else:
                        sp.dma_start(v_d[lay][u * S2:(u + 1) * S2, :], vo[:, nv % 2, :]).then_inc(v_st[nv % 2], 16)
                        nv += 1
                for i in range(2):
                    sp.wait_ge(k_st[i], 32 * nk // 2)
                    sp.wait_ge(v_st[i], 16 * nv // 2)

            @block.scalar
            def _(act):
                def high_parts(i):
                    act.wait_ge(w_in[i], 16)
                    for c in range(C):
                        act.activation(wh[:, i, c], raw[:, i, c], ACT.Copy).then_inc(hi_done, 1)

                high_parts(0)
                for c in range(C):
                    act.wait_ge(ctx_in[c], 16)
                    act.activation(ch[:, c], craw[:, c], ACT.Copy).then_inc(hi_done, 1)
                nk = 0
                for n, (lay, kind, u) in enumerate(units):
                    if n in SPLITS:
                        high_parts(SPLITS[n])
                    if n == len(units) // 2:
                        act.wait_ge(bias_in, 32)
                    if kind == "k":
                        act.wait_ge(full[n % 2], n // 2 + 1)
                        if nk >= 2:
                            act.wait_ge(k_st[nk % 2], 32 * (nk // 2))
                        bias = bk[:, u // 2:u // 2 + 1] if lay else 0.0
                        act.activation(kh[:, nk % 2, :], bank[n % 2][:, 0:HALF], ACT.Identity, bias=bias)\
                           .then_inc(k_hi, 1)
                        nk += 1

            @block.vector
            def _(dve):
                def low_parts(hi, lo, whole, before):
                    for c in range(C):
                        dve.wait_ge(hi_done, before + c + 1)
                        dve.tensor_tensor(lo[:, c], whole[:, c], f(hi[:, c]), ALU.subtract).then_inc(lo_done, 1)

                low_parts(wh[:, 0], wl[:, 0], raw[:, 0], 0)
                low_parts(ch, cl, craw, C)
                nk = nv = 0
                for n, (lay, kind, u) in enumerate(units):
                    if n in SPLITS:
                        w = SPLITS[n]
                        low_parts(wh[:, w], wl[:, w], raw[:, w], C * (w + 1))
                    if n == len(units) // 2:
                        dve.wait_ge(bias_in, 32)
                    src = bank[n % 2]
                    if kind == "k":
                        dve.wait_ge(k_hi, nk + 1)
                        if nk >= 2:
                            dve.wait_ge(k_st[nk % 2], 32 * (nk // 2))
                        bias = bk[:, u // 2:u // 2 + 1] if lay else 0.0
                        dve.scalar_tensor_tensor(out=kl[:, nk % 2, :], in0=src[:, 0:HALF], scalar=bias,
                                                 in1=f(kh[:, nk % 2, :]), op0=ALU.add, op1=ALU.subtract)\
                           .then_inc(free[n % 2], 1)
                        nk += 1
                    else:
                        dve.wait_ge(full[n % 2], n // 2 + 1)
                        if nv >= 2:
                            dve.wait_ge(v_st[nv % 2], 16 * (nv // 2))
                        if lay:
                            dve.tensor_tensor(vo[:, nv % 2, :], src[0:S2, :], bv[:, :], ALU.add)\
                               .then_inc(free[n % 2], 1)
                        else:
                            dve.tensor_copy(vo[:, nv % 2, :], src[0:S2, :])\
                               .then_inc(free[n % 2], 1)
                        nv += 1

            @block.tensor
            def _(pe):
                for n, (lay, kind, u) in enumerate(units):
                    i = 2 * lay + (kind == "v")
                    if n:
                        pe.wait_ge(lo_done, C * (i + 2))
                    pe.wait_ge(free[n % 2], n // 2)
                    if kind == "k":
                        m, half = u // 2, u % 2
                        cols = slice(half * HALF, (half + 1) * HALF)
                        last = three_passes(
                            pe, bank[n % 2][:, 0:HALF],
                            lambda c: (wh[:, i, c, m * P:(m + 1) * P], wl[:, i, c, m * P:(m + 1) * P]),
                            lambda c: (ch[:, c, cols], cl[:, c, cols]),
                            None if n else lambda c: pe.wait_ge(lo_done, C + c + 1))
                    else:
                        cols = slice(u * S2, (u + 1) * S2)
                        last = three_passes(pe, bank[n % 2][0:S2, :],
                                            lambda c: (ch[:, c, cols], cl[:, c, cols]),
                                            lambda c: (wh[:, i, c, :], wl[:, i, c, :]))
                    last.then_inc(full[n % 2], 1)


class Uses:

    def __init__(self, before, turn, last, after=(), first=None):
        self.before, self.turn, self.last, self.after = before, turn, last, after
        self.first = turn if first is None else first

    def n(self, i, kind, k):
        known = i is None or isinstance(i, int)
        names = {None: self.before, 0: self.first, B - 1: self.last, B: self.after}.get(i, self.turn) \
            if known else self.turn
        at = [x for x, name in enumerate(names) if name == kind][k]
        if i is None:
            return at
        at += len(self.before)
        if known and i == 0:
            return at
        if known and i == B:
            return at + len(self.first) + len(self.turn) * (B - 2) + len(self.last)
        return i * len(self.turn) + (at + len(self.first) - len(self.turn))


def attention(nc, lay, io):
    route, merge = lay == 0, lay == 1
    if route:
        TP = Uses(["ln1"] * 2, ["ln2"] * 2 + ["ln1"] * 2 + ["bc"] * 2 + ["chosen"] * 2,
                  ["ln2"] * 2 + ["bc"] * 2 + ["chosen"] * 2, ["ln2"] * 2 + ["chosen"] * 2, ["ln1"] * 2 + ["bc"] * 2)
        PJ = Uses(["q"] * 2, ["pv"] * 2 + ["q"] * 2 + ["o"] * 2, ["pv"] * 2 + ["o"] * 2)
        MT = Uses(["mt"], ["logits", "mt"], ["logits"], ["logits"], ["mt"])
    else:
        TP = Uses(["ln1"] * 2, ["ln1"] * 2 + ["bc"] * 2, ["bc"] * 2)
        PJ = Uses(["merge", "merge", "q", "q"], ["merge", "pv", "merge", "pv", "q", "q", "o", "o"],
                  ["pv", "pv", "o", "o"])
        MT = Uses(["mt"], ["mt"], [])
    SC = Uses(["max"] * 8, ["score"] * 8 + ["max"] * 8, ["score"] * 8)
    SM = Uses([], ["sum"], ["sum"])
    AR = 4 if route else 2
    EARLY, LATE = ((0, 1), (2, 3)) if route else ((), range(C))
    MAXES = (range(0, 6), range(6, 12), range(12, C * NT), range(0))
    CHOSEN = ((), (0,), (1,), (2, 3))

    with ExitStack() as ctx:
        sb, banks, sem = tools(nc, ctx)
        n_ = lambda s: f"a{lay}_{s}"
        wqh, wql = sb(n_("wqh"), [P, C, D], F32R), sb(n_("wql"), [P, C, D], F32R)
        woh, wol = sb(n_("woh"), [P, C, D], F32R), sb(n_("wol"), [P, C, D], F32R)
        ident, mhalf = sb(n_("ident"), [P, P]), sb(n_("mhalf"), [P, NT])
        gate = sb(n_("gate"), [P, 2])
        x2 = sb(n_("x2"), [P, 2, NT, D])
        xn = sb(n_("xn"), [P, NT, D])
        stats, mv = sb(n_("stats"), [P, NT, 6]), sb(n_("mv"), [P, NT, 2])
        mark = sb(n_("mark"), [P, NT + 1])
        ve, rstd = sb(n_("ve"), [P, 2, NT]), sb(n_("rstd"), [P, 2, NT])
        xth, xtl = sb(n_("xth"), [P, C, T], F32R), sb(n_("xtl"), [P, C, T], F32R)
        qh, ql = sb(n_("qh"), [P, C, T], F32R), sb(n_("ql"), [P, C, T], F32R)
        qs = sb(n_("qs"), [STACK, H, T], F32R)
        ks = sb(n_("ks"), [STACK, H, S2], F32R)
        kbd = sb(n_("kbd"), [P, C, HJ * S2], F32R)
        v = sb(n_("v"), [S2, D])
        pick = sb(n_("pick"), [S2, HJ, DK])
        bc = sb(n_("bc"), [P, C, P], F32R)
        part = sb(n_("part"), [P, 1])
        pr = sb(n_("pr"), [S2, RING, T])
        mx, mt = sb(n_("mx"), [P, NT, H]), sb(n_("mt"), [H, T], F32R)
        rs, rx = sb(n_("rs"), [P, T]), sb(n_("rx"), [P, T], F32R)
        pvs, ao = sb(n_("pvs"), [P, C, T]), sb(n_("ao"), [P, AR, T])
        ath, atl = sb(n_("ath"), [P, C, T], F32R), sb(n_("atl"), [P, C, T], F32R)
        raw_q, raw_o = pvs[:, :, :], x2[:, 1]
        if route:
            wch, wcl = sb(n_("wch"), [P, C, ES], F32R), sb(n_("wcl"), [P, C, ES], F32R)
            bcol, tie = sb(n_("bcol"), [P, 1]), sb(n_("tie"), [P, G])
            lg, gmax = sb(n_("lg"), [P, T]), sb(n_("gmax"), [P, GB])
            perm = sb(n_("perm"), [P, T])
            chosen = sb(n_("chosen"), [P, 2, ES])
        else:
            bq = sb(n_("bq"), [P, C])
            mcol_i = sb(n_("mcol_i"), [S2, B], I32)
            mall_i = xn[0:S2, 2:4].rearrange("p c t -> p (c t)")[:, 0:B * S2].bitcast(I32)
            mall_f = pr[:, :, :].rearrange("p h t -> p (h t)")[:, 0:B * S2]
            rows_, ones = sb(n_("rows"), [DK + 1, 2 * D], F32R), sb(n_("ones"), [DK + 1, P], F32R)
            mrow = rows_[0:1, 0:B * S2].rearrange("p (b s) -> p b s", b=B)
            bo = rows_[DK:DK + 1, :].rearrange("p (a n) -> p a n", a=2)
            bo_raw = xn[DK:DK + 1, 0, :]
            mall = sb(n_("mall"), [S2, B])
            kscale, kbias, kcur = sb(n_("kscale"), [S2, B]), sb(n_("kbias"), [S2, B]), sb(n_("kcur"), [S2, 2])
            rp = sb(n_("rp"), [ES, 2, RG, D])
            permb = sb(n_("permb"), [ES, T])
            b2 = sb(n_("b2"), [ES, D])

        ps = banks(*(n_(b) for b in ("sc0", "sc1", "tp0", "tp1", "pj0", "pj1", "sm", "x")))
        bank = {k: ps[n_(k)] for k in ("sc0", "sc1", "tp0", "tp1", "pj0", "pj1", "sm", "x")}
        full = {k: sem(n_("full_" + k)) for k in bank}
        free = {k: sem(n_("free_" + k)) for k in bank}
        x_in, x_st = ([sem(n_(f"{k}{t}")) for t in range(NT if merge else 1)] for k in ("x_in", "x_st"))
        k_in, kbd_in, v_in = sem(n_("k_in")), sem(n_("kbd_in")), sem(n_("v_in"))
        w_in = [sem(n_(f"w_in{i}")) for i in range(3)]
        c_in = sem(n_("c_in"))
        w_hi, w_lo, const = sem(n_("w_hi")), sem(n_("w_lo")), sem(n_("const"))
        ve_done, rstd_done = sem(n_("ve_done")), sem(n_("rstd_done"))
        xn1, xn2 = sem(n_("xn1")), sem(n_("xn2"))
        xt_hi, q_hi, a_hi, a_lo = sem(n_("xt_hi")), sem(n_("q_hi")), sem(n_("a_hi")), sem(n_("a_lo"))
        q_stacked, m_stacked = sem(n_("q_stacked")), sem(n_("m_stacked"))
        dchain, fchain = sem(n_("dchain")), sem(n_("fchain"))
        if route:
            xn_st, perm_st = sem(n_("xn_st")), sem(n_("perm_st"))
            chosen_st = [sem(n_(f"chosen_st{i}")) for i in range(2)]
            permed, step = sem(n_("permed")), sem(n_("step"))
        else:
            kcur_done = sem(n_("kcur_done"))
            spare = {1: pvs[:, :, :], 3: xn[:, :, :]}
            spare_in = {t: sem(n_(f"spare_in{t}")) for t in spare}
            rp_in, permb_in = [sem(n_(f"rp_in{i}")) for i in range(2)], sem(n_("permb_in"))

        last_turn = lambda i: isinstance(i, int) and i == B - 1
        first_turn = lambda i: isinstance(i, int) and i == 0

        def norms_before(i, which):
            if which == 1:
                return 0 if i is None else 2 * i + 1 if route else i + 1
            return 2 * B - 1 if isinstance(i, int) and i == B else 2 * i

        def turns(eng, turn, last=1):
            if route:
                turn(0)
            with eng.Fori(1 if route else 0, B - last) as i:
                turn(i)
            for i in range(B - last, B):
                turn(i)

        def xt_base(i, which):
            return 0 if i is None else C * norms_before(i, which)

        with nc.Block() as block:
            @block.sync
            def _(sp):
                rows = lambda w: w.rearrange("(c p) n -> p c n", p=P)
                def load_x(j):
                    for t, x_in_ in enumerate(x_in):
                        ts = slice(t, t + 1) if merge else slice(0, NT)
                        sp.dma_start(x2[:, j % 2, ts], io["x"][j].rearrange("(t p) d -> p t d", p=P)[:, ts])\
                          .then_inc(x_in_, 16)

                def load_keys(j):
                    cols = bass.ds(j * S2, S2)
                    for r, k in enumerate((io["kh"], io["kl"], io["kh"])):
                        sp.dma_start(f(ks[r * DK:(r + 1) * DK]), k.rearrange("(h p) s -> p h s", p=DK)[:, :, cols])\
                          .then_inc(k_in, 16)

                def load_max_keys(j):
                    cols = bass.ds(j * S2, S2)
                    src = io["kh"].rearrange("(c j p) s -> j p c s", p=DK, j=HJ)
                    for a in range(HJ):
                        sp.dma_start(f(kbd[a * DK:(a + 1) * DK, :, a * S2:(a + 1) * S2]), src[a][:, :, cols])\
                          .then_inc(kbd_in, 16)

                def load_v(j):
                    sp.dma_start(v[:, :], io["v"][bass.ds(j * S2, S2), :]).then_inc(v_in, 16)

                def load_experts(j, t):
                    for a in range(2):
                        sp.dma_start(rp[:, a], io["rp"][bass.ds(j * GB + t * GT + a * RG, RG)].rearrange(
                            "n e d -> e n d")).then_inc(rp_in[a], 16)

                def load_spare(j, t):
                    sp.dma_start(spare[t], io["rp"][bass.ds(j * GB + t * GT, GT)].rearrange("n e d -> e n d"))\
                      .then_inc(spare_in[t], 16)

                def load_perm(j):
                    sp.dma_start(permb[:, :], io["perm"][:, bass.ds(j * T, T)]).then_inc(permb_in, 16)

                def stack_queries(i, j):
                    for k in range(2):
                        sp.wait_ge(free[f"pj{k}"], PJ.n(i, "q", 1) + 1)
                    for r, q in enumerate((qh, qh, ql)):
                        for a in range(HJ):
                            sp.dma_start(f(qs[r * DK:(r + 1) * DK]).rearrange("p (c a) t -> p c a t", a=HJ)[:, :, a],
                                         f(q[a * DK:(a + 1) * DK])).then_inc(q_stacked, 16)

                def stack_max(i):
                    sp.wait_ge(free["x"], MT.n(i, "mt", 0) + 1)
                    sp.dma_start(f(qs[3 * DK:STACK]).rearrange("a h t -> a (h t)"), f(mt[:, :])).then_inc(m_stacked, 16)

                def load_weight(i):
                    w, raw = ((io["wq"], raw_q), (io["wo"], raw_o))[i]
                    sp.dma_start(raw, rows(w)).then_inc(w_in[i], 16)

                if route:
                    load_x(0)
                sp.dma_start(gate[:, 0:1], io["gate"].partition_broadcast(P)).then_inc(c_in, 16)
                sp.dma_start(gate[:, 1:2], io["gate_before"].partition_broadcast(P)).then_inc(c_in, 16)
                if route:
                    sp.dma_start(bcol[:, :], io["bc"].rearrange("(p a) -> p a", a=1)).then_inc(c_in, 16)
                    sp.dma_start(tie[:, :], io["tie"].partition_broadcast(P)).then_inc(c_in, 16)
                    sp.dma_start(xn[:, 0, :].rearrange("p (c n) -> p c n", c=C), rows(io["wc"])).then_inc(w_in[2], 16)
                    load_weight(0)
                    load_weight(1)
                    load_keys(0)
                    load_v(0)
                else:
                    sp.dma_start(bq[:, :], io["bq"]).then_inc(c_in, 16)
                    sp.dma_start(bo_raw, io["bo"].rearrange("(a n) -> a n", a=1)).then_inc(c_in, 16)
                    sp.dma_start(mcol_i[:, :], io["mask_t"]).then_inc(c_in, 16)
                    sp.dma_start(mall_i, io["mask"].rearrange("b s -> (b s)").partition_broadcast(S2))\
                      .then_inc(c_in, 16)
                    sp.dma_start(b2[:, :], io["b2"]).then_inc(c_in, 16)
                    load_perm(0)
                    load_experts(0, 0)
                    load_x(0)
                    for t in range(1, NT):
                        sp.wait_ge(full[f"pj{(t - 1) % 2}"], PJ.n(None, "merge", (t - 1) // 2) + 1)
                        load_experts(0, t)
                        if t <= 2:
                            load_weight(t - 1)
                    load_keys(0)
                    load_v(0)
                sp.wait_ge(const, 2)
                load_max_keys(0)
                sp.wait_ge(w_lo, 1 + 2 * C)
                if merge:
                    load_x(1)
                    sp.wait_ge(full["pj1"], PJ.n(None, "merge", 1) + 1)
                    load_perm(1)
                    load_experts(1, 0)
                    for k in range(2):
                        sp.wait_ge(full[f"tp{k}"], TP.n(None, "ln1", 1) + 1)
                    load_spare(1, 3)
                    load_spare(1, 1)
                stack_queries(None, 0)
                stack_max(None)

                def store_normed(i):
                    sp.wait_ge(xn2, NT * i)
                    sp.dma_start(io["xn_out"][i - 1].rearrange("(t p) d -> p t d", p=P), xn[:, :, :])\
                      .then_inc(xn_st, 16)

                def store_perm(i):
                    sp.wait_ge(permed, i)
                    sp.dma_start(io["perm"][:, bass.ds((i - 1) * T, T)], perm[:, :]).then_inc(perm_st, 16)

                def store_chosen(i, ts):
                    for t in ts:
                        sp.wait_ge(free[f"tp{t % 2}"], TP.n(i, "chosen", t // 2) + 1)
                        sp.dma_start(io["chosen"][:, (i - 1) * NT + t], chosen[:, t % 2]).then_inc(chosen_st[t % 2], 16)

                def turn(i):
                    last, tail = last_turn(i), route and not first_turn(i)
                    ahead = merge and not last and not (isinstance(i, int) and i == B - 2)
                    if route and not last:
                        if tail:
                            sp.wait_ge(xn2, NT * i)
                            sp.sem_inc(step, 1)
                            sp.wait_ge(x_st[0], 16 * i)
                        load_x(i + 1)
                    if tail:
                        store_normed(i)
                    if not last:
                        load_max_keys(i + 1)
                        if merge:
                            sp.wait_ge(full["pj0"], PJ.n(i, "merge", 0) + 1)
                            load_experts(i + 1, 2)
                    if tail:
                        store_perm(i)
                    if not last:
                        for k in range(2):
                            sp.wait_ge(full[f"sc{k}"], SC.n(i, "score", 7) + 1)
                        load_keys(i + 1)
                        if ahead:
                            sp.wait_ge(full["pj1"], PJ.n(i, "merge", 1) + 1)
                            load_perm(i + 2)
                            load_experts(i + 2, 0)
                        for k in range(2):
                            sp.wait_ge(full[f"pj{k}"], PJ.n(i, "pv", 1) + 1)
                        load_v(i + 1)
                        if ahead:
                            for k in range(2):
                                sp.wait_ge(full[f"tp{k}"], TP.n(i, "ln1", 1) + 1)
                            load_spare(i + 2, 3)
                        stack_queries(i, i + 1)
                        if ahead:
                            for k in range(2):
                                sp.wait_ge(free[f"tp{k}"], TP.n(i, "bc", 1) + 1)
                            load_spare(i + 2, 1)
                    if tail:
                        store_chosen(i, (0, 1))
                    if route:
                        if not last:
                            stack_max(i)
                        if tail:
                            store_chosen(i, (2, 3))
                        for k in range(2):
                            sp.wait_ge(free[f"pj{k}"], PJ.n(i, "o", 1) + 1)
                        sp.dma_start(io["x_out"][i].rearrange("(t p) d -> p t d", p=P), x2[:, i % 2])\
                          .then_inc(x_st[0], 16)
                    else:
                        for t in range(NT):
                            if t == NT - 1 and not last:
                                stack_max(i)
                            sp.wait_ge(free[f"pj{t % 2}"], PJ.n(i, "o", t // 2) + 1)
                            sp.dma_start(io["x_out"][i].rearrange("(t p) d -> p t d", p=P)[:, t], x2[:, i % 2, t])\
                              .then_inc(x_st[t], 16)
                        if not last and not (isinstance(i, int) and i == B - 2):
                            for t in range(NT):
                                sp.wait_ge(x_st[t], 16 * (i + 1))
                                sp.dma_start(x2[:, i % 2, t], io["x"][i + 2].rearrange("(t p) d -> p t d", p=P)[:, t])\
                                  .then_inc(x_in[t], 16)

                turns(sp, turn, 2 if merge else 1)
                if route:
                    store_normed(B)
                    store_perm(B)
                    store_chosen(B, range(NT))
                for stored in x_st:
                    sp.wait_ge(stored, 16 * B)
                if route:
                    sp.wait_ge(xn_st, 16 * B)
                    sp.wait_ge(perm_st, 16 * B)
                    for k in range(2):
                        sp.wait_ge(chosen_st[k], 16 * B * NT // 2)

            @block.gpsimd
            def _(pool):
                steps = Steps(pool, fchain)
                steps.link(pool.memset(ident[:, :], 0.0))
                steps.link(pool.affine_select(out=ident[:, :], in_=ident[:, :], compare_op=ALU.not_equal, fill=1.0,
                                              base=0, pattern=[[-1, P]], channel_multiplier=1))
                steps.link(pool.memset(mhalf[:, :], -0.5))
                pool.drain().then_inc(const, 1)
                steps.link(pool.memset(f(kbd[:, :, :]), 0.0))
                steps.link(pool.memset(f(ks[3 * DK:STACK]), 1.0))
                pool.drain().then_inc(const, 1)

                def power(which, count):
                    pool.wait_ge(ve_done, count + 1)
                    pool.tensor_tensor(rstd[:, which, :], ve[:, which, :], mhalf[:, :], ALU.pow).then_inc(rstd_done, 1)

                power(0, 0)
                steps.link(pool.memset(pick[:, :, :], 0.0))
                for g in range(HJ):
                    steps.link(pool.memset(pick[:, g].rearrange("p (a b) -> p a b", b=HJ)[:, :, g:g + 1], 1.0))
                steps.link(pool.memset(part[:, :], -1.0))
                for j in range(HJ):
                    steps.link(pool.memset(part[j * DK:j * DK + C], 0.0))
                spread = ao[:, 0, :].rearrange("p (g c) -> p g c", g=C)
                steps.link(pool.memset(spread, 0.0))
                for g in range(C):
                    view = spread[:, g].rearrange("p (j i) -> p j i", i=DK)
                    for row in (g, C + g):
                        steps.link(pool.affine_select(out=view, in_=view, compare_op=ALU.not_equal, fill=1.0,
                                                      base=-row, pattern=[[-DK, HJ], [0, DK]],
                                                      channel_multiplier=1))
                steps.link(pool.tensor_copy(bc[:, :, :], spread))
                if merge:
                    pool.memset(f(ones[:, :]), 1.0)
                pool.drain().then_inc(const, 1)

                if merge:
                    pool.wait_ge(w_lo, 2 * C + 1)

                def turn(i):
                    last = last_turn(i)
                    if merge:
                        pool.tensor_copy(kcur[:, 0:1], kscale[:, bass.ds(i, 1)]).then_inc(kcur_done, 1)
                        pool.tensor_copy(kcur[:, 1:2], kbias[:, bass.ds(i, 1)]).then_inc(kcur_done, 1)
                    if route and not first_turn(i):
                        power(1, norms_before(i, 2))
                    if not last:
                        power(0, norms_before(i, 1))
                    for g in range(C):
                        pool.wait_ge(a_hi, C * i + g + 1)
                        pool.tensor_tensor(atl[:, g], ao[:, g % AR], f(ath[:, g]), ALU.subtract).then_inc(a_lo, 1)

                turns(pool, turn)
                if route:
                    power(1, norms_before(B, 2))

            @block.scalar
            def _(act):
                act.wait_ge(c_in, 16 * (4 if route else 7))
                act.activation(gate[:, :], gate[:, :], ACT.Tanh).then_inc(w_hi, 1)
                if route:
                    act.wait_ge(w_in[2], 16)
                    act.activation(wch[:, :, :], xn[:, 0, :].rearrange("p (c n) -> p c n", c=C), ACT.Copy)\
                       .then_inc(w_hi, 1)
                else:
                    act.activation(bo[:, 0, :], bo_raw, ACT.Copy).then_inc(w_hi, 1)
                for i, (hi, raw) in enumerate(((wqh, raw_q), (woh, raw_o))):
                    act.wait_ge(w_in[i], 16)
                    for c in range(C):
                        act.activation(hi[:, c], raw[:, c], ACT.Copy).then_inc(w_hi, 1)

                def transposed(i, which, chunks=range(C)):
                    for c in chunks:
                        kind = "ln1" if which == 1 else "ln2"
                        act.wait_ge(full[f"tp{c % 2}"], TP.n(i, kind, c // 2) + 1)
                        act.activation(xth[:, c], bank[f"tp{c % 2}"][:, :], ACT.Copy).then_inc(xt_hi, 1)

                def queries(i, j, ms):
                    for m in ms:
                        act.wait_ge(full[f"pj{m % 2}"], PJ.n(i, "q", m // 2) + 1)
                        act.activation(qh[:, m], bank[f"pj{m % 2}"][:, :], ACT.Identity,
                                       bias=bq[:, m:m + 1] if merge else 0.0).then_inc(q_hi, 1)

                def negated_max(i):
                    act.wait_ge(full["x"], MT.n(i, "mt", 0) + 1)
                    act.activation(mt[:, :], bank["x"][0:H, :], ACT.Copy, scale=-1.0).then_inc(free["x"], 1)

                transposed(None, 1)
                queries(None, 0, range(C))
                negated_max(None)
                act.wait_ge(w_lo, 2 * C + 1)

                def turn(i):
                    last = last_turn(i)

                    def exp(h):
                        act.wait_ge(full[f"sc{h % 2}"], SC.n(i, "score", h // 2) + 1)
                        if h >= RING:
                            g = (h - RING) // HJ
                            act.wait_ge(full[f"pj{g % 2}"], PJ.n(i, "pv", g // 2) + 1)
                        src = bank[f"sc{h % 2}"][0:S2, :]
                        if merge:
                            act.activation(pr[:, h % RING, :], src, ACT.Exp, scale=kcur[:, 0:1], bias=kcur[:, 1:2])\
                               .then_inc(free[f"sc{h % 2}"], 1)
                        else:
                            act.activation(pr[:, h % RING, :], src, ACT.Exp, scale=SCALE)\
                               .then_inc(free[f"sc{h % 2}"], 1)

                    def values(g):
                        act.wait_ge(full[f"pj{g % 2}"], PJ.n(i, "pv", g // 2) + 1)
                        act.activation(pvs[:, g], bank[f"pj{g % 2}"][:, :], ACT.Copy).then_inc(free[f"pj{g % 2}"], 1)

                    if merge:
                        act.wait_ge(kcur_done, 2 * (i + 1))
                    for h in range(6):
                        exp(h)
                    values(0)
                    for h in range(6, 10):
                        exp(h)
                    if route and not first_turn(i):
                        transposed(i, 2)
                    values(1)
                    for h in range(10, 16):
                        exp(h)
                    values(2)
                    if not last:
                        transposed(i, 1, EARLY)
                    values(3)
                    if not last:
                        transposed(i, 1, LATE)
                        queries(i, i + 1, (0, 1))
                    for g in range(C):
                        act.wait_ge(free[f"tp{g % 2}"], TP.n(i, "bc", g // 2) + 1)
                        act.activation(ath[:, g], ao[:, g % AR], ACT.Copy).then_inc(a_hi, 1)
                        if not last and g % 2:
                            queries(i, i + 1, (2 + g // 2,))
                    if not last:
                        negated_max(i)

                turns(act, turn)
                if route:
                    transposed(B, 2)

            @block.vector
            def _(dve):
                steps = Steps(dve, dchain)

                def split_weight(i):
                    hi, lo, raw = ((wqh, wql, raw_q), (woh, wol, raw_o))[i]
                    for c in range(C):
                        dve.wait_ge(w_hi, 2 + C * i + c + 1)
                        dve.tensor_tensor(lo[:, c], raw[:, c], f(hi[:, c]), ALU.subtract).then_inc(w_lo, 1)

                dve.wait_ge(w_hi, 2)
                if route:
                    dve.tensor_tensor(wcl[:, :, :], xn[:, 0, :].rearrange("p (c n) -> p c n", c=C), f(wch[:, :, :]),
                                      ALU.subtract).then_inc(w_lo, 1)
                else:
                    dve.tensor_scalar(mrow, mall_i[0:1].rearrange("a (b s) -> a b s", b=B), 0.0, -BIG,
                                      ALU.is_equal, ALU.mult)
                    steps.link(dve.tensor_scalar(mall_f, mall_i, 0.0, None, ALU.is_equal))
                    steps.link(dve.tensor_reduce(mall[:, :], mall_f.rearrange("p (b s) -> p b s", b=B), AX.X,
                                                 ALU.min))
                    steps.link(dve.tensor_scalar(mall[:, :], mall[:, :], BIG, -BIG, ALU.mult, ALU.add))
                    steps.link(dve.tensor_scalar(kbias[:, :], mcol_i[:, :], 0.0, None, ALU.is_equal))
                    steps.link(dve.tensor_scalar(kscale[:, :], kbias[:, :], -SCALE, SCALE, ALU.mult, ALU.add))
                    steps.link(dve.tensor_tensor(kbias[:, :], kbias[:, :], mall[:, :], ALU.mult))
                    dve.tensor_tensor(bo[:, 1, :], bo_raw, f(bo[:, 0, :]), ALU.subtract).then_inc(w_lo, 1)
                LN1, LN2, LOG = LN_STEPS + (NT - 1 if merge else 0), (LN_STEPS if route else 0), (1 if route else 0)
                FIRST = LN1 + 2
                TURN = FIRST + LN2 + LOG

                def statistics(steps, x, t):
                    steps.count(dve.memset(mark[:, t:t + 1], 0.0))
                    return dve.bn_stats(stats[:, t, :], x[:, t, :])

                def norm(steps, x, which, count, done, stored=None, ins=None):
                    if ins is None:
                        ins = statistics(steps, x, 0)
                        for t in range(1, NT):
                            ins = dve.bn_stats(stats[:, t, :], x[:, t, :])
                    steps.link(ins)
                    steps.count(dve.memset(mark[:, NT:NT + 1], 0.0))
                    for t in range(NT):
                        ins = dve.bn_aggr(mv[:, t, :], stats[:, t, :])
                    steps.link(ins)
                    dve.tensor_scalar(ve[:, which, :], mv[:, :, 1], EPS, None, ALU.add).then_inc(ve_done, 1)
                    if stored is not None:
                        dve.wait_ge(xn_st, stored)
                    dve.wait_ge(rstd_done, count + 1)
                    for t in range(NT):
                        dve.tensor_scalar(xn[:, t, :], x[:, t, :], mv[:, t, 0:1], rstd[:, which, t:t + 1],
                                          ALU.subtract, ALU.mult).then_inc(done, 1)

                def merged(steps, i, j, t):
                    dve.wait_ge(x_in[t], 16 * (j + 1))
                    dve.wait_ge(full[f"pj{t % 2}"], PJ.n(i, "merge", t // 2) + 1)
                    xt = x2[:, j % 2, t]
                    dve.scalar_tensor_tensor(out=xt, in0=bank[f"pj{t % 2}"][:, :], scalar=gate[:, 1:2], in1=xt,
                                             op0=ALU.mult, op1=ALU.add).then_inc(free[f"pj{t % 2}"], 1)
                    dve.wait_ge(free[f"pj{t % 2}"], PJ.n(i, "merge", t // 2) + 1)
                    return statistics(steps, x2[:, j % 2], t)

                def transposed(i, which):
                    kind = "ln1" if which == 1 else "ln2"
                    for c in range(C):
                        dve.wait_ge(xt_hi, xt_base(i, which) + c + 1)
                        dve.tensor_tensor(xtl[:, c], bank[f"tp{c % 2}"][:, :], f(xth[:, c]), ALU.subtract)\
                           .then_inc(free[f"tp{c % 2}"], 1)

                def queries(i, j, ms):
                    for m in ms:
                        dve.wait_ge(q_hi, C * j + m + 1)
                        src, dst = bank[f"pj{m % 2}"][:, :], ql[:, m]
                        if merge:
                            ins = dve.scalar_tensor_tensor(out=dst, in0=src, scalar=bq[:, m:m + 1], in1=f(qh[:, m]),
                                                           op0=ALU.add, op1=ALU.subtract)
                        else:
                            ins = dve.tensor_tensor(dst, src, f(qh[:, m]), ALU.subtract)
                        ins.then_inc(free[f"pj{m % 2}"], 1)

                def maxima(i, k):
                    m, t = k // NT, k % NT
                    dve.wait_ge(full[f"sc{k % 2}"], SC.n(i, "max", k // 2) + 1)
                    dve.tensor_reduce(mx[:, t, m * HJ:(m + 1) * HJ],
                                      bank[f"sc{k % 2}"][:, 0:HJ * S2].rearrange("p (a s) -> p a s", a=HJ), AX.X,
                                      ALU.max).then_inc(free[f"sc{k % 2}"], 1)

                if route:
                    dve.wait_ge(x_in[0], 16)
                ins = None
                for t in range(NT if merge else 0):
                    ins = merged(steps, None, 0, t)
                    if t == 2:
                        split_weight(0)
                norm(steps, x2[:, 0], 0, 0, xn1, ins=ins)
                if route:
                    split_weight(0)
                transposed(None, 1)
                split_weight(1)
                queries(None, 0, (0, 1, 2))
                for k in range(C * NT):
                    if k == NT:
                        queries(None, 0, (3,))
                    maxima(None, k)
                BEFORE = steps.n
                dve.wait_ge(const, 3)

                def normed_tail(steps, i):
                    for k in range(2):
                        dve.wait_ge(free[f"pj{k}"], PJ.n(i - 1, "o", 1) + 1)
                    norm(steps, x2[:, (i - 1) % 2], 1, norms_before(i, 2), xn2)
                    transposed(i, 2)

                def choose(steps, i):
                    dve.wait_ge(full["x"], MT.n(i, "logits", 0) + 1)
                    grouped = lambda a: a.rearrange("p (n t) -> p n t", t=G)
                    dve.scalar_tensor_tensor(out=grouped(lg[:, :]), in0=grouped(bank["x"][:, :]),
                                             scalar=bcol[:, 0:1],
                                             in1=tie[:, :].unsqueeze(1).broadcast_to([P, GB, G]),
                                             op0=ALU.add, op1=ALU.add).then_inc(free["x"], 1)
                    dve.wait_ge(free["x"], MT.n(i, "logits", 0) + 1)
                    steps.link(dve.tensor_reduce(gmax[:, :], grouped(lg[:, :]), AX.X, ALU.max))
                    if not (isinstance(i, int) and i == 1):
                        dve.wait_ge(perm_st, 16 * (i - 1))
                    dve.tensor_tensor(grouped(perm[:, :]), grouped(lg[:, :]),
                                      gmax[:, :].unsqueeze(2).broadcast_to([P, GB, G]), ALU.is_equal)\
                       .then_inc(permed, 1)

                def choices(i, ts):
                    for t in ts:
                        dve.wait_ge(full[f"tp{t % 2}"], TP.n(i, "chosen", t // 2) + 1)
                        count = NT // 2 * (i - 1) + t // 2
                        if not (isinstance(count, int) and count == 0):
                            dve.wait_ge(chosen_st[t % 2], 16 * count)
                        dve.tensor_copy(chosen[:, t % 2], bank[f"tp{t % 2}"][:, 0:ES])\
                           .then_inc(free[f"tp{t % 2}"], 1)

                def turn(i):
                    last, tail = last_turn(i), route and not first_turn(i)
                    steps = Steps(dve, dchain, BEFORE if first_turn(i) else TURN * i + (BEFORE + FIRST - TURN))
                    if tail:
                        normed_tail(steps, i)
                    if not last:
                        j = i + 1
                        if route:
                            dve.wait_ge(x_in[0], 16 * (j + 1))
                        ins = [merged(steps, i, j, t) for t in range(NT)][-1] if merge else None
                        norm(steps, x2[:, j % 2], 0, norms_before(i, 1), xn1, 16 * i if tail else None, ins)
                    if tail:
                        choose(steps, i)
                    if not last:
                        transposed(i, 1)
                    dve.wait_ge(full["sm"], SM.n(i, "sum", 0) + 1)
                    steps.link(dve.reciprocal(rs[:, :], bank["sm"][:, :]))
                    steps.link(dve.tensor_copy(rx[:, :], rs[:, :]))
                    dve.scalar_tensor_tensor(out=rx[:, :], in0=f(rx[:, :]), scalar=part[:, 0:1], in1=rs[:, :],
                                             op0=ALU.mult, op1=ALU.add).then_inc(free["sm"], 1)
                    for g in range(C):
                        if not last and g % 2 == 0:
                            queries(i, j, (g // 2,))
                        dve.wait_ge(full[f"tp{g % 2}"], TP.n(i, "bc", g // 2) + 1)
                        dve.wait_ge(free[f"pj{g % 2}"], PJ.n(i, "pv", g // 2) + 1)
                        if g >= AR:
                            dve.wait_ge(a_lo, C * i + g - AR + 1)
                        dve.tensor_tensor(ao[:, g % AR], bank[f"tp{g % 2}"][:, :], pvs[:, g], ALU.mult)\
                           .then_inc(free[f"tp{g % 2}"], 1)
                    if not last:
                        queries(i, j, (2, 3))
                    for t in range(NT):
                        if tail:
                            choices(i, CHOSEN[t])
                        if not last:
                            for k in MAXES[t]:
                                maxima(i, k)
                        dve.wait_ge(full[f"pj{t % 2}"], PJ.n(i, "o", t // 2) + 1)
                        xt = x2[:, i % 2, t]
                        dve.scalar_tensor_tensor(out=xt, in0=bank[f"pj{t % 2}"][:, :], scalar=gate[:, 0:1], in1=xt,
                                                 op0=ALU.mult, op1=ALU.add).then_inc(free[f"pj{t % 2}"], 1)

                turns(dve, turn)
                if route:
                    steps = Steps(dve, dchain, BEFORE + FIRST + TURN * (B - 1) - LN1)
                    normed_tail(steps, B)
                    choose(steps, B)
                    choices(B, range(NT))

            @block.tensor
            def _(pe):
                def transposes(i, which, chunks=range(C)):
                    kind = "ln1" if which == 1 else "ln2"
                    if which == 1:
                        pe.wait_ge(xn1, NT * (1 if i is None else i + 2))
                    else:
                        pe.wait_ge(xn2, NT * i)
                    for c in chunks:
                        u = TP.n(i, kind, c // 2)
                        pe.wait_ge(free[f"tp{c % 2}"], u)
                        for t in range(NT):
                            last = pe.transpose(bank[f"tp{c % 2}"][:, t * P:(t + 1) * P], xn[:, t, c * P:(c + 1) * P],
                                                ident[:, :])
                        last.then_inc(full[f"tp{c % 2}"], 1)

                def transposed(i, kind):
                    return lambda c: pe.wait_ge(free[f"tp{c % 2}"], TP.n(i, kind, c // 2) + 1)

                def queries(i, ms):
                    for m in ms:
                        pe.wait_ge(free[f"pj{m % 2}"], PJ.n(i, "q", m // 2))
                        cols = slice(m * P, (m + 1) * P)
                        three_passes(pe, bank[f"pj{m % 2}"][:, :],
                                     lambda c: (wqh[:, c, cols], wql[:, c, cols]),
                                     lambda c: (xth[:, c, :], xtl[:, c, :]),
                                     transposed(i, "ln1") if m == 0 else None).then_inc(full[f"pj{m % 2}"], 1)

                def max_tile(i, j, k):
                    m, t = k // NT, k % NT
                    pe.wait_ge(free[f"sc{k % 2}"], SC.n(i, "max", k // 2))
                    if t == 0:
                        pe.wait_ge(q_hi, C * j + m + 1)
                    out = bank[f"sc{k % 2}"][:, 0:HJ * S2]
                    last = pe.matmul(out, qh[:, m, t * P:(t + 1) * P], kbd[:, m, :], start=True, stop=not merge)
                    if merge:
                        last = pe.matmul(out.rearrange("p (a s) -> p a s", a=HJ), ones[0:1, :],
                                         mrow[:, bass.ds(j, 1), :].broadcast_to([1, HJ, S2]), start=False, stop=True)
                    last.then_inc(full[f"sc{k % 2}"], 1)

                def max_rows(i):
                    for k in range(2):
                        pe.wait_ge(free[f"sc{k}"], SC.n(i, "max", 7) + 1)
                    pe.wait_ge(free["x"], MT.n(i, "mt", 0))
                    for t in range(NT):
                        last = pe.transpose(bank["x"][0:H, t * P:(t + 1) * P], mx[:, t, :], ident[:, :])
                    last.then_inc(full["x"], 1)

                def merge_tile(i, j, t):
                    pe.wait_ge(permb_in, 16 * (j + 1))
                    pe.wait_ge(free[f"pj{t % 2}"], PJ.n(i, "merge", t // 2))
                    out = bank[f"pj{t % 2}"]
                    pe.matmul(out[:, :], permb[:, t * P:(t + 1) * P], b2[:, :], start=True, stop=False,
                              skip_group_check=True)
                    for a in range(GT):
                        col = t * P + a * G
                        if i is None or t % 2 == 0:
                            if a % RG == 0:
                                pe.wait_ge(rp_in[a // RG], 16 * (t + 1) if i is None else 32 * j + 16 * (3 + t // 2))
                            results = rp[:, a // RG, a % RG, :]
                        else:
                            if a == 0:
                                pe.wait_ge(spare_in[t], 16 * j)
                            results = spare[t][:, a, :]
                        last = pe.matmul(out[a * G:(a + 1) * G, :], permb[:, col:col + G], results,
                                         start=False, stop=True, skip_group_check=True)
                    last.then_inc(full[f"pj{t % 2}"], 1)

                if merge:
                    for t in range(NT):
                        merge_tile(None, 0, t)
                pe.wait_ge(const, 1)
                transposes(None, 1)
                pe.wait_ge(w_lo, 1 + C)
                queries(None, (0, 1, 2))
                pe.wait_ge(const, 3)
                pe.wait_ge(kbd_in, 16 * HJ)
                for k in range(C * NT):
                    if k == NT:
                        queries(None, (3,))
                    max_tile(None, 0, k)
                max_rows(None)
                pe.wait_ge(w_lo, 1 + 2 * C)

                def logits(i):
                    pe.wait_ge(free["x"], MT.n(i, "logits", 0))
                    three_passes(pe, bank["x"][:, :], lambda c: (wch[:, c, :], wcl[:, c, :]),
                                 lambda c: (xth[:, c, :], xtl[:, c, :]),
                                 transposed(i, "ln2")).then_inc(full["x"], 1)

                def choices(i, ts):
                    for t in ts:
                        pe.wait_ge(permed, i)
                        pe.wait_ge(free[f"tp{t % 2}"], TP.n(i, "chosen", t // 2))
                        pe.transpose(bank[f"tp{t % 2}"][:, 0:ES], perm[:, t * P:(t + 1) * P], ident[:, :])\
                          .then_inc(full[f"tp{t % 2}"], 1)

                def turn(i):
                    last_, tail = last_turn(i), route and not first_turn(i)

                    def score(h):
                        pe.wait_ge(free[f"sc{h % 2}"], SC.n(i, "score", h // 2))
                        pe.matmul(bank[f"sc{h % 2}"][0:S2, :], ks[:, h, :], qs[:, h, :], start=True, stop=True)\
                          .then_inc(full[f"sc{h % 2}"], 1)

                    def values(g):
                        h = HJ * g + HJ - 1
                        for k in range(2):
                            pe.wait_ge(free[f"sc{k}"], SC.n(i, "score", h // 2) + 1)
                        pe.wait_ge(free[f"pj{g % 2}"], PJ.n(i, "pv", g // 2))
                        if g == 0:
                            pe.wait_ge(free["sm"], SM.n(i, "sum", 0))
                        for a in range(HJ):
                            ins = pe.matmul(bank["sm"][a * DK:(a + 1) * DK, :], pick[:, g, :],
                                            pr[:, (HJ * g + a) % RING, :], start=(g == 0), stop=(g == C - 1),
                                            skip_group_check=True)
                        if g == C - 1:
                            ins.then_inc(full["sm"], 1)
                        for a in range(HJ):
                            h = HJ * g + a
                            ins = pe.matmul(bank[f"pj{g % 2}"][a * DK:(a + 1) * DK, :], v[:, h * DK:(h + 1) * DK],
                                            pr[:, h % RING, :], start=True, stop=True)
                        ins.then_inc(full[f"pj{g % 2}"], 1)

                    def spread(g):
                        pe.wait_ge(free[f"tp{g % 2}"], TP.n(i, "bc", g // 2))
                        if g == 0:
                            pe.wait_ge(free["sm"], SM.n(i, "sum", 0) + 1)
                        pe.matmul(bank[f"tp{g % 2}"][:, :], bc[:, g, :], rx[:, :], start=True, stop=True)\
                          .then_inc(full[f"tp{g % 2}"], 1)

                    merging = merge and not last_

                    def merge_(t):
                        if merging:
                            merge_tile(i, i + 1, t)

                    merge_(0)
                    pe.wait_ge(k_in, 48 * (i + 1))
                    pe.wait_ge(q_stacked, 16 * 3 * HJ * (i + 1))
                    pe.wait_ge(m_stacked, 16 * (i + 1))
                    for h in range(2):
                        score(h)
                    merge_(1)
                    for h in range(2, 6):
                        score(h)
                    pe.wait_ge(v_in, 16 * (i + 1))
                    values(0)
                    for h in range(6, 8):
                        score(h)
                    merge_(2)
                    for h in range(8, 10):
                        score(h)
                    if tail:
                        transposes(i, 2)
                    values(1)
                    for h in range(10, 12):
                        score(h)
                    merge_(3)
                    if tail:
                        logits(i)
                    for h in range(12, 16):
                        score(h)
                    values(2)
                    if not last_ and EARLY:
                        transposes(i, 1, EARLY)
                    values(3)
                    if not last_:
                        transposes(i, 1, LATE)
                        queries(i, (0, 1))
                    for g in range(0, C, 2):
                        spread(g)
                        spread(g + 1)
                        if not last_:
                            queries(i, (2 + g // 2,))
                    if not last_:
                        pe.wait_ge(kbd_in, 16 * HJ * (i + 2))
                    for t in range(NT):
                        if tail:
                            choices(i, CHOSEN[t])
                        pe.wait_ge(free[f"pj{t % 2}"], PJ.n(i, "o", t // 2))
                        out, cols = bank[f"pj{t % 2}"][:, :], slice(t * P, (t + 1) * P)
                        if merge:
                            pe.matmul(out, ones[DK:DK + 1, :], bo[:, 0, :], start=True, stop=False)
                            pe.matmul(out, ones[DK:DK + 1, :], bo[:, 1, :], start=False, stop=False)
                        maxes = MAXES[t]
                        for m in range(C):
                            if t == 0:
                                pe.wait_ge(a_lo, C * i + m + 1)
                            pe.matmul(out, ath[:, m, cols], woh[:, m, :], start=(route and m == 0), stop=False)
                            pe.matmul(out, ath[:, m, cols], wol[:, m, :], start=False, stop=False)
                            ins = pe.matmul(out, atl[:, m, cols], woh[:, m, :], start=False, stop=(m == C - 1))
                            if m == C - 1:
                                ins.then_inc(full[f"pj{t % 2}"], 1)
                            if not last_:
                                for k in maxes[m * len(maxes) // C:(m + 1) * len(maxes) // C]:
                                    max_tile(i, i + 1, k)
                                if t == NT - 1 and m == 0:
                                    max_rows(i)

                turns(pe, turn)
                if route:
                    transposes(B, 2)
                    logits(B)
                    pe.wait_ge(permed, B)
                    choices(B, range(NT))


def experts(nc, io):
    XQ = NTILE // 4
    NG4, NW = 4, 2
    WG = EK // 4
    with ExitStack() as outer:
        inner = outer.enter_context(nc.sbuf_tensor("e_inner", [P, EK, NG], F32))
        with ExitStack() as ctx:
            sb, banks, sem = tools(nc, ctx)
            bd = sb("e_bd", [P, NTILE, ES * GT], F32R)
            gt = sb("e_gt", [P, ES, NG])
            raw = sb("e_raw", [P, 2, XQ, P])
            xh, xl = sb("e_xh", [P, NTILE, P], F32R), sb("e_xl", [P, NTILE, P], F32R)
            w1 = sb("e_w1", [P, ES, EF])
            b1 = sb("e_b1", [P, EK])
            gmask = sb("e_gmask", [P, GT])
            chosen = inner[:, :, :]
            ON_POOL = [n for n in range(NTILE) if n % 3 == 2]

            def spread(eng, n, done):
                eng.tensor_tensor(bd[:, n].rearrange("p (e g) -> p e g", g=GT),
                                  chosen[:, n].unsqueeze(2).broadcast_to([P, ES, GT]),
                                  gmask[:, :].unsqueeze(1).broadcast_to([P, ES, GT]), ALU.mult).then_inc(done, 1)
            names = [f"e_g{i}" for i in range(NG4)] + [f"e_h{i}" for i in range(NW)]
            bank = banks(*names)
            full, free = {k: sem(k + "_full") for k in names}, {k: sem(k + "_free") for k in names}
            raw_in, w1_in, b1_in = [sem(f"e_raw_in{i}") for i in range(2)], sem("e_w1_in"), sem("e_b1_in")
            chosen_in = [sem(f"e_chosen_in{i}") for i in range(4)]
            chain, masked, bd_pool, bd_dve = sem("e_chain"), sem("e_masked"), sem("e_bd_pool"), sem("e_bd_dve")
            x_hi, x_lo, init = sem("e_x_hi"), sem("e_x_lo"), sem("e_init")
            GU, WU = NTILE // NG4, WG // NW

            with nc.Block() as block:
                @block.sync
                def _(sp):
                    def load_tokens(c, q):
                        sp.dma_start(raw[:, q % 2], io["xn"][q * XQ:(q + 1) * XQ].rearrange("n p d -> p n d")[
                            :, :, bass.ds(c * P, P)]).then_inc(raw_in[q % 2], 16)

                    def load_choices(q):
                        sp.dma_start(chosen[:, q * XQ:(q + 1) * XQ], io["chosen"][:, q * XQ:(q + 1) * XQ])\
                          .then_inc(chosen_in[q], 16)

                    def load_w1(c):
                        sp.dma_start(w1[:, :, :], io["w1"][bass.ds(c * P, P), :].rearrange(
                            "p (e f) -> p e f", f=EF)).then_inc(w1_in, 16)

                    load_tokens(0, 0)
                    load_choices(0)
                    load_tokens(0, 1)
                    for q in range(1, 4):
                        load_choices(q)
                    sp.dma_start(b1[:, :], io["b1"]).then_inc(b1_in, 16)
                    for q in range(2, 4):
                        sp.wait_ge(x_lo, q - 1)
                        load_tokens(0, q)
                    load_w1(0)
                    with sp.Fori(0, C - 1) as c:
                        for q in range(4):
                            sp.wait_ge(x_lo, 4 * c + q + 3)
                            load_tokens(c + 1, q)
                        for w in range(NW):
                            sp.wait_ge(full[f"e_h{w}"], WU * (c + 1))
                        load_w1(c + 1)

                @block.scalar
                def _(act):
                    def turn(c, tiles):
                        for g in range(NG4):
                            act.wait_ge(full[f"e_g{g}"], GU * c)
                        for q in range(4):
                            act.wait_ge(raw_in[q % 2], 16 * (2 * c + q // 2 + 1))
                            act.activation(xh[:, q * XQ:(q + 1) * XQ], raw[:, q % 2], ACT.Copy).then_inc(x_hi, 1)
                            if isinstance(c, int):
                                gathered(c, [n for n in tiles if q and n // XQ == q - 1])
                        if isinstance(c, int):
                            gathered(c, [n for n in tiles if n // XQ == 3])
                        else:
                            for w in range(NW):
                                act.wait_ge(full[f"e_h{w}"], WU * c)
                            gathered(c, tiles)

                    def gathered(c, tiles):
                        for n in tiles:
                            k = n % NG4
                            act.wait_ge(full[f"e_g{k}"], GU * c + n // NG4 + 1)
                            act.activation(gt[:, :, n * GT:(n + 1) * GT],
                                           bank[f"e_g{k}"][:, :].rearrange("p (e g) -> p e g", g=GT), ACT.Copy)\
                               .then_inc(free[f"e_g{k}"], 1)

                    turn(0, range(NTILE))
                    with act.Fori(1, C) as c:
                        turn(c, range(0, NTILE, 2))

                @block.gpsimd
                def _(pool):
                    steps = Steps(pool, chain)
                    steps.link(pool.memset(gmask[:, :], 0.0))
                    for a in range(GT):
                        steps.link(pool.memset(gmask[a * G:(a + 1) * G, a:a + 1], 1.0))
                    pool.drain().then_inc(masked, 1)

                    def low_part(c, q):
                        pool.wait_ge(x_hi, 4 * c + q + 1)
                        pool.tensor_tensor(xl[:, q * XQ:(q + 1) * XQ], raw[:, q % 2],
                                           f(xh[:, q * XQ:(q + 1) * XQ]), ALU.subtract).then_inc(x_lo, 1)

                    for q in range(4):
                        low_part(0, q)
                        pool.wait_ge(chosen_in[q], 16)
                        for n in range(q * XQ, (q + 1) * XQ):
                            if n in ON_POOL:
                                spread(pool, n, bd_pool)
                    with pool.Fori(1, C) as c:
                        for q in range(4):
                            low_part(c, q)

                @block.vector
                def _(dve):
                    dve.wait_ge(masked, 1)
                    for n in range(NTILE):
                        if n % XQ == 0:
                            dve.wait_ge(chosen_in[n // XQ], 16)
                        if n not in ON_POOL:
                            spread(dve, n, bd_dve)
                    dve.wait_ge(b1_in, 16)
                    dve.wait_ge(bd_dve, NTILE - len(ON_POOL))
                    dve.wait_ge(bd_pool, len(ON_POOL))
                    dve.tensor_copy(inner[:, :, :], b1[:, :].unsqueeze(2).broadcast_to([P, EK, NG])).then_inc(init, 1)
                    dve.wait_ge(init, 1)

                    def turn(c, tiles):
                        for w in range(NW):
                            dve.wait_ge(full[f"e_h{w}"], WU * c)
                        for n in tiles:
                            k = n % NG4
                            dve.wait_ge(full[f"e_g{k}"], GU * c + n // NG4 + 1)
                            dve.tensor_copy(gt[:, :, n * GT:(n + 1) * GT],
                                            bank[f"e_g{k}"][:, :].rearrange("p (e g) -> p e g", g=GT))\
                               .then_inc(free[f"e_g{k}"], 1)
                        for w in range(WG):
                            k = w % NW
                            dve.wait_ge(full[f"e_h{k}"], WU * c + w // NW + 1)
                            part = inner[:, 4 * w:4 * w + 4, :]
                            dve.tensor_tensor(part, bank[f"e_h{k}"][:, :].rearrange("p (k n) -> p k n", n=NG), part,
                                              ALU.add).then_inc(free[f"e_h{k}"], 1)

                    turn(0, ())
                    with dve.Fori(1, C) as c:
                        turn(c, range(1, NTILE, 2))

                @block.tensor
                def _(pe):
                    with pe.Fori(0, C) as c:
                        for n in range(NTILE):
                            k = n % NG4
                            if n % XQ == 0:
                                pe.wait_ge(x_lo, 4 * c + n // XQ + 1)
                            if n in ON_POOL:
                                pe.wait_ge(bd_pool, ON_POOL.index(n) + 1)
                            else:
                                pe.wait_ge(bd_dve, n + 1 - sum(m < n for m in ON_POOL))
                            pe.wait_ge(free[f"e_g{k}"], GU * c + n // NG4)
                            pe.matmul(bank[f"e_g{k}"][:, :], xh[:, n, :], bd[:, n, :], start=True, stop=False)
                            pe.matmul(bank[f"e_g{k}"][:, :], xl[:, n, :], bd[:, n, :], start=False, stop=True)\
                              .then_inc(full[f"e_g{k}"], 1)
                        pe.wait_ge(w1_in, 16 * (c + 1))
                        for k in range(NG4):
                            pe.wait_ge(free[f"e_g{k}"], GU * (c + 1))
                        for w in range(WG):
                            k = w % NW
                            pe.wait_ge(free[f"e_h{k}"], WU * c + w // NW)
                            for b in range(4):
                                for a in range(EJ):
                                    e = (4 * w + b) * EJ + a
                                    ins = pe.matmul(bank[f"e_h{k}"][a * EF:(a + 1) * EF, b * NG:(b + 1) * NG],
                                                    w1[:, e, :], gt[:, e, :], start=True, stop=True,
                                                    skip_group_check=True)
                            ins.then_inc(full[f"e_h{k}"], 1)

        with ExitStack() as ctx:
            sb, banks, sem = tools(nc, ctx)
            diag = sb("o_diag", [P, 2, 4, EJ, NG])
            w2 = sb("o_w2", [P, 2, 4, D])
            out = sb("o_out", [NG, 4, EJ, D])
            names = [f"o_p{i}" for i in range(8)]
            bank = banks(*names)
            full, free = [sem(k + "_full") for k in names], [sem(k + "_free") for k in names]
            w2_in, out_st = [sem(f"o_w2_in{i}") for i in range(2)], [sem(f"o_out_st{i}") for i in range(4)]
            zero, diag_done = sem("o_zero"), sem("o_diag_done")
            NE = 16
            TURNS = WG // 2

            with nc.Block() as block:
                @block.sync
                def _(sp):
                    def load(g, s, first):
                        if not first:
                            for k in range(8):
                                sp.wait_ge(full[k], 4 * (g // 2) + 2 * s)
                        sp.dma_start(w2[:, s], io["w2"].rearrange("(k p) d -> p k d", p=P)[:, bass.ds(g * 4, 4)])\
                          .then_inc(w2_in[s], 16)

                    for s in range(2):
                        sp.dma_start(w2[:, s], io["w2"].rearrange("(k p) d -> p k d", p=P)[:, s * 4:s * 4 + 4])\
                          .then_inc(w2_in[s], 16)

                    def turn(u, last):
                        for s in range(2):
                            for q in range(4):
                                for k in range(4):
                                    sp.wait_ge(free[(4 * q + k) % 8], 4 * u + 2 * s + q // 2 + 1)
                                sp.dma_start(io["rp"][:, bass.ds(u * 2 * NE + s * NE + 4 * q, 4), :], out[:, q])\
                                  .then_inc(out_st[q], 16)
                            if not last:
                                for k in range(8):
                                    sp.wait_ge(full[k], 4 * u + 2 * s + 2)
                                sp.dma_start(w2[:, s], io["w2"].rearrange("(k p) d -> p k d", p=P)[
                                    :, bass.ds(u * 8 + 8 + s * 4, 4)]).then_inc(w2_in[s], 16)

                    with sp.Fori(0, TURNS - 1) as u:
                        turn(u, False)
                    turn(TURNS - 1, True)
                    for q in range(4):
                        sp.wait_ge(out_st[q], 16 * WG)

                def read_out(eng, copy, u, s, parity):
                    for e in range(parity, NE, 2):
                        k, q = e % 8, e // 4
                        eng.wait_ge(full[k], 4 * u + 2 * s + e // 8 + 1)
                        if e % 4 == parity:
                            eng.wait_ge(out_st[q], 16 * (2 * u + s))
                        copy(out[:, q, e % 4], bank[names[k]][:, :]).then_inc(free[k], 1)

                @block.gpsimd
                def _(pool):
                    pool.memset(diag[:, :, :, :, :], 0.0).then_inc(zero, 1)

                @block.scalar
                def _(act):
                    with act.Fori(0, TURNS) as u:
                        for s in range(2):
                            read_out(act, lambda o, x: act.activation(o, x, ACT.Copy), u, s, 0)

                @block.vector
                def _(dve):
                    dve.wait_ge(zero, 1)

                    def spread(u, s):
                        for a in range(EJ):
                            rows = slice(a * EF, (a + 1) * EF)
                            dve.tensor_scalar(diag[rows, s, :, a, :], inner[rows, bass.ds(u * 8 + s * 4, 4), :], 0.0,
                                              None, ALU.max).then_inc(diag_done, 1)

                    spread(0, 0)

                    def turn(u, last):
                        for s in range(2):
                            if s == 0:
                                for k in range(8):
                                    dve.wait_ge(full[k], 4 * u)
                                spread(u, 1)
                            elif not last:
                                for k in range(8):
                                    dve.wait_ge(full[k], 4 * u + 2)
                                spread(u + 1, 0)
                            read_out(dve, dve.tensor_copy, u, s, 1)

                    with dve.Fori(0, TURNS - 1) as u:
                        turn(u, False)
                    turn(TURNS - 1, True)

                @block.tensor
                def _(pe):
                    with pe.Fori(0, TURNS) as u:
                        for s in range(2):
                            pe.wait_ge(diag_done, EJ * (2 * u + s + 1))
                            pe.wait_ge(w2_in[s], 16 * (u + 1))
                            for e in range(NE):
                                k = e % 8
                                pe.wait_ge(free[k], 4 * u + 2 * s + e // 8)
                                pe.matmul(bank[names[k]][:, :], diag[:, s, e // EJ, e % EJ, :], w2[:, s, e // EJ, :],
                                          start=True, stop=True).then_inc(full[k], 1)


def feed_forward(nc, io):
    TP = Uses(["t"] * 2, ["t"] * 2, [])
    last_turn = lambda i: isinstance(i, int) and i == B - 1
    with ExitStack() as ctx:
        sb, banks, sem = tools(nc, ctx)
        wh, wl = sb("f_wh", [P, 3, C, D], F32R), sb("f_wl", [P, 3, C, D], F32R)
        ident, mhalf = sb("f_ident", [P, P]), sb("f_mhalf", [P, NT])
        mu, gate = sb("f_mu", [P, 2, C]), sb("f_gate", [P, 1])
        x4 = sb("f_x4", [P, 4, NT, D])
        xn = sb("f_xn", [P, NT, D])
        stats, mv = sb("f_stats", [P, NT, 6]), sb("f_mv", [P, NT, 2])
        mark = sb("f_mark", [P, 1])
        ve, rstd = sb("f_ve", [P, NT]), sb("f_rstd", [P, NT])
        xt, dif = sb("f_xt", [P, C, T + 1]), sb("f_dif", [P, C, T])
        mix = sb("f_mix", [P, 2, 2, T])
        xm = [[sb(f"f_xm{a}{b}", [P, C, T], F32R) for b in "hl"] for a in "kr"]
        ka, kk = sb("f_ka", [P, 2, T]), sb("f_kk", [P, 2, T])
        kh, kl = sb("f_kh", [P, C, T], F32R), sb("f_kl", [P, C, T], F32R)
        th, tmp = sb("f_th", [P, NT, D]), sb("f_tmp", [P, 2, D])
        names = [f"f_{a}{b}" for a in "tkrv" for b in range(2)]
        bank = banks(*names)
        full, free = {k: sem(k + "_full") for k in names}, {k: sem(k + "_free") for k in names}
        w_in, c_in, x_in, x_st = [sem(f"f_w_in{i}") for i in range(3)], sem("f_c_in"), sem("f_x_in"), sem("f_x_st")
        w_hi, w_lo, const, gated = sem("f_w_hi"), sem("f_w_lo"), sem("f_const"), sem("f_gated")
        ve_done, rstd_done, xn_done = sem("f_ve_done"), sem("f_rstd_done"), sem("f_xn_done")
        stored = sem("f_stored")
        mixed, mix_hi, mix_lo = ([sem(f"f_{n}{a}") for a in "kr"] for n in ("mixed", "mix_hi", "mix_lo"))
        squared, k_hi, k_lo = sem("f_squared"), sem("f_k_hi"), sem("f_k_lo")
        dchain, fchain, out_done = sem("f_dchain"), sem("f_fchain"), sem("f_out_done")

        raws = (x4[:, 2], x4[:, 3], th[:, :, :])

        with nc.Block() as block:
            @block.sync
            def _(sp):
                def load_x(j):
                    sp.dma_start(x4[:, j % 4], io["x"][j].rearrange("(t p) d -> p t d", p=P)).then_inc(x_in, 16)

                load_x(0)
                for i in range(2):
                    sp.dma_start(mu[:, i, :], io["mu"][i]).then_inc(c_in, 16)
                sp.dma_start(gate[:, :], io["gate"].partition_broadcast(P)).then_inc(c_in, 16)
                for i in range(3):
                    sp.dma_start(raws[i], io["w"][i].rearrange("(c p) n -> p c n", p=P)).then_inc(w_in[i], 16)
                sp.wait_ge(x_in, 16)
                load_x(1)

                def turn(i):
                    if not isinstance(i, int):
                        sp.wait_ge(x_st, 16 * i)
                        sp.sem_inc(stored, 1)
                        sp.wait_ge(xn_done, NT * (i + 2))
                        load_x(i + 2)
                    sp.wait_ge(out_done, NT * (i + 1))
                    sp.dma_start(io["out"][i].rearrange("(t p) d -> p t d", p=P), x4[:, i % 4]).then_inc(x_st, 16)

                with sp.Fori(0, B - 2) as i:
                    turn(i)
                turn(B - 2)
                turn(B - 1)
                sp.wait_ge(x_st, 16 * B)

            @block.gpsimd
            def _(pool):
                steps = Steps(pool, fchain)
                steps.link(pool.memset(ident[:, :], 0.0))
                pool.affine_select(out=ident[:, :], in_=ident[:, :], compare_op=ALU.not_equal, fill=1.0, base=0,
                                   pattern=[[-1, P]], channel_multiplier=1)
                steps.link(pool.memset(mhalf[:, :], -0.5))
                pool.memset(xt[:, :, 0:1], 0.0)
                pool.drain().then_inc(const, 1)

                def power(j):
                    pool.wait_ge(ve_done, j + 1)
                    pool.tensor_tensor(rstd[:, :], ve[:, :], mhalf[:, :], ALU.pow).then_inc(rstd_done, 1)

                def mixes(j, a):
                    for c in range(C):
                        pool.wait_ge(mix_hi[a], C * j + c + 1)
                        pool.tensor_tensor(xm[a][1][:, c], mix[:, a, c % 2], f(xm[a][0][:, c]), ALU.subtract)\
                            .then_inc(mix_lo[a], 1)

                power(0)
                mixes(0, 0)
                mixes(0, 1)

                def turn(i):
                    if not last_turn(i):
                        power(i + 1)
                    for m in range(C):
                        pool.wait_ge(free[f"f_k{m % 2}"], 2 * i + m // 2 + 1)
                        if m >= 2:
                            pool.wait_ge(k_lo, C * i + m - 1)
                        pool.tensor_tensor(kk[:, m % 2], ka[:, m % 2], ka[:, m % 2], ALU.mult).then_inc(squared, 1)
                    if not last_turn(i):
                        mixes(i + 1, 0)
                        mixes(i + 1, 1)

                with pool.Fori(0, B - 1) as i:
                    turn(i)
                turn(B - 1)

            @block.scalar
            def _(act):
                def high_parts(i):
                    act.wait_ge(w_in[i], 16)
                    for c in range(C):
                        act.activation(wh[:, i, c], raws[i][:, c], ACT.Copy).then_inc(w_hi, 1)

                act.wait_ge(c_in, 48)
                act.activation(gate[:, :], gate[:, :], ACT.Tanh).then_inc(gated, 1)
                high_parts(0)
                act.wait_ge(const, 1)

                def transposed(i):
                    for c in range(C):
                        act.wait_ge(full[f"f_t{c % 2}"], TP.n(i, "t", c // 2) + 1)
                        act.activation(xt[:, c, 1:T + 1], bank[f"f_t{c % 2}"][:, :], ACT.Copy)\
                           .then_inc(free[f"f_t{c % 2}"], 1)

                def mixes(j, a):
                    for c in range(C):
                        act.wait_ge(mixed[a], C * j + c + 1)
                        act.activation(xm[a][0][:, c], mix[:, a, c % 2], ACT.Copy).then_inc(mix_hi[a], 1)

                transposed(None)
                mixes(0, 0)
                mixes(0, 1)
                high_parts(1)
                high_parts(2)

                def turn(i):
                    def relu(m):
                        act.wait_ge(full[f"f_k{m % 2}"], 2 * i + m // 2 + 1)
                        if m >= 2:
                            act.wait_ge(squared, C * i + m - 1)
                        act.activation(ka[:, m % 2], bank[f"f_k{m % 2}"][:, :], ACT.Relu)\
                           .then_inc(free[f"f_k{m % 2}"], 1)

                    def high(m):
                        act.wait_ge(squared, C * i + m + 1)
                        act.activation(kh[:, m], kk[:, m % 2], ACT.Copy).then_inc(k_hi, 1)

                    relu(0)
                    relu(1)
                    high(0)
                    relu(2)
                    high(1)
                    relu(3)
                    high(2)
                    high(3)
                    if not last_turn(i):
                        transposed(i)
                        mixes(i + 1, 0)
                    for t in range(NT):
                        act.wait_ge(full[f"f_r{t % 2}"], 2 * i + t // 2 + 1)
                        for k in range(2):
                            act.wait_ge(free[f"f_v{k}"], 2 * i)
                        act.activation(th[:, t], bank[f"f_r{t % 2}"][:, :], ACT.Tanh, scale=0.5)\
                           .then_inc(free[f"f_r{t % 2}"], 1)
                    if not last_turn(i):
                        mixes(i + 1, 1)

                with act.Fori(0, B - 1) as i:
                    turn(i)
                turn(B - 1)

            @block.vector
            def _(dve):
                def low_parts(i):
                    for c in range(C):
                        dve.wait_ge(w_hi, C * i + c + 1)
                        dve.tensor_tensor(wl[:, i, c], raws[i][:, c], f(wh[:, i, c]), ALU.subtract).then_inc(w_lo, 1)

                dve.wait_ge(const, 1)
                steps = Steps(dve, dchain)
                dve.wait_ge(gated, 1)
                steps.link(dve.tensor_scalar(gate[:, :], gate[:, :], 0.5, None, ALU.mult))

                def norm(steps, x, j):
                    steps.count(dve.memset(mark[:, :], 0.0))
                    for t in range(NT):
                        ins = dve.bn_stats(stats[:, t, :], x[:, t, :])
                    steps.link(ins)
                    steps.count(dve.memset(mark[:, :], 0.0))
                    for t in range(NT):
                        ins = dve.bn_aggr(mv[:, t, :], stats[:, t, :])
                    steps.link(ins)
                    dve.tensor_scalar(ve[:, :], mv[:, :, 1], EPS, None, ALU.add).then_inc(ve_done, 1)
                    dve.wait_ge(rstd_done, j + 1)
                    for t in range(NT):
                        dve.tensor_scalar(xn[:, t, :], x[:, t, :], mv[:, t, 0:1], rstd[:, t:t + 1],
                                          ALU.subtract, ALU.mult).then_inc(xn_done, 1)

                def mixes(steps, i, j, a):
                    for c in range(C):
                        if a == 0:
                            dve.wait_ge(free[f"f_t{c % 2}"], TP.n(i, "t", c // 2) + 1)
                            steps.link(dve.tensor_tensor(dif[:, c], xt[:, c, 1:T + 1], xt[:, c, 0:T], ALU.subtract))
                        if c >= 2:
                            dve.wait_ge(mix_lo[a], C * j + c - 1)
                        dve.scalar_tensor_tensor(out=mix[:, a, c % 2], in0=dif[:, c], scalar=mu[:, a, c:c + 1],
                                                 in1=xt[:, c, 0:T], op0=ALU.mult, op1=ALU.add).then_inc(mixed[a], 1)

                dve.wait_ge(x_in, 16)
                dve.wait_ge(c_in, 48)
                norm(steps, x4[:, 0], 0)
                low_parts(0)
                mixes(steps, None, 0, 0)
                mixes(steps, None, 0, 1)
                low_parts(1)
                low_parts(2)
                BEFORE = steps.n

                def turn(i):
                    steps = Steps(dve, dchain, BEFORE + TURN * i)
                    if not last_turn(i):
                        dve.wait_ge(x_in, 16 * (i + 2))
                        norm(steps, x4[:, (i + 1) % 4], i + 1)
                    for m in range(C):
                        dve.wait_ge(k_hi, C * i + m + 1)
                        dve.tensor_tensor(kl[:, m], kk[:, m % 2], f(kh[:, m]), ALU.subtract).then_inc(k_lo, 1)
                    if not last_turn(i):
                        mixes(steps, i, i + 1, 0)
                        for k in range(2):
                            dve.wait_ge(full[f"f_r{k}"], 2 * i + 2)
                        mixes(steps, i, i + 1, 1)
                    for t in range(NT):
                        dve.wait_ge(free[f"f_r{t % 2}"], 2 * i + t // 2 + 1)
                        dve.wait_ge(full[f"f_v{t % 2}"], 2 * i + t // 2 + 1)
                        dve.scalar_tensor_tensor(out=tmp[:, t % 2], in0=th[:, t], scalar=1.0,
                                                 in1=bank[f"f_v{t % 2}"][:, :], op0=ALU.add, op1=ALU.mult)\
                           .then_inc(free[f"f_v{t % 2}"], 1)
                        dve.wait_ge(free[f"f_v{t % 2}"], 2 * i + t // 2 + 1)
                        xt_ = x4[:, i % 4, t]
                        dve.scalar_tensor_tensor(out=xt_, in0=tmp[:, t % 2], scalar=gate[:, 0:1], in1=xt_,
                                                 op0=ALU.mult, op1=ALU.add).then_inc(out_done, 1)

                TURN = LN_STEPS + C
                with dve.Fori(0, B - 1) as i:
                    turn(i)
                turn(B - 1)

            @block.tensor
            def _(pe):
                pe.wait_ge(const, 1)

                def transposes(i):
                    pe.wait_ge(xn_done, NT * (1 if i is None else i + 2))
                    for c in range(C):
                        pe.wait_ge(free[f"f_t{c % 2}"], TP.n(i, "t", c // 2))
                        for t in range(NT):
                            last = pe.transpose(bank[f"f_t{c % 2}"][:, t * P:(t + 1) * P],
                                                xn[:, t, c * P:(c + 1) * P], ident[:, :])
                        last.then_inc(full[f"f_t{c % 2}"], 1)

                transposes(None)
                pe.wait_ge(w_lo, C)

                def turn(i):
                    pe.wait_ge(mix_lo[0], C * (i + 1))
                    for m in range(C):
                        cols = slice(m * P, (m + 1) * P)
                        pe.wait_ge(free[f"f_k{m % 2}"], 2 * i + m // 2)
                        three_passes(pe, bank[f"f_k{m % 2}"][:, :],
                                     lambda c: (wh[:, 0, c, cols], wl[:, 0, c, cols]),
                                     lambda c: (xm[0][0][:, c], xm[0][1][:, c])).then_inc(full[f"f_k{m % 2}"], 1)
                    if not last_turn(i):
                        transposes(i)
                    pe.wait_ge(w_lo, 2 * C)
                    pe.wait_ge(mix_lo[1], C * (i + 1))
                    for t in range(NT):
                        cols = slice(t * P, (t + 1) * P)
                        pe.wait_ge(free[f"f_r{t % 2}"], 2 * i + t // 2)
                        three_passes(pe, bank[f"f_r{t % 2}"][:, :],
                                     lambda c: (xm[1][0][:, c, cols], xm[1][1][:, c, cols]),
                                     lambda c: (wh[:, 1, c], wl[:, 1, c])).then_inc(full[f"f_r{t % 2}"], 1)
                    pe.wait_ge(w_lo, 3 * C)
                    pe.wait_ge(k_lo, C * (i + 1))
                    for t in range(NT):
                        cols = slice(t * P, (t + 1) * P)
                        pe.wait_ge(free[f"f_v{t % 2}"], 2 * i + t // 2)
                        three_passes(pe, bank[f"f_v{t % 2}"][:, :],
                                     lambda c: (kh[:, c, cols], kl[:, c, cols]),
                                     lambda c: (wh[:, 2, c], wl[:, 2, c])).then_inc(full[f"f_v{t % 2}"], 1)

                with pe.Fori(0, B - 1) as i:
                    turn(i)
                turn(B - 1)


def build(nc, a, out):
    def dram(name, shape, dt=F32):
        return nc.dram_tensor(name, shape, dt).ap()

    N = B * S2
    kh_d = [dram(f"s_kh{i}", (D, N)) for i in range(2)]
    kl_d = [dram(f"s_kl{i}", (D, N)) for i in range(2)]
    v_d = [dram(f"s_v{i}", (N, D)) for i in range(2)]
    x1_d, x3_d, xn_d = dram("s_x1", (B, T, D)), dram("s_x3", (B, T, D)), dram("s_xn", (B, T, D))
    perm_d = dram("s_perm", (ES, B * T))
    chosen_d = dram("s_chosen", (P, NTILE, ES))
    rp_d = dram("s_rp", (NG, ES, D))
    keys_and_values(nc, a["ctx_t"], [a["k0"], a["v0"], a["k1"], a["v1"]], [a["bk"], a["bv"]], kh_d, kl_d, v_d)
    attention(nc, 0, dict(x=a["x"], wq=a["q0"], wo=a["o0"], gate=a["g_xattn"][0:1], gate_before=a["g_ffn"][0:1],
                          wc=a["wc"], bc=a["bc"], tie=a["tie"], kh=kh_d[0], kl=kl_d[0], v=v_d[0], x_out=x1_d,
                          xn_out=xn_d, perm=perm_d, chosen=chosen_d))
    experts(nc, dict(chosen=chosen_d, xn=xn_d.rearrange("b (t p) d -> (b t) p d", p=P), w1=a["w1"], b1=a["b1"], w2=a["w2"],
                     rp=rp_d))
    attention(nc, 1, dict(x=x1_d, wq=a["q1"], wo=a["o1"], gate=a["g_xattn"][1:2], gate_before=a["g_ffn"][0:1],
                          bq=a["bq"], bo=a["bo"], mask=a["mask"], mask_t=a["mask_t"], kh=kh_d[1], kl=kl_d[1],
                          v=v_d[1], x_out=x3_d, perm=perm_d, rp=rp_d, b2=a["b2"]))
    feed_forward(nc, dict(w=[a["wk"], a["wr"], a["wv"]], mu=[a["mu_k"], a["mu_r"]], gate=a["g_ffn"][1:2], x=x3_d,
                          out=out))


def kernel(**inputs):
    import concourse.bacc as bacc
    from concourse.bass_utils import run_bass_kernel_spmd

    g = {k: np.asarray(v) for k, v in inputs.items()}
    columns = lambda a: a.reshape(C, P).T
    arrays = dict(
        x=g["x"], ctx_t=g["ctx_1024"].reshape(B * S2, D).T, mask=g["mask_BxS2_ik0"], mask_t=g["mask_BxS2_ik0"].T,
        g_xattn=g["g_xattn"], g_ffn=g["g_ffn"],
        q0=g["L0_xattn_W_q"].T, k0=g["L0_xattn_W_k"].T, v0=g["L0_xattn_W_v"].T, o0=g["L0_xattn_W_o"].T,
        wc=g["L0_ffn_Wc"].reshape(D, ES), bc=g["L0_ffn_bc"].reshape(ES),
        w1=g["L0_ffn_W1"].reshape(ES, D, EF).transpose(1, 0, 2).reshape(D, ES * EF),
        b1=g["L0_ffn_b1"].reshape(EK, P).T,
        w2=g["L0_ffn_W2"].reshape(ES, D, EF).transpose(0, 2, 1).reshape(ES * EF, D),
        b2=g["L0_ffn_b2"].reshape(ES, D),
        q1=g["L1_xattn_Wq"].T, k1=g["L1_xattn_Wk"].T, v1=g["L1_xattn_Wv"].T, o1=g["L1_xattn_Wo"].T,
        bq=columns(g["L1_xattn_bq"]), bk=columns(g["L1_xattn_bk"]), bv=g["L1_xattn_bv"], bo=g["L1_xattn_bo"],
        wr=g["L1_ffn_W_r"].T, wk=g["L1_ffn_W_k"].T, wv=g["L1_ffn_W_v"].T,
        mu_r=columns(g["L1_ffn_mu_r"]), mu_k=columns(g["L1_ffn_mu_k"]),
        tie=np.linspace(0.0, 1e-6, G, dtype=np.float32),
    )
    nc = bacc.Bacc("TRN2", target_bir_lowering=False, num_devices=1)
    feed, aps = {}, {}
    for name, value in arrays.items():
        feed["in_" + name] = np.ascontiguousarray(value)
        aps[name] = nc.dram_tensor("in_" + name, value.shape, mybir.dt.from_np(value.dtype), kind="ExternalInput").ap()
    out = nc.dram_tensor("out", (B, T, D), F32, kind="ExternalOutput").ap()
    build(nc, aps, out)
    return run_bass_kernel_spmd(nc, [feed], core_ids=[0]).results[0]["out"]
```
